# Optimizing a Trainium2 kernel written in Bass

```python
import numpy as np
import jax
import jax.numpy as jnp

def _softmax(x, axis=-1):
    return jax.nn.softmax(x, axis=axis)

def _gelu(x):
    return jax.nn.gelu(x, approximate=True)

def _silu(x):
    return jax.nn.silu(x)

def _sigmoid(x):
    return jax.nn.sigmoid(x)

def _layernorm(x, axis=-1, eps=1e-05):
    m = jnp.mean(x, axis=axis, keepdims=True)
    v = jnp.var(x, axis=axis, keepdims=True)
    return (x - m) / jnp.sqrt(v + eps)

def _scatter_add(tgt, idx, src, axis=0):
    return tgt.at[idx].add(src)

def _segment_sum(src, seg, n):
    return jax.ops.segment_sum(src, seg, n)
kernel_name = 'mk_gps_d1_gnn_r32_18eaaa'

def setup_inputs(seed: int=0):
    np.random.seed(seed)
    _w = jnp.asarray

    def _rec_inputs():
        import jax
        import jax.numpy as jnp
        _gk = jax.random.key(seed)
        x = -0.0002117 + 1 * jax.random.normal(jax.random.fold_in(_gk, 1), (3125, 256), jnp.float32)
        _s = jax.random.randint(jax.random.fold_in(_gk, 2), (25000,), 0, 3125, jnp.int32)
        _d = jax.random.randint(jax.random.fold_in(_gk, 3), (25000,), 0, 3125, jnp.int32)
        _loop = jnp.arange(3125, dtype=jnp.int32)
        src = jnp.concatenate([_s, _d, _loop])
        dst = jnp.concatenate([_d, _s, _loop])
        _o = jnp.argsort(dst, stable=True)
        src = src[_o]
        dst = dst[_o]
        return (x, src, dst)
    x, src, dst = _rec_inputs()

    def _L0_gnn_setup():
        import jax, jax.numpy as jnp
        import numpy as np
        N_NODES = 3125
        N_EDGES = 100000
        D_FEAT = 256
        LEAKY_ALPHA = 0.2
        key = jax.random.key(seed)
        k1, k2, k3 = jax.random.split(key, 3)
        x = jax.random.normal(k1, (N_NODES, D_FEAT), dtype=jnp.float32)
        edge_index = jax.random.randint(k2, (2, N_EDGES), 0, N_NODES, dtype=jnp.int32)
        W = jax.random.normal(k3, (D_FEAT, D_FEAT), dtype=jnp.float32) * (1.0 / np.sqrt(D_FEAT))
        b = jnp.zeros((D_FEAT,), dtype=jnp.float32)
        return {'x': x, 'edge_index': edge_index, 'W': W, 'b': b}
    _L0_gnn_all = _L0_gnn_setup()
    _L0_gnn_in = {k: v for k, v in _L0_gnn_all.items() if k in ('W', 'b')}
    del _L0_gnn_all

    def _L0_mix_setup():
        import jax, jax.numpy as jnp
        import numpy as np
        N, F, C, H = (32, 128, 256, 8)
        D = C // H
        EPS_ATTN = 1e-06
        EPS_LN = 1e-05

        def layer_norm(x, g, b):
            mu = jnp.mean(x, axis=-1, keepdims=True)
            var = jnp.var(x, axis=-1, keepdims=True)
            return (x - mu) * jax.lax.rsqrt(var + EPS_LN) * g + b
        key = jax.random.key(seed)
        ks = jax.random.split(key, 8)
        s = 1.0 / np.sqrt(C)
        return {'x': jax.random.normal(ks[0], (N, F, C), jnp.float32), 'Wqkv': jax.random.uniform(ks[1], (3 * C, C), jnp.float32, -s, s), 'ln1_g': jnp.ones((C,), jnp.float32), 'ln1_b': jnp.zeros((C,), jnp.float32), 'W1': jax.random.uniform(ks[2], (C, C), jnp.float32, -s, s), 'b1': jax.random.uniform(ks[3], (C,), jnp.float32, -s, s), 'W2': jax.random.uniform(ks[4], (C, C), jnp.float32, -s, s), 'b2': jax.random.uniform(ks[5], (C,), jnp.float32, -s, s), 'ln2_g': jnp.ones((C,), jnp.float32), 'ln2_b': jnp.zeros((C,), jnp.float32)}
    _L0_mix_all = _L0_mix_setup()
    _L0_mix_in = {k: v for k, v in _L0_mix_all.items() if k in ('Wqkv', 'ln1_g', 'ln1_b', 'W1', 'b1', 'W2', 'b2', 'ln2_g', 'ln2_b')}
    del _L0_mix_all

    def _L0_ffn_setup():
        import jax, jax.numpy as jnp
        import numpy as np
        TOP_K = 2
        LN_EPS = 1e-05
        key = jax.random.key(seed)
        ks = jax.random.split(key, 8)
        B, S, D, E, H = (16, 1024, 256, 8, 1024)
        x = jax.random.normal(ks[0], (B, S, D), dtype=jnp.float32)
        Wr = jax.random.normal(ks[1], (D, E), dtype=jnp.float32) * 0.1
        br = jnp.zeros((E,), dtype=jnp.float32)
        ln_g = jnp.ones((E, D), dtype=jnp.float32)
        ln_b = jnp.zeros((E, D), dtype=jnp.float32)
        W1 = jax.random.normal(ks[2], (E, D, H), dtype=jnp.float32) * (1.0 / np.sqrt(D))
        b1 = jnp.zeros((E, H), dtype=jnp.float32)
        W2 = jax.random.normal(ks[3], (E, H, D), dtype=jnp.float32) * (1.0 / np.sqrt(H))
        b2 = jnp.zeros((E, D), dtype=jnp.float32)
        return {'x': x, 'Wr': Wr, 'br': br, 'ln_g': ln_g, 'ln_b': ln_b, 'W1': W1, 'b1': b1, 'W2': W2, 'b2': b2}
    _L0_ffn_all = _L0_ffn_setup()
    _L0_ffn_in = {k: v for k, v in _L0_ffn_all.items() if k in ('Wr', 'br', 'ln_g', 'ln_b', 'W1', 'b1', 'W2', 'b2')}
    del _L0_ffn_all
    return {'x': x, 'src': src, 'dst': dst, 'L0_gnn_W': _L0_gnn_in['W'], 'L0_gnn_b': _L0_gnn_in['b'], 'L0_mix_Wqkv': _L0_mix_in['Wqkv'], 'L0_mix_ln1_g': _L0_mix_in['ln1_g'], 'L0_mix_ln1_b': _L0_mix_in['ln1_b'], 'L0_mix_W1': _L0_mix_in['W1'], 'L0_mix_b1': _L0_mix_in['b1'], 'L0_mix_W2': _L0_mix_in['W2'], 'L0_mix_b2': _L0_mix_in['b2'], 'L0_mix_ln2_g': _L0_mix_in['ln2_g'], 'L0_mix_ln2_b': _L0_mix_in['ln2_b'], 'L0_ffn_Wr': _L0_ffn_in['Wr'], 'L0_ffn_br': _L0_ffn_in['br'], 'L0_ffn_ln_g': _L0_ffn_in['ln_g'], 'L0_ffn_ln_b': _L0_ffn_in['ln_b'], 'L0_ffn_W1': _L0_ffn_in['W1'], 'L0_ffn_b1': _L0_ffn_in['b1'], 'L0_ffn_W2': _L0_ffn_in['W2'], 'L0_ffn_b2': _L0_ffn_in['b2']}

def reference(x, src, dst, L0_gnn_W, L0_gnn_b, L0_mix_Wqkv, L0_mix_ln1_g, L0_mix_ln1_b, L0_mix_W1, L0_mix_b1, L0_mix_W2, L0_mix_b2, L0_mix_ln2_g, L0_mix_ln2_b, L0_ffn_Wr, L0_ffn_br, L0_ffn_ln_g, L0_ffn_ln_b, L0_ffn_W1, L0_ffn_b1, L0_ffn_W2, L0_ffn_b2):
    import jax
    import jax.numpy as jnp

    def _L0_gnn_ref(x, edge_index, W, b):
        import jax, jax.numpy as jnp
        import numpy as np
        N_NODES = 3125
        N_EDGES = 100000
        D_FEAT = 256
        LEAKY_ALPHA = 0.2
        N = x.shape[0]
        row = edge_index[0]
        col = edge_index[1]
        ones = jnp.ones(row.shape[0], dtype=x.dtype)
        deg = jax.ops.segment_sum(ones, row, num_segments=N)
        deg_safe = jnp.where(deg > 0, deg, 1.0)
        dinv_sqrt = jnp.where(deg > 0, jax.lax.rsqrt(deg_safe), 0.0)
        w = dinv_sqrt[row] * dinv_sqrt[col]
        h = jax.ops.segment_sum(w[:, None] * x[col], row, num_segments=N)
        h = h @ W + b
        return jnp.where(h >= 0, h, LEAKY_ALPHA * h)

    def _L0_mix_ref(x, Wqkv, ln1_g, ln1_b, W1, b1, W2, b2, ln2_g, ln2_b):
        import jax, jax.numpy as jnp
        import numpy as np
        N, F, C, H = (32, 128, 256, 8)
        D = C // H
        EPS_ATTN = 1e-06
        EPS_LN = 1e-05

        def layer_norm(x, g, b):
            mu = jnp.mean(x, axis=-1, keepdims=True)
            var = jnp.var(x, axis=-1, keepdims=True)
            return (x - mu) * jax.lax.rsqrt(var + EPS_LN) * g + b
        n, f, c = x.shape
        qkv = jnp.einsum('nfc,oc->nfo', x, Wqkv)
        q, k, v = jnp.split(qkv, 3, axis=-1)
        q = q.reshape(n, f, H, D)
        k = k.reshape(n, f, H, D)
        v = v.reshape(n, f, H, D)
        q = jax.nn.elu(q) + 1.0
        k = jax.nn.elu(k) + 1.0
        kv = jnp.einsum('nshd,nshm->nhmd', k, v)
        ksum = jnp.sum(k, axis=1)
        z = 1.0 / (jnp.einsum('nlhd,nhd->nlh', q, ksum) + EPS_ATTN)
        t = jnp.einsum('nlhd,nhmd,nlh->nlhm', q, kv, z)
        t = t.reshape(n, f, c)
        x1 = layer_norm(t + x, ln1_g, ln1_b)
        h = jax.nn.gelu(jnp.einsum('nfc,oc->nfo', x1, W1) + b1, approximate=False)
        y = jnp.einsum('nfc,oc->nfo', h, W2) + b2
        return layer_norm(y + x1, ln2_g, ln2_b)

    def _L0_ffn_ref(x, Wr, br, ln_g, ln_b, W1, b1, W2, b2):
        import jax, jax.numpy as jnp
        import numpy as np
        TOP_K = 2
        LN_EPS = 1e-05
        B, S, D = x.shape
        N = B * S
        xt = x.reshape(N, D)
        logits = xt @ Wr + br
        probs = jax.nn.softmax(logits, axis=-1)
        top_p, top_idx = jax.lax.top_k(probs, TOP_K)
        weights = top_p / top_p.sum(axis=-1, keepdims=True)
        mu = xt.mean(axis=-1, keepdims=True)
        var = ((xt - mu) ** 2).mean(axis=-1, keepdims=True)
        xn = (xt - mu) * jax.lax.rsqrt(var + LN_EPS)
        xe = xn[None, :, :] * ln_g[:, None, :] + ln_b[:, None, :]
        h = jax.nn.gelu(jnp.einsum('end,edh->enh', xe, W1) + b1[:, None, :], approximate=False)
        y = jnp.einsum('enh,ehd->end', h, W2) + b2[:, None, :]
        y_tok = jnp.transpose(y, (1, 0, 2))
        sel = jnp.take_along_axis(y_tok, top_idx[:, :, None], axis=1)
        out = (weights[:, :, None] * sel).sum(axis=1)
        return out.reshape(B, S, D)
    edge_index = jnp.stack([src, dst])
    xn = _layernorm(x, axis=-1)
    x = x + _L0_gnn_ref(xn, edge_index, L0_gnn_W, L0_gnn_b) + _L0_mix_ref(xn[None], L0_mix_Wqkv, L0_mix_ln1_g, L0_mix_ln1_b, L0_mix_W1, L0_mix_b1, L0_mix_W2, L0_mix_b2, L0_mix_ln2_g, L0_mix_ln2_b)[0]
    x = x + _L0_ffn_ref(_layernorm(x, axis=-1)[None], L0_ffn_Wr, L0_ffn_br, L0_ffn_ln_g, L0_ffn_ln_b, L0_ffn_W1, L0_ffn_b1, L0_ffn_W2, L0_ffn_b2)[0]
    return x

_drawn_inputs = setup_inputs


def setup_inputs(seed=0):
    import zlib

    import numpy as np

    out = dict(_drawn_inputs(seed))
    spreads = {'L0_gnn_b': (0.0, 0.1),
     'L0_mix_ln1_g': (1.0, 0.2),
     'L0_mix_ln1_b': (0.0, 0.1),
     'L0_mix_ln2_g': (1.0, 0.2),
     'L0_mix_ln2_b': (0.0, 0.1),
     'L0_ffn_br': (0.0, 0.1),
     'L0_ffn_ln_g': (1.0, 0.2),
     'L0_ffn_ln_b': (0.0, 0.311),
     'L0_ffn_b1': (0.0, 0.308),
     'L0_ffn_b2': (0.0, 0.1)}
    factors = {'L0_mix_Wqkv': 4.043, 'L0_mix_b1': 4.04}
    for name, (base, spread) in spreads.items():
        noise = np.random.default_rng([zlib.crc32(name.encode()), seed]).standard_normal(out[name].shape)
        drawn = base * np.exp(spread * noise) if base else spread * noise
        out[name] = jnp.asarray(drawn.astype(out[name].dtype))
    for name, factor in factors.items():
        out[name] = (out[name] * factor).astype(out[name].dtype)
    return out
```

```python
from contextlib import ExitStack

import concourse.bass as bass
from concourse import mybir

ALU = mybir.AluOpType
ACT = mybir.ActivationFunctionType
AX = mybir.AxisListType
F32 = mybir.dt.float32
BF16 = mybir.dt.bfloat16
I32 = mybir.dt.int32
ds = bass.ds

P = 128


class Chain:

    def __init__(self, engine, sem, base=0):
        self.engine, self.sem, self.base, self.n = engine, sem, base, 0

    def link(self, ins):
        ins.then_inc(self.sem, 1)
        self.n += 1
        self.engine.wait_ge(self.sem, self.base + self.n)

    def count(self, ins):
        ins.then_inc(self.sem, 1)
        self.n += 1


def gps_layer(nc, x, src, dst, gnn_w, gnn_b, wqkv_t, ln1_g, ln1_b, w1_t, b1, w2_t, b2, ln2_g, ln2_b,
              wr, br, ffn_g, ffn_b, ffn_w1, ffn_b1, ffn_w2, ffn_b2, out):
    N, D = x.shape
    EDGES = src.shape[0]
    H = 8
    HD = D // H
    E, _, F = ffn_w1.shape
    EPS = 1e-5
    EPS_ATTN = 1e-6
    KC = D // P
    FC = F // P
    NT = -(-N // P)
    TAIL = N - (NT - 1) * P
    NP_ = NT * P
    HALF = NT // 2
    assert NT % 2 == 1 and KC == 2 and TAIL <= 64

    EP = 125
    EC = EDGES // EP
    CH = 85
    NCH = EC // CH
    assert EP * EC == EDGES and CH * NCH == EC
    DBITS = 12
    SC = 512
    PAD_KEY = float(NP_ << DBITS)
    ET = -(-EDGES // P)
    STEPS = ET + NT - 1
    R = 8
    GROUPS = STEPS // R
    assert STEPS % R == 0 and GROUPS > 2 * NT and GROUPS % 2 == 1 and (NP_ << DBITS) < 1 << 24 and NP_ <= 1 << DBITS
    PC = -(-STEPS // P)

    XT = -(-(2 * N) // P) + E - 1
    XT += XT % 2
    SLOTS = XT * P

    with ExitStack() as ctx:
        def sb(name, shape, dt=F32):
            return ctx.enter_context(nc.sbuf_tensor(name, shape, dt))

        def sem(name):
            return ctx.enter_context(nc.semaphore(name))

        def sems(name, n=2):
            return [sem(f"{name}{i}") for i in range(n)]

        y_table = nc.dram_tensor("y_table", [NP_, D], F32, kind="Internal").ap()
        x2_rows = nc.dram_tensor("x2_rows", [NP_, D], F32, kind="Internal").ap()
        path_dram = nc.dram_tensor("path_dram", [1, PC * P], I32, kind="Internal").ap()
        moe_in = nc.dram_tensor("moe_in", [SLOTS, D], F32, kind="Internal").ap()
        moe_out = nc.dram_tensor("moe_out", [SLOTS, D], F32, kind="Internal").ap()

        arena_a = sb("arena_a", [P, E * KC * F])
        arena_b = sb("arena_b", [P, E * FC * D + E * F])
        arena_w = sb("arena_w", [P, 7680])

        def carve(arena, at, n, dt=F32):
            v = arena[:, at:at + n]
            return v if dt == F32 else v.bitcast(dt)

        LO_F, HI_F = CH * P // 2, -(-CH * NT // 2)
        oh_lo = [carve(arena_a, b * LO_F, LO_F, BF16) for b in range(2)]
        oh_hi = [carve(arena_a, 2 * LO_F + b * HI_F, HI_F, BF16) for b in range(2)]
        qT_all = carve(arena_a, 0, KC * NP_)
        at = KC * NP_
        key_i = carve(arena_a, at, ET, I32); at += ET
        dst_i = carve(arena_a, at, ET, I32); at += ET
        tmp_i = carve(arena_a, at, ET, I32); at += ET
        src_f = carve(arena_a, at, ET); at += ET
        end_f = carve(arena_a, at, ET); at += ET
        cmp_f = carve(arena_a, at, ET); at += ET
        nT = [carve(arena_a, at + b * D, D) for b in range(2)]; at += 2 * D
        exp_k = [carve(arena_a, at + b * D, D) for b in range(2)]; at += 2 * D
        exp_q = [carve(arena_a, at + b * D, D) for b in range(2)]; at += 2 * D
        rel_k = [carve(arena_a, at + b * D, D) for b in range(2)]; at += 2 * D
        rel_q = [carve(arena_a, at + b * D, D) for b in range(2)]; at += 2 * D
        VW = P + 4
        v_ext = [carve(arena_a, at + b * KC * VW, KC * VW) for b in range(2)]; at += 2 * KC * VW
        assert at <= 13056
        at = 13056
        wqkv_sb = carve(arena_a, at, KC * 3 * D); at += KC * 3 * D
        w1_sb = carve(arena_a, at, KC * D); at += KC * D
        w2_sb = carve(arena_a, at, KC * D); at += KC * D
        gw_sb = carve(arena_a, at, KC * D); at += KC * D
        assert at <= E * KC * F
        xn_all = carve(arena_b, 0, NT * D); at = NT * D
        h_all = carve(arena_b, at, NT * D); at += NT * D
        node_iota = carve(arena_b, at, NP_); at += NP_
        rows_s = [carve(arena_b, at + b * SC, SC) for b in range(2)]; at += 2 * SC
        cols_s = [carve(arena_b, at + b * SC, SC) for b in range(2)]; at += 2 * SC
        y_all = carve(arena_b, at, NT * D)
        iota_lo = carve(arena_b, at, LO_F, BF16)
        iota_hi = carve(arena_b, at + LO_F, HI_F, BF16)
        assert at + LO_F + HI_F <= E * FC * D + E * F
        at = 0
        reps = []
        for _ in range(6):
            reps.append(carve(arena_w, at, D)); at += D
        ln1g_r, ln1b_r, ln2g_r, ln2b_r, b2_r, gb_r = reps
        rows_g = [carve(arena_w, at + u * D, D) for u in range(R)]; at += R * D
        hot_g = [carve(arena_w, at + u * P, P) for u in range(R)]; at += R * P
        work = [[carve(arena_w, at + (3 * b + k) * D, D) for k in range(3)] for b in range(2)]; at += 6 * D
        zero_w = rows_g[0]
        e0, EB = 6 * D + D, -(-EC // 2)
        src_i = carve(arena_w, e0, EC, I32)
        dst_e = carve(arena_w, e0 + EC, EC, I32)
        part_i = carve(arena_w, e0 + 2 * EC, EC, I32)
        lo_b = carve(arena_w, e0 + 3 * EC, EB, BF16)[:, 0:EC]
        hi_b = carve(arena_w, e0 + 3 * EC + EB, EB, BF16)[:, 0:EC]
        assert 3 * EC + 2 * EB <= (R - 1) * D
        assert at <= 7680
        w1_all = carve(arena_a, 0, E * KC * F)
        w2_all = carve(arena_b, 0, E * FC * D)
        b1_all = carve(arena_b, E * FC * D, E * F)
        at = 0
        b2_all = carve(arena_w, at, E * D); at += E * D
        xd = [carve(arena_w, at + b * D, D) for b in range(2)]; at += 2 * D
        xeT = [carve(arena_w, at + b * D, D) for b in range(2)]; at += 2 * D
        hid = [carve(arena_w, at + b * F, F) for b in range(2)]; at += 2 * F
        hidT = [carve(arena_w, at + b * F, F) for b in range(2)]; at += 2 * F
        yt = [carve(arena_w, at + b * D, D) for b in range(2)]; at += 2 * D
        assert at <= 7680
        fin_x = [carve(arena_a, b * D, D) for b in range(2)]
        fin_1 = [carve(arena_a, (2 + b) * D, D) for b in range(2)]
        fin_2 = [carve(arena_a, (4 + b) * D, D) for b in range(2)]

        ident = sb("ident", [P, P])
        below = sb("below", [P, P])
        ones_m = sb("ones_m", [P, P])
        last_m = sb("last_m", [P, P])
        step_f = sb("step_f", [P, PC])
        tile_f = sb("tile_f", [P, PC])
        tile_i = sb("tile_i", [P, PC], I32)
        path = sb("path", [1, PC * P], I32)
        idx_g = sb("idx_g", [P, 2 * R], I32)
        stats = sb("stats", [P, NT, 6])
        mv = sb("mv", [P, NT, 2])
        rstd = sb("rstd", [P, NT])
        nw_v = sb("nw_v", [P, NT])
        nw_i = sb("nw_i", [P, NT], I32)
        nw_a = sb("nw_a", [P, NT])
        deg = sb("deg", [P, NT])
        has = sb("has", [P, NT])
        dinv = sb("dinv", [P, NT])
        stats_flat = stats[:, :, :].rearrange("p t six -> p (t six)")
        mv_flat = mv[:, :, :].rearrange("p t two -> p (t two)")
        kvbd = sb("kvbd", [P, KC, VW])
        zden = sb("zden", [P, 2, H])
        st_b = sb("st_b", [P, 2, 6])
        b1_col = sb("b1_col", [P, KC])
        wr_sb = sb("wr_sb", [P, KC, E])
        br_r = sb("br_r", [P, E])
        eg_col = sb("eg_col", [P, E * KC])
        eb_col = sb("eb_col", [P, E * KC])
        NE = NT * E
        logit = sb("logit", [P, NE])
        prob = sb("prob", [P, NE])
        hot1 = sb("hot1", [P, NE])
        hot2 = sb("hot2", [P, NE])
        rt_a = sb("rt_a", [P, NE])
        rt_b = sb("rt_b", [P, NE])
        rank_w = sb("rank_w", [P, NE])
        valid = sb("valid", [P, NE])
        c_m = sb("c_m", [P, NT])
        c_s = sb("c_s", [P, NT])
        p_1 = sb("p_1", [P, NT])
        p_2 = sb("p_2", [P, NT])
        wt_1 = sb("wt_1", [P, NT])
        wt_2 = sb("wt_2", [P, NT])
        slot_f = sb("slot_f", [P, NT])
        slot_1 = sb("slot_1", [P, NT], I32)
        slot_2 = sb("slot_2", [P, NT], I32)
        e_f = sb("e_f", [P, E])
        e_cum = sb("e_cum", [P, E])
        e_base = sb("e_base", [P, E])
        e_i = sb("e_i", [P, E], I32)
        xt_iota = carve(arena_w, 6144, XT * E)[0:1]
        xt_cmp = carve(arena_w, 6144 + XT * E, XT * E)[0:1]
        xt_f = sb("xt_f", [1, XT])
        expert_of = sb("expert_of", [1, XT + 2], I32)
        const_end = sb("const_end", [1, 2])

        ps = ctx.enter_context(nc.psum_tensor("ps", [P, 8, 512], F32))

        s_edges = sem("s_edges"); s_x = sem("s_x"); s_wts = sem("s_wts"); s_reps = sem("s_reps")
        s_const = sem("s_const"); s_pool = sem("s_pool"); s_hzero = sem("s_hzero")
        s_dve0 = sem("s_dve0")
        oh_ready = sems("oh_ready"); oh_used = sems("oh_used"); s_deg = sem("s_deg")
        s_ln = sem("s_ln"); s_dinv = sem("s_dinv"); s_y = sem("s_y"); s_ytab = sem("s_ytab")
        s_sort = sem("s_sort"); s_turned = sem("s_turned")
        s_path = sem("s_path"); s_last = sem("s_last"); s_tiles = sem("s_tiles"); s_pdram = sem("s_pdram")
        s_prow = sem("s_prow")
        m_tp = sems("m_tp"); m_nT = sems("m_nT"); m_qkv = sems("m_qkv"); m_exp = sems("m_exp")
        m_phi = sems("m_phi"); m_kv = sems("m_kv"); s_vone = sem("s_vone"); s_bd = sem("s_bd")
        a_num = sems("a_num"); a_x1 = sems("a_x1"); a_tp = sems("a_tp"); a_x1T = sems("a_x1T")
        a_h = sems("a_h"); a_hT = sems("a_hT"); a_y = sems("a_y"); a_out = sems("a_out")
        s_tile = sem("s_tile"); s_xn = sem("s_xn"); a_s = sems("a_s")
        idx_ready = sem("idx_ready"); gathered = sems("gathered", R)
        hot_ready = sem("hot_ready"); summed = sems("summed", R); added = sem("added")
        c_sc = sems("c_sc"); c_tp = sems("c_tp"); c_T = sems("c_T"); c_mm = sems("c_mm")
        c_x = sems("c_x"); c_x2 = sems("c_x2"); c_x2o = sems("c_x2o")
        c_xt = sems("c_xt"); c_tp2 = sems("c_tp2"); c_T2 = sems("c_T2"); c_lg = sems("c_lg")
        c_lc = sems("c_lc")
        s_zero = sem("s_zero"); s_small = sem("s_small"); s_moe0 = sem("s_moe0"); s_bias = sem("s_bias")
        in_place = sems("in_place")
        s_route = sem("s_route"); s_exp = sem("s_exp")
        s_cnt = sem("s_cnt"); s_rank = sem("s_rank"); s_slot = sem("s_slot"); s_etab = sem("s_etab")
        s_scat = sem("s_scat"); s_w1 = sem("s_w1"); s_w2 = sem("s_w2")
        x_in = sems("x_in"); x_tp = sems("x_tp"); x_T = sems("x_T"); x_h = sems("x_h", 4)
        x_b1 = sems("x_b1", 4); x_g = sems("x_g"); x_ht = sems("x_ht"); x_hTa = sems("x_hTa")
        x_hTb = sems("x_hTb"); x_y = sems("x_y"); x_yb = sems("x_yb"); x_out = sems("x_out")
        f_x = sems("f_x"); f_1 = sems("f_1"); f_2 = sems("f_2"); f_y = sems("f_y")
        f_out = sems("f_out")

        def rep(v, n):
            return v.rearrange("(a n) -> a n", a=1).broadcast_to([P, n])

        def bank(k):
            return ps[:, k, :]

        FIRST_TILES = 6
        LAST_PAIRS = 2
        PH_ROWS = 8
        turns = []

        def node_tiles(engine, body):
            body(0, 0, 0, False)
            body(0, 1, 1, False)
            with engine.Fori(1, HALF) as i:
                body(i, 0, i * 2, False)
                body(i, 1, i * 2 + 1, False)
            body(HALF, 0, NT - 1, True)

        def staggered(engine, front, back):
            def turn(i):
                front(i, 1, i * 2 + 1, False)
                back(i, 0, i * 2, False)
                front(i + 1, 0, i * 2 + 2, False)
                back(i, 1, i * 2 + 1, False)

            front(0, 0, 0, False)
            turn(0)
            with engine.Fori(1, HALF) as i:
                turn(i)
            back(HALF, 0, NT - 1, True)

        def repeat(engine, n, body):
            body(0)
            with engine.Fori(1, n) as i:
                body(i)

        def step_sum(u):
            return ps[:, 4 + u // 2, (u % 2) * D:(u % 2 + 1) * D]

        def i_is_late(t):
            return not (isinstance(t, int) and t == 0)

        block = ctx.enter_context(nc.Block())

        @block.vector
        def _(dve):
            V = nc.vector
            ch = Chain(dve, s_dve0)

            def inv_sqrt(c, dst, var, eps):
                c.link(V.tensor_scalar(nw_v[:, :], var, eps, None, ALU.add))
                c.link(V.tensor_single_scalar(nw_i[:, :], nw_v[:, :].bitcast(I32), 1, ALU.logical_shift_right))
                c.link(V.tensor_scalar(dst[:, :].bitcast(I32), nw_i[:, :], -1.0, float(0x5F3759DF), ALU.mult, ALU.add))
                for _ in range(4):
                    c.link(V.tensor_tensor(nw_a[:, :], dst[:, :], dst[:, :], ALU.mult))
                    c.link(V.tensor_tensor(nw_a[:, :], nw_a[:, :], nw_v[:, :], ALU.mult))
                    c.link(V.tensor_scalar(nw_a[:, :], nw_a[:, :], -0.5, 1.5, ALU.mult, ALU.add))
                    c.link(V.tensor_tensor(dst[:, :], dst[:, :], nw_a[:, :], ALU.mult))

            V.memset(rows_s[0], PAD_KEY).then_inc(s_sort, 1)
            V.memset(kvbd[:, :, :], 0.0).then_inc(s_bd, 1)
            dve.wait_ge(s_edges, 32)
            dve.wait_ge(s_sort, 1)
            V.scalar_tensor_tensor(out=rows_s[0][0:EP, 0:EC], in0=src_i[0:EP, :], scalar=float(1 << DBITS),
                                   in1=dst_e[0:EP, :], op0=ALU.mult, op1=ALU.add).then_inc(s_sort, 1)
            ch.link(V.tensor_single_scalar(part_i[0:EP, :], src_i[0:EP, :], P - 1, ALU.bitwise_and))
            ch.link(V.tensor_copy(lo_b[0:EP, :], part_i[0:EP, :]))
            ch.link(V.tensor_single_scalar(part_i[0:EP, :], src_i[0:EP, :], 7, ALU.logical_shift_right))
            ch.link(V.tensor_copy(hi_b[0:EP, :], part_i[0:EP, :]))
            dve.wait_ge(s_const, 2)
            for c in range(NCH):
                b = c % 2
                if c >= 2:
                    dve.wait_ge(oh_used[b], c // 2)
                lo = lo_b[0:EP, c * CH:(c + 1) * CH].unsqueeze(1).broadcast_to([EP, P, CH])
                hi = hi_b[0:EP, c * CH:(c + 1) * CH].unsqueeze(1).broadcast_to([EP, NT, CH])
                V.tensor_tensor(oh_lo[b][0:EP, 0:P * CH].rearrange("p (n c) -> p n c", c=CH), lo,
                                iota_lo[0:EP, 0:P * CH].rearrange("p (n c) -> p n c", c=CH),
                                ALU.is_equal).then_inc(oh_ready[b], 1)
                V.tensor_tensor(oh_hi[b][0:EP, 0:NT * CH].rearrange("p (n c) -> p n c", c=CH), hi,
                                iota_hi[0:EP, 0:NT * CH].rearrange("p (n c) -> p n c", c=CH),
                                ALU.is_equal).then_inc(oh_ready[b], 1)
            dve.wait_ge(s_x, 32)
            dve.wait_ge(s_hzero, 2)
            for t in range(NT):
                last = V.bn_stats(stats[:, t, :], xn_all[:, t * D:(t + 1) * D])
            ch.link(last)
            for t in range(NT):
                last = V.bn_aggr(mv[:, t, :], stats[:, t, :])
            ch.link(last)
            inv_sqrt(ch, rstd, mv[:, :, 1], EPS)
            for t in range(NT):
                xt = xn_all[:, t * D:(t + 1) * D]
                last = V.tensor_scalar(xt, xt, mv[:, t, 0:1], rstd[:, t:t + 1], ALU.subtract, ALU.mult)
            last.then_inc(s_ln, 1)
            dve.wait_ge(s_deg, 1)
            ch.link(V.tensor_copy(deg[:, :], bank(7)[:, 0:NT]))
            ch.link(V.tensor_scalar(has[:, :], deg[:, :], 0.0, None, ALU.is_gt))
            ch.link(V.tensor_scalar(deg[:, :], deg[:, :], 1.0, None, ALU.max))
            inv_sqrt(ch, deg, deg[:, :], 0.0)
            V.tensor_tensor(dinv[:, :], deg[:, :], has[:, :], ALU.mult).then_inc(s_dinv, 1)

            n_sort = [2]
            cur = [0, 0]

            def settle():
                dve.wait_ge(s_sort, n_sort[0])

            def exchange(which, dist):
                a = (rows_s, cols_s)[which]
                s = a[cur[which]].rearrange("p (a two d) -> p a two d", two=2, d=dist)
                o = a[1 - cur[which]].rearrange("p (a two d) -> p a two d", two=2, d=dist)
                V.tensor_tensor(o[:, :, 0, :], s[:, :, 0, :], s[:, :, 1, :], ALU.min).then_inc(s_sort, 1)
                V.tensor_tensor(o[:, :, 1, :], s[:, :, 0, :], s[:, :, 1, :], ALU.max).then_inc(s_sort, 1)
                n_sort[0] += 2
                settle()
                cur[which] = 1 - cur[which]

            def negate(view):
                V.tensor_scalar(view, view, -1.0, None, ALU.mult).then_inc(s_sort, 1)
                n_sort[0] += 1
                settle()

            def turn(to_cols):
                turns.append((to_cols, cur[0 if to_cols else 1], n_sort[0]))
                k = len(turns)
                dve.wait_ge(s_turned, k)
                b = bank(0)
                if to_cols:
                    cur[1] = 0
                    V.tensor_copy(cols_s[0].rearrange("q (p c) -> q c p", c=4),
                                  b.rearrange("q (c p) -> q c p", c=4)).then_inc(s_sort, 1)
                else:
                    cur[0] = 0
                    V.tensor_copy(rows_s[0], b).then_inc(s_sort, 1)
                n_sort[0] += 1
                settle()

            def half_view(a, h):
                return a.rearrange("p (a two h) -> p a two h", two=2, h=h)[:, :, 1, :]

            def mid_view(a, h):
                return a.rearrange("p (a q h) -> p a q h", q=4, h=h)[:, :, 1:3, :]

            settle()
            negate(half_view(rows_s[0], 2))
            for k in range(1, PH_ROWS + 1):
                for j in range(k - 1, -1, -1):
                    exchange(0, 1 << j)
                if k < PH_ROWS:
                    negate(mid_view(rows_s[cur[0]], 1 << k))
            negate(rows_s[cur[0]][:, SC // 2:SC])
            turn(True)
            negate(half_view(cols_s[0], 4))
            for k in range(PH_ROWS + 1, 17):
                for j in range(k - 8, -1, -1):
                    exchange(1, 1 << j)
                turn(False)
                for j in range(6, -1, -1):
                    exchange(0, 1 << j)
                turn(True)
                if k < 15:
                    negate(mid_view(cols_s[0], 1 << (k - 7)))
                elif k == 15:
                    negate(cols_s[0][:, SC // 2:SC])

            ch.link(V.tensor_copy(key_i, cols_s[0][:, 0:ET]))
            ch.link(V.tensor_single_scalar(dst_i, key_i, (1 << DBITS) - 1, ALU.bitwise_and))
            ch.link(V.tensor_single_scalar(tmp_i, key_i, DBITS, ALU.logical_shift_right))
            ch.link(V.tensor_copy(src_f, tmp_i))
            ch.link(V.tensor_single_scalar(tmp_i, key_i, DBITS + 7, ALU.logical_shift_right))
            ch.link(V.tensor_copy(cmp_f, tmp_i))
            dve.wait_ge(s_const, 3)
            V.tensor_tensor(end_f[:, 0:ET - 1], cmp_f[:, 0:ET - 1], node_iota[:, 0:ET - 1],
                            ALU.add).then_inc(s_path, 1)
            dve.wait_ge(s_last, 1)
            for c in range(PC):
                ch.link(V.tensor_scalar(cmp_f[:, 0:ET - 1], bank(0)[:, 0:ET - 1], step_f[:, c:c + 1], None,
                                        ALU.is_lt))
                ch.link(V.tensor_reduce(tile_f[:, c:c + 1], cmp_f[:, 0:ET - 1], AX.X, ALU.add))
            V.tensor_copy(tile_i[:, :], tile_f[:, :]).then_inc(s_tiles, 1)

            dve.wait_ge(m_kv[0], HALF + 1)
            dve.wait_ge(m_kv[1], HALF)
            dve.wait_ge(s_bd, 1)
            for c in range(KC):
                for h in range(4):
                    r = slice(h * HD, (h + 1) * HD)
                    V.tensor_copy(kvbd[r, c, r], bank(6 + c)[r, r]).then_inc(s_bd, 1)
                    V.tensor_copy(kvbd[r, c, P + h:P + h + 1], bank(6 + c)[r, P:P + 1]).then_inc(s_bd, 1)

            tiles = [dve.alloc_register(f"dve_tile{u}") for u in range(R)]

            def group_at(g):
                dve.reg_load(tiles, path[0:1, ds(g * R, R)])
                at_tile = [dve.snap(r, min_val=0, max_val=ET - 1) for r in tiles]
                at_block = [nc.s_assert_within(
                    dve.snap(g * R + u - at_tile[u]), 0, NT - 1,
                    skip_runtime_bounds_check_because="a step moves either the tile or the block on")
                            for u in range(R)]
                return at_tile, at_block

            def make_hots(g):
                at_tile, at_block = group_at(g)
                for u in range(R):
                    if i_is_late(g):
                        dve.wait_ge(summed[u], g)
                    V.tensor_scalar(hot_g[u], node_iota[:, ds(at_block[u] * P, P)],
                                    src_f[:, ds(at_tile[u], 1)], None, ALU.is_equal).then_inc(hot_ready, 1)

            def sum_rows(g):
                at_block = group_at(g)[1]
                for u in range(R):
                    if u % 2 == 0:
                        dve.wait_ge(summed[u + 1], g + 1)
                    if u or i_is_late(g):
                        dve.wait_ge(added, g * R + u)
                    block_h = h_all[:, ds(at_block[u] * D, D)]
                    V.tensor_tensor(block_h, block_h, step_sum(u), ALU.add).then_inc(added, 1)

            def moments(c, b, rows, t):
                c.link(V.bn_stats(st_b[:, b, :], rows))
                c.count(keep(stats_flat[:, ds(t * 6, 6)], st_b[:, b, :]))

            def keep(out_, in_):
                return V.tensor_scalar(out_, in_, 1.0, None, ALU.mult)

            def means(c):
                dve.wait_ge(s_tile, c.base)
                for t in range(NT):
                    last = V.bn_aggr(mv[:, t, :], stats[:, t, :])
                c.link(last)
                inv_sqrt(c, rstd, mv[:, :, 1], EPS)

            def normed(out_, in_, t):
                return V.tensor_scalar(out_, in_, mv_flat[:, ds(t * 2, 1)], rstd[:, ds(t, 1)],
                                       ALU.subtract, ALU.mult)

            def tile_of(a, t):
                return a[:, ds(t * D, D)]

            per = 7
            base = [0]

            def pass2(i, b, t, tail):
                if i_is_late(t):
                    sum_rows(t - 1)
                make_hots(t)
                c = Chain(dve, s_tile, t * per + base[0])
                w0 = work[b][0]
                dve.wait_ge(a_num[b], i + 1)
                num = bank(b)[:, 0:KC * VW].rearrange("p (c v) -> p c v", c=KC)
                z = zden[:, b, :].rearrange("p (c h) -> p c h", c=KC)
                c.link(V.tensor_scalar(z, num[:, :, P:VW], EPS_ATTN, None, ALU.add))
                c.link(V.reciprocal(zden[:, b, :], zden[:, b, :]))
                for cc in range(KC):
                    ins = V.tensor_tensor(w0[:, cc * P:(cc + 1) * P].rearrange("p (h d) -> p h d", d=HD),
                                          num[:, cc, 0:P].rearrange("p (h d) -> p h d", d=HD),
                                          zden[:, b, cc * 4:cc * 4 + 4].unsqueeze(2).broadcast_to([P, 4, HD]),
                                          ALU.mult)
                    if cc == 0:
                        c.link(ins)
                ins.then_inc(a_s[b], 1)
                dve.wait_ge(a_s[b], i + 1)
                c.link(V.tensor_tensor(w0, w0, tile_of(xn_all, t), ALU.add))
                c.link(keep(tile_of(xn_all, t), w0))
                moments(c, b, w0, t)
                assert c.n == per, c.n

            dve.wait_ge(s_y, 1)
            dve.wait_ge(s_const, 3)
            dve.wait_ge(s_prow, 16)
            dve.wait_ge(s_hzero, 1)
            node_tiles(dve, pass2)
            base[0] += NT * per
            c = Chain(dve, s_tile, base[0])
            means(c)
            base[0] += c.n

            dve.wait_ge(s_reps, 6 * 16)
            base_x1 = base[0]

            def ffn_front(i, b, t, tail):
                c = Chain(dve, s_tile, base_x1 + (t * 6 - 4 if i_is_late(t) else 0))
                w1 = work[b][1]
                c.link(normed(w1, tile_of(xn_all, t), t))
                c.link(V.tensor_tensor(w1, w1, ln1g_r, ALU.mult))
                V.tensor_tensor(w1, w1, ln1b_r, ALU.add).then_inc(a_x1[b], 1)

            def ffn_back(i, b, t, tail):
                sum_rows(t + (NT - 1))
                make_hots(t + NT)
                c = Chain(dve, s_tile, base_x1 + t * 6 + (2 if tail else 4))
                w1, w2 = work[b][1:]
                dve.wait_ge(a_y[b], i + 1)
                dve.wait_ge(a_x1[b], i + 1)
                c.link(V.tensor_tensor(w2, bank(2 + b)[:, 0:D], b2_r, ALU.add))
                V.tensor_tensor(w2, w2, w1, ALU.add).then_inc(a_out[b], 1)
                dve.wait_ge(a_out[b], i + 1)
                c.link(keep(tile_of(xn_all, t), w2))
                moments(c, b, w2, t)

            staggered(dve, ffn_front, ffn_back)
            base[0] += NT * 6
            c = Chain(dve, s_tile, base[0])
            means(c)
            base[0] += c.n

            with dve.Fori(NT, (GROUPS - 1) // 2) as i:
                for q in range(2):
                    sum_rows(i * 2 + q - 1)
                    make_hots(i * 2 + q)
            sum_rows(GROUPS - 2)
            make_hots(GROUPS - 1)
            sum_rows(GROUPS - 1)

            base_x2 = base[0]

            def combine(i, b, t, tail):
                c = Chain(dve, s_tile, base_x2 + t * 9)
                w0, w1, w2 = work[b]
                c.link(normed(w2, tile_of(xn_all, t), t))
                c.link(V.tensor_tensor(w2, w2, ln2g_r, ALU.mult))
                c.link(V.tensor_tensor(w2, w2, ln2b_r, ALU.add))
                dve.wait_ge(c_mm[b], i + 1)
                dve.wait_ge(c_x[b], 16 * (i + 1))
                dve.wait_ge(c_x2o[b], 16 * i)
                c.link(V.tensor_tensor(w0, bank(4 + b)[:, 0:D], gb_r, ALU.add))
                c.link(V.scalar_tensor_tensor(out=w0, in0=w0, scalar=0.2, in1=w0, op0=ALU.mult, op1=ALU.max))
                c.link(V.tensor_tensor(w0, w0, rows_g[b], ALU.add))
                V.tensor_tensor(w1, w0, w2, ALU.add).then_inc(c_x2[b], 1)
                dve.wait_ge(c_x2[b], i + 1)
                c.link(keep(tile_of(h_all, t), w1))
                moments(c, b, w1, t)
                assert c.n == 9

            node_tiles(dve, combine)
            base[0] += NT * 9
            c = Chain(dve, s_tile, base[0])
            means(c)
            base[0] += c.n
            base_xt = base[0]

            def route_in(i, b, t, tail):
                c = Chain(dve, s_tile, base_xt + t * 3)
                w2 = work[b][2]
                dve.wait_ge(c_tp2[b], i)
                normed(w2, tile_of(h_all, t), t).then_inc(c_xt[b], 1)
                dve.wait_ge(c_xt[b], i + 1)
                c.link(keep(tile_of(h_all, t), w2))
                moments(c, b, w2, t)
                dve.wait_ge(c_lg[b], i + 1)
                V.tensor_tensor(logit[:, ds(t * E, E)], bank(6 + b)[:, 0:E], br_r[:, :],
                                ALU.add).then_inc(c_lc[b], 1)

            dve.wait_ge(s_small, 5 * 16)
            node_tiles(dve, route_in)
            base[0] += NT * 3
            c = Chain(dve, s_tile, base[0])
            means(c)
            base[0] += c.n
            with dve.Fori(0, NT) as t:
                normed(tile_of(h_all, t), tile_of(h_all, t), t).then_inc(s_xn, 1)

            def te(a):
                return a.rearrange("p (t e) -> p t e", e=E)

            def over_e(a):
                return a[:, :].unsqueeze(2).broadcast_to([P, NT, E])

            def over_t(a):
                return a[:, :].unsqueeze(1).broadcast_to([P, NT, E])

            dve.wait_ge(c_lc[0], HALF + 1)
            dve.wait_ge(c_lc[1], HALF)
            ch.link(V.tensor_reduce(c_m[:, :], te(logit[:, :]), AX.X, ALU.max))
            V.tensor_tensor(te(logit[:, :]), te(logit[:, :]), over_e(c_m), ALU.subtract).then_inc(s_route, 1)
            dve.wait_ge(s_exp, 1)
            ch.link(V.tensor_reduce(c_s[:, :], te(prob[:, :]), AX.X, ALU.add))
            ch.link(V.reciprocal(c_s[:, :], c_s[:, :]))
            ch.link(V.tensor_tensor(te(prob[:, :]), te(prob[:, :]), over_e(c_s), ALU.mult))
            dve.wait_ge(s_const, 3)
            for p_k, hot in ((p_1, hot1), (p_2, hot2)):
                ch.link(V.tensor_reduce(p_k[:, :], te(prob[:, :]), AX.X, ALU.max))
                ch.link(V.tensor_tensor(te(rt_a[:, :]), te(prob[:, :]), over_e(p_k), ALU.is_equal))
                ch.link(V.tensor_tensor(rt_a[:, :], rt_a[:, :], rank_w[:, :], ALU.mult))
                ch.link(V.tensor_reduce(c_m[:, :], te(rt_a[:, :]), AX.X, ALU.max))
                ch.link(V.tensor_tensor(te(hot[:, :]), te(rt_a[:, :]), over_e(c_m), ALU.is_equal))
                if hot is hot1:
                    ch.link(V.scalar_tensor_tensor(out=prob[:, :], in0=hot[:, :], scalar=-2.0, in1=prob[:, :],
                                                   op0=ALU.mult, op1=ALU.add))
            ch.link(V.tensor_tensor(c_s[:, :], p_1[:, :], p_2[:, :], ALU.add))
            ch.link(V.reciprocal(c_s[:, :], c_s[:, :]))
            ch.link(V.tensor_tensor(wt_1[:, :], p_1[:, :], c_s[:, :], ALU.mult))
            ch.link(V.tensor_tensor(wt_2[:, :], p_2[:, :], c_s[:, :], ALU.mult))
            ch.link(V.tensor_tensor(rt_b[:, :], hot1[:, :], hot2[:, :], ALU.add))
            V.tensor_tensor(rt_b[:, :], rt_b[:, :], valid[:, :], ALU.mult).then_inc(s_cnt, 1)
            dve.wait_ge(s_rank, 1)
            ch.link(V.tensor_copy(rt_b[:, :], bank(1)[:, 0:NE]))
            for e in range(E):
                last = V.tensor_tensor_scan(te(rt_a[:, :])[:, :, e], ones_m[:, 0:NT], te(rt_b[:, :])[:, :, e],
                                            0.0, ALU.mult, ALU.add)
            ch.link(last)
            ch.link(V.tensor_copy(e_f[:, :], te(rt_a[:, :])[:, NT - 1, :]))
            ch.link(V.tensor_tensor(rt_a[:, :], rt_a[:, :], rt_b[:, :], ALU.subtract))
            ch.link(V.tensor_scalar(e_f[:, :], e_f[:, :], float(P - 1), None, ALU.add))
            ch.link(V.tensor_copy(e_i[:, :], e_f[:, :]))
            ch.link(V.tensor_single_scalar(e_i[:, :], e_i[:, :], 7, ALU.logical_shift_right))
            ch.link(V.tensor_copy(e_f[:, :], e_i[:, :]))
            ch.link(V.tensor_tensor_scan(e_cum[:, :], ones_m[:, 0:E], e_f[:, :], 0.0, ALU.mult, ALU.add))
            ch.link(V.tensor_tensor(e_base[:, :], e_cum[:, :], e_f[:, :], ALU.subtract))
            ch.link(V.tensor_scalar(e_base[:, :], e_base[:, :], float(P), None, ALU.mult))
            ch.link(V.tensor_tensor(rt_a[:, :], rt_a[:, :], bank(0)[:, 0:NE], ALU.add))
            ch.link(V.tensor_tensor(te(rt_a[:, :]), te(rt_a[:, :]), over_t(e_base), ALU.add))
            for hot, slot in ((hot1, slot_1), (hot2, slot_2)):
                ch.link(V.tensor_tensor(rt_b[:, :], hot[:, :], rt_a[:, :], ALU.mult))
                ch.link(V.tensor_reduce(slot_f[:, :], te(rt_b[:, :]), AX.X, ALU.add))
                V.tensor_copy(slot[:, :], slot_f[:, :]).then_inc(s_slot, 1)
                dve.wait_ge(s_slot, 1 if hot is hot1 else 2)
            ch.link(V.tensor_tensor(xt_cmp[:, :].rearrange("p (k e) -> p k e", e=E),
                                    xt_iota[:, :].rearrange("p (k e) -> p k e", e=E),
                                    e_cum[0:1, :].unsqueeze(1).broadcast_to([1, XT, E]), ALU.is_ge))
            ch.link(V.tensor_reduce(xt_f[:, :], xt_cmp[:, :].rearrange("p (k e) -> p k e", e=E), AX.X, ALU.add))
            V.memset(expert_of[:, XT:XT + 2], 0).then_inc(s_etab, 1)
            V.tensor_scalar(expert_of[:, 0:XT], xt_f[:, :], float(E - 1), None, ALU.min).then_inc(s_etab, 1)

            dve.wait_ge(s_etab, 2)
            dve.wait_ge(s_bias, 32)
            dve.wait_ge(s_small, 5 * 16)
            er = [dve.alloc_register(f"dve_expert{n}") for n in range(3)]

            def evac_x(e, b, i, first=True):
                dve.wait_ge(x_tp[b], i + 1)
                for k in range(KC):
                    V.tensor_scalar(xeT[b][:, k * P:(k + 1) * P], bank(4)[:, k * P:(k + 1) * P],
                                    eg_col[:, ds(e * KC + k, 1)], eb_col[:, ds(e * KC + k, 1)],
                                    ALU.mult, ALU.add).then_inc(x_T[b], 1)

            def bias_h(e, b, i):
                dve.wait_ge(x_hTb[b], i)
                for s in range(2):
                    dve.wait_ge(x_h[2 * b + s], i + 1)
                    V.tensor_tensor(hid[b][:, s * 512:(s + 1) * 512], bank(2 * b + s),
                                    b1_all[:, ds(e * F + s * 512, 512)], ALU.add).then_inc(x_b1[2 * b + s], 1)

            def evac_hT(b, i):
                dve.wait_ge(x_ht[b], 2 * (i + 1))
                V.tensor_copy(hidT[b][:, 512:1024], bank(6)).then_inc(x_hTb[b], 1)

            def bias_y(e, b, i):
                dve.wait_ge(x_y[b], i + 1)
                dve.wait_ge(x_out[b], 16 * i)
                V.tensor_tensor(yt[b], bank(7)[:, 0:D], b2_all[:, ds(e * D, D)], ALU.add).then_inc(x_yb[b], 1)

            def tile_step(e_prev, e_this, e_next, b, i, ip, inx):
                if e_prev is not None:
                    evac_hT(1 - b, ip)
                if e_this is not None:
                    bias_h(e_this, b, i)
                if e_prev is not None:
                    bias_y(e_prev, 1 - b, ip)
                if e_next is not None:
                    evac_x(e_next, 1 - b, inx)

            def experts(regs, at):
                dve.reg_load(regs, expert_of[0:1, ds(at, len(regs))])
                return [dve.snap(r, min_val=0, max_val=E - 1) for r in regs]

            e0, e1 = experts(er[0:2], 0)
            evac_x(e0, 0, 0)
            tile_step(None, e0, e1, 0, 0, None, 0)
            def expert_tiles(i):
                ea, eb, ec = experts(er, i * 2)
                tile_step(ea, eb, ec, 1, i, i, i + 1)
                eb, ec, ed = experts(er, i * 2 + 1)
                tile_step(eb, ec, ed, 0, i + 1, i, i + 1)

            repeat(dve, XT // 2 - 1, expert_tiles)
            ea, eb = experts(er[0:2], XT - 2)
            tile_step(ea, eb, None, 1, XT // 2 - 1, XT // 2 - 1, None)
            tile_step(eb, None, None, 0, None, XT // 2 - 1, None)

            base_fin = base[0]

            def final(i, b, t, tail):
                n = TAIL if tail else P
                dve.wait_ge(f_x[b], 16 * (i + 1))
                dve.wait_ge(f_1[b], 16 * (i + 1))
                V.scalar_tensor_tensor(out=fin_x[b][0:n], in0=fin_1[b][0:n], scalar=wt_1[0:n, ds(t, 1)],
                                       in1=fin_x[b][0:n], op0=ALU.mult, op1=ALU.add).then_inc(s_tile, 1)
                dve.wait_ge(s_tile, base_fin + t + 1)
                dve.wait_ge(f_2[b], 16 * (i + 1))
                V.scalar_tensor_tensor(out=fin_x[b][0:n], in0=fin_2[b][0:n], scalar=wt_2[0:n, ds(t, 1)],
                                       in1=fin_x[b][0:n], op0=ALU.mult, op1=ALU.add).then_inc(f_y[b], 1)

            node_tiles(dve, final)

        @block.tensor
        def _(pe):
            T = nc.tensor
            for c in range(NCH):
                b = c % 2
                pe.wait_ge(oh_ready[b], 2 * (c // 2 + 1))
                lo = oh_lo[b][0:EP, 0:P * CH].rearrange("p (n c) -> p n c", c=CH)
                hi = oh_hi[b][0:EP, 0:NT * CH].rearrange("p (n c) -> p n c", c=CH)
                for j in range(CH):
                    last = T.matmul(bank(7)[:, 0:NT], lo[:, :, j], hi[:, :, j],
                                    start=(c == 0 and j == 0), stop=(c == NCH - 1 and j == CH - 1))
                last.then_inc(oh_used[b] if c < NCH - 1 else s_deg, 1)
            pe.wait_ge(s_const, 3)

            def turn2(dst, rows, signal):
                for k in range(KC):
                    last = T.transpose(dst[:, k * P:(k + 1) * P], rows(k), ident[:, :])
                last.then_inc(signal, 1)

            def wkv(k, o, n):
                return wqkv_sb[:, k * 3 * D + o:k * 3 * D + o + n]

            def pass1_front(t):
                i, b = t // 2, t % 2
                pe.wait_ge(in_place[b], i + 1)
                if t:
                    pe.wait_ge(m_nT[1 - b], i + b)
                turn2(bank(1), lambda k: work[b][0][:, k * P:(k + 1) * P], m_tp[b])
                pe.wait_ge(m_nT[b], i + 1)
                if i:
                    pe.wait_ge(m_exp[b], i * 5)
                for k in range(KC):
                    T.matmul(bank(2 + b), nT[b][:, k * P:(k + 1) * P], wkv(k, D, 2 * D),
                             start=(k == 0), stop=(k == KC - 1))
                for o in range(KC):
                    for k in range(KC):
                        last = T.matmul(bank(4 + b)[:, o * P:(o + 1) * P], wkv(k, o * P, P),
                                        nT[b][:, k * P:(k + 1) * P], start=(k == 0), stop=(k == KC - 1))
                last.then_inc(m_qkv[b], 1)

            def pass1_back(t):
                i, b = t // 2, t % 2
                pe.wait_ge(m_phi[b], (i + 1) * 2)
                pe.wait_ge(m_exp[b], (i + 1) * 5)
                n = TAIL if t == NT - 1 else P
                for c in range(KC):
                    last = T.matmul(bank(6 + c)[:, 0:P + 1], rel_k[b][0:n, c * P:(c + 1) * P],
                                    v_ext[b][0:n, c * VW:c * VW + P + 1], start=False, stop=(t == NT - 1),
                                    skip_group_check=True)
                last.then_inc(m_kv[b], 1)

            fronts = [0]

            def pass1(n):
                for t in range(fronts[0], min(fronts[0] + n, NT)):
                    pass1_front(t)
                    if t:
                        pass1_back(t - 1)
                    fronts[0] = t + 1

            pe.wait_ge(s_wts, 4 * 16)
            pe.wait_ge(s_dinv, 1)
            pe.wait_ge(s_zero, 1)
            pe.wait_ge(s_vone, 2)
            for c in range(KC):
                T.matmul(bank(6 + c)[:, 0:P + 1], zero_w[:, 0:P], zero_w[:, 0:P + 1], start=True, stop=False,
                         skip_group_check=True)
            pass1(FIRST_TILES)
            for k, (to_cols, live, count) in enumerate(turns):
                pe.wait_ge(s_sort, count)
                for c in range(4):
                    if to_cols:
                        blk = rows_s[live][:, c * P:(c + 1) * P]
                    else:
                        blk = cols_s[live].rearrange("q (p c) -> q c p", c=4)[:, c, :]
                    last = T.transpose(bank(0)[:, c * P:(c + 1) * P], blk, ident[:, :])
                last.then_inc(s_turned, 1)
                pass1(2 if k >= len(turns) - LAST_PAIRS else 1)
            pass1(NT)
            pe.wait_ge(s_path, 1)
            T.matmul(bank(0)[:, 0:ET - 1], last_m[:, :], end_f[:, 0:ET - 1], start=True,
                     stop=True).then_inc(s_last, 1)
            pass1_back(NT - 1)

            def edge_steps(g):
                for u in range(R):
                    pe.wait_ge(gathered[u], 16 * (g + 1))
                    pe.wait_ge(hot_ready, g * R + u + 1)
                    if u % 2 == 0 and i_is_late(g):
                        pe.wait_ge(added, g * R + (u + 2 - R))
                    T.matmul(step_sum(u), hot_g[u], rows_g[u], start=True, stop=True).then_inc(summed[u], 1)

            pe.wait_ge(s_bd, 1 + 8 * KC)

            def pass2(i, b, t, tail):
                pe.wait_ge(in_place[b], i + 1 + (HALF + 1 - b))
                pe.wait_ge(a_s[b], i)
                for c in range(KC):
                    last = T.matmul(bank(b)[:, c * VW:(c + 1) * VW], exp_q[b][:, c * P:(c + 1) * P],
                                    kvbd[:, c, :], start=True, stop=True)
                last.then_inc(a_num[b], 1)
                edge_steps(t)

            node_tiles(pe, pass2)

            def ffn_front(i, b, t, tail):
                pe.wait_ge(a_x1[b], i + 1)
                pe.wait_ge(a_x1T[1 - b], i + b)
                turn2(bank(0), lambda k: work[b][1][:, k * P:(k + 1) * P], a_tp[b])
                pe.wait_ge(a_x1T[b], i + 1)
                pe.wait_ge(a_hT[1 - b], 2 * i + 2 * b)
                for o in range(KC):
                    for k in range(KC):
                        last = T.matmul(bank(1)[:, o * P:(o + 1) * P], w1_sb[:, k * D + o * P:k * D + (o + 1) * P],
                                        nT[b][:, k * P:(k + 1) * P], start=(k == 0), stop=(k == KC - 1))
                last.then_inc(a_h[b], 1)

            def ffn_back(i, b, t, tail):
                pe.wait_ge(a_hT[b], 2 * (i + 1))
                pe.wait_ge(a_out[b], i)
                for k in range(KC):
                    last = T.matmul(bank(2 + b)[:, 0:D], exp_k[b][:, k * P:(k + 1) * P],
                                    w2_sb[:, k * D:(k + 1) * D], start=(k == 0), stop=(k == KC - 1))
                last.then_inc(a_y[b], 1)
                edge_steps(t + NT)

            staggered(pe, ffn_front, ffn_back)

            with pe.Fori(NT, (GROUPS - 1) // 2) as i:
                edge_steps(i * 2)
                edge_steps(i * 2 + 1)
            edge_steps(GROUPS - 1)

            def combine(i, b, t, tail):
                pe.wait_ge(c_sc[b], i + 1)
                pe.wait_ge(c_T[b], i)
                turn2(bank(b), lambda k: exp_k[b][:, k * P:(k + 1) * P], c_tp[b])
                pe.wait_ge(c_T[b], i + 1)
                pe.wait_ge(c_x2[b], i)
                for k in range(KC):
                    last = T.matmul(bank(4 + b)[:, 0:D], nT[b][:, k * P:(k + 1) * P],
                                    gw_sb[:, k * D:(k + 1) * D], start=(k == 0), stop=(k == KC - 1))
                last.then_inc(c_mm[b], 1)

            def route_in(i, b, t, tail):
                pe.wait_ge(c_xt[b], i + 1)
                pe.wait_ge(c_T2[b], i)
                turn2(bank(2 + b), lambda k: work[b][2][:, k * P:(k + 1) * P], c_tp2[b])
                pe.wait_ge(c_T2[b], i + 1)
                pe.wait_ge(c_lc[b], i)
                for k in range(KC):
                    last = T.matmul(bank(6 + b)[:, 0:E], exp_q[b][:, k * P:(k + 1) * P], wr_sb[:, k, :],
                                    start=(k == 0), stop=(k == KC - 1))
                last.then_inc(c_lg[b], 1)

            pe.wait_ge(added, STEPS)
            node_tiles(pe, combine)
            pe.wait_ge(s_small, 5 * 16)
            node_tiles(pe, route_in)
            pe.wait_ge(s_cnt, 1)
            T.matmul(bank(0)[:, 0:NE], below[:, :], rt_b[:, :], start=True, stop=True)
            T.matmul(bank(1)[:, 0:NE], ones_m[:, :], rt_b[:, :], start=True, stop=True).then_inc(s_rank, 1)

            pe.wait_ge(s_slot, 2)
            pe.wait_ge(s_etab, 2)
            er = [pe.alloc_register(f"pe_expert{n}") for n in range(2)]

            def turn_x(b, i, seen):
                pe.wait_ge(x_in[b], 16 * (i + 1))
                other, n = seen
                pe.wait_ge(x_T[other], 2 * n)
                turn2(bank(4), lambda k: xd[b][:, k * P:(k + 1) * P], x_tp[b])

            def first(e, b, i, s):
                if s == 0:
                    pe.wait_ge(x_T[b], 2 * (i + 1))
                pe.wait_ge(x_b1[2 * b + s], i)
                for k in range(KC):
                    last = T.matmul(bank(2 * b + s), xeT[b][:, k * P:(k + 1) * P],
                                    w1_all[:, ds(e * (KC * F) + (k * F + s * 512), 512)],
                                    start=(k == 0), stop=(k == KC - 1))
                last.then_inc(x_h[2 * b + s], 1)

            def turn_h(b, i, ia, ib):
                pe.wait_ge(x_hTa[1 - b], ia)
                pe.wait_ge(x_hTb[1 - b], ib)
                for s in range(2):
                    pe.wait_ge(x_g[b], 2 * i + s + 1)
                    for k in range(4):
                        c = 4 * s + k
                        last = T.transpose(bank(5 + s)[:, k * P:(k + 1) * P], hid[b][:, c * P:(c + 1) * P],
                                           ident[:, :])
                    last.then_inc(x_ht[b], 1)

            def second(e, b, i, seen):
                pe.wait_ge(x_hTa[b], i + 1)
                pe.wait_ge(x_hTb[b], i + 1)
                pe.wait_ge(x_yb[1 - b], seen)
                for k in range(FC):
                    last = T.matmul(bank(7)[:, 0:D], hidT[b][:, k * P:(k + 1) * P],
                                    w2_all[:, ds(e * (FC * D) + k * D, D)], start=(k == 0), stop=(k == FC - 1))
                last.then_inc(x_y[b], 1)

            def experts(regs, at):
                pe.reg_load(regs, expert_of[0:1, ds(at, len(regs))])
                return [pe.snap(r, min_val=0, max_val=E - 1) for r in regs]

            e0, = experts(er[0:1], 0)
            pe.wait_ge(s_w1, 16)
            turn_x(0, 0, (1, 0))
            first(e0, 0, 0, 0)
            first(e0, 0, 0, 1)
            turn_x(1, 0, (0, 1))
            pe.wait_ge(s_w2, 16)
            def expert_tiles(i):
                ea, eb = experts(er, i * 2)
                first(eb, 1, i, 0)
                turn_h(0, i, i, i)
                first(eb, 1, i, 1)
                second(ea, 0, i, i)
                turn_x(0, i + 1, (1, i + 1))
                eb, ec = experts(er, i * 2 + 1)
                first(ec, 0, i + 1, 0)
                turn_h(1, i, i + 1, i + 1)
                first(ec, 0, i + 1, 1)
                second(eb, 1, i, i + 1)
                turn_x(1, i + 1, (0, i + 2))

            repeat(pe, XT // 2 - 1, expert_tiles)
            n = XT // 2 - 1
            ea, eb = experts(er, XT - 2)
            first(eb, 1, n, 0)
            turn_h(0, n, n, n)
            first(eb, 1, n, 1)
            second(ea, 0, n, n)
            turn_h(1, n, n + 1, n + 1)
            second(eb, 1, n, n + 1)

        @block.scalar
        def _(act):
            A = nc.scalar
            act.wait_ge(s_ln, 1)
            act.wait_ge(s_dinv, 1)
            for t in range(NT):
                last = A.activation(y_all[:, t * D:(t + 1) * D], xn_all[:, t * D:(t + 1) * D], ACT.Copy,
                                    scale=dinv[:, t:t + 1])
            last.then_inc(s_y, 1)

            def pass1_front(i, b, t, tail):
                act.wait_ge(m_tp[b], i)
                A.activation(work[b][0], xn_all[:, ds(t * D, D)], ACT.Copy).then_inc(in_place[b], 1)
                act.wait_ge(m_tp[b], i + 1)
                act.wait_ge(m_qkv[b], i)
                A.activation(nT[b], bank(1)[:, 0:D], ACT.Copy).then_inc(m_nT[b], 1)

            def pass1_back(i, b, t, tail):
                act.wait_ge(m_qkv[b], i + 1)
                act.wait_ge(m_phi[b], 2 * i)
                act.wait_ge(m_kv[b], i)
                A.activation(exp_k[b], bank(2 + b)[:, 0:D], ACT.Exp).then_inc(m_exp[b], 1)
                A.activation(rel_k[b], bank(2 + b)[:, 0:D], ACT.Relu).then_inc(m_exp[b], 1)
                A.activation(exp_q[b], bank(4 + b)[:, 0:D], ACT.Exp).then_inc(m_exp[b], 1)
                A.activation(rel_q[b], bank(4 + b)[:, 0:D], ACT.Relu).then_inc(m_exp[b], 1)
                A.activation(v_ext[b].rearrange("p (c v) -> p c v", c=KC)[:, :, 0:P],
                             bank(2 + b)[:, D:2 * D].rearrange("p (c v) -> p c v", c=KC),
                             ACT.Copy).then_inc(m_exp[b], 1)

            act.wait_ge(s_vone, 2)
            staggered(act, pass1_front, pass1_back)

            act.wait_ge(s_prow, 16)
            tiles = [act.alloc_register(f"act_tile{u}") for u in range(R)]

            def indices(g, half):
                act.reg_load(tiles, path[0:1, ds(g * R, R)])
                for u in range(R):
                    t = act.snap(tiles[u], min_val=0, max_val=ET - 1)
                    if not isinstance(g, int) or g >= 2:
                        act.wait_ge(gathered[u], 16 * g - 16)
                    A.activation(idx_g[:, half * R + u:half * R + u + 1], dst_i[:, ds(t, 1)],
                                 ACT.Copy).then_inc(idx_ready, 1)

            indices(0, 0)

            def pass2(i, b, t, tail):
                act.wait_ge(a_num[b], i)
                act.wait_ge(m_phi[b], 2 * (HALF + (1 - b)))
                A.activation(exp_q[b], qT_all[:, ds(t * D, D)], ACT.Copy).then_inc(in_place[b], 1)
                indices(t + 1, 1 - b)

            node_tiles(act, pass2)

            def ffn(i, b, t, tail):
                act.wait_ge(a_tp[b], i + 1)
                act.wait_ge(a_h[b], i)
                A.activation(nT[b], bank(0)[:, 0:D], ACT.Copy).then_inc(a_x1T[b], 1)
                act.wait_ge(a_h[b], i + 1)
                act.wait_ge(a_y[b], i)
                for o in range(KC):
                    A.activation(exp_k[b][:, o * P:(o + 1) * P], bank(1)[:, o * P:(o + 1) * P], ACT.Gelu,
                                 bias=b1_col[:, o:o + 1]).then_inc(a_hT[b], 1)
                indices(t + (NT + 1), b)

            act.wait_ge(s_small, 5 * 16)
            node_tiles(act, ffn)
            for g in range(2 * NT + 1, GROUPS):
                indices(g, g % 2)

            act.wait_ge(added, STEPS)

            def combine(i, b, t, tail):
                act.wait_ge(c_tp[b], i)
                A.activation(exp_k[b], h_all[:, ds(t * D, D)], ACT.Copy,
                             scale=dinv[:, ds(t, 1)]).then_inc(c_sc[b], 1)
                act.wait_ge(c_tp[b], i + 1)
                act.wait_ge(c_mm[b], i)
                A.activation(nT[b], bank(b)[:, 0:D], ACT.Copy).then_inc(c_T[b], 1)

            def route_in(i, b, t, tail):
                act.wait_ge(c_tp2[b], i + 1)
                act.wait_ge(c_lg[b], i)
                A.activation(exp_q[b], bank(2 + b)[:, 0:D], ACT.Copy).then_inc(c_T2[b], 1)

            node_tiles(act, combine)
            node_tiles(act, route_in)
            act.wait_ge(s_route, 1)
            A.activation(prob[:, :], logit[:, :], ACT.Exp).then_inc(s_exp, 1)

            def gelu(b, i):
                for s in range(2):
                    act.wait_ge(x_b1[2 * b + s], i + 1)
                    A.activation(hid[b][:, s * 512:(s + 1) * 512], hid[b][:, s * 512:(s + 1) * 512],
                                 ACT.Gelu).then_inc(x_g[b], 1)

            def evac_hT(b, i):
                act.wait_ge(x_ht[b], 2 * i + 1)
                act.wait_ge(x_y[b], i)
                A.activation(hidT[b][:, 0:512], bank(5), ACT.Copy).then_inc(x_hTa[b], 1)

            gelu(0, 0)
            def expert_tiles(i):
                evac_hT(0, i)
                gelu(1, i)
                evac_hT(1, i)
                gelu(0, i + 1)

            repeat(act, XT // 2 - 1, expert_tiles)
            evac_hT(0, XT // 2 - 1)
            gelu(1, XT // 2 - 1)
            evac_hT(1, XT // 2 - 1)

        @block.gpsimd
        def _(pool):
            G = nc.gpsimd
            ch = Chain(pool, s_pool)
            G.memset(h_all, 0.0).then_inc(s_hzero, 1)
            G.memset(xn_all[:, (NT - 1) * D:NT * D], 0.0).then_inc(s_hzero, 1)
            G.memset(zero_w, 0.0).then_inc(s_zero, 1)
            G.iota(iota_lo[:, 0:P * CH], pattern=[[1, P], [0, CH]], base=0, channel_multiplier=0,
                   allow_small_or_imprecise_dtypes=True).then_inc(s_const, 1)
            G.iota(iota_hi[:, 0:NT * CH], pattern=[[1, NT], [0, CH]], base=0, channel_multiplier=0,
                   allow_small_or_imprecise_dtypes=True).then_inc(s_const, 1)
            ch.link(G.memset(ident[:, :], 0.0))
            ch.link(G.affine_select(out=ident[:, :], in_=ident[:, :], compare_op=ALU.not_equal, fill=1.0,
                                    base=0, pattern=[[-1, P]], channel_multiplier=1))
            ch.link(G.memset(last_m[:, :], 0.0))
            ch.link(G.affine_select(out=last_m[:, :], in_=last_m[:, :], compare_op=ALU.not_equal, fill=1.0,
                                    base=-(P - 1), pattern=[[0, P]], channel_multiplier=1))
            ch.link(G.memset(below[:, :], 1.0))
            ch.link(G.affine_select(out=below[:, :], in_=below[:, :], compare_op=ALU.is_gt, fill=0.0,
                                    base=0, pattern=[[1, P]], channel_multiplier=-1))
            G.memset(ones_m[:, :], 1.0)
            G.iota(step_f[:, :], pattern=[[P, PC]], base=0, channel_multiplier=1,
                   allow_small_or_imprecise_dtypes=True)
            G.iota(rank_w[:, :], pattern=[[0, NT], [-1, E]], base=E, channel_multiplier=0,
                   allow_small_or_imprecise_dtypes=True)
            G.iota(xt_iota[:, :], pattern=[[1, XT], [0, E]], base=0, channel_multiplier=0,
                   allow_small_or_imprecise_dtypes=True)
            ch.link(G.memset(valid[:, :], 1.0))
            ch.link(G.affine_select(out=valid[:, :], in_=valid[:, :], compare_op=ALU.is_ge, fill=0.0,
                                    base=N - 1, pattern=[[-P, NT], [0, E]], channel_multiplier=-1))
            ch.link(G.iota(node_iota, pattern=[[1, NP_]], base=0, channel_multiplier=0,
                           allow_small_or_imprecise_dtypes=True))
            G.memset(const_end[:, :], 0.0).then_inc(s_const, 1)

            pool.wait_ge(s_deg, 1)
            for b in range(2):
                G.memset(v_ext[b], 1.0).then_inc(s_vone, 1)

            for t in range(NT):
                i, b = t // 2, t % 2
                pool.wait_ge(m_exp[b], i * 5 + 1)
                G.tensor_scalar(exp_k[b], exp_k[b], 1.0, None, ALU.min).then_inc(s_pool, 1)
                pool.wait_ge(m_exp[b], i * 5 + 3)
                G.tensor_scalar(exp_q[b], exp_q[b], 1.0, None, ALU.min).then_inc(s_pool, 1)
                pool.wait_ge(s_pool, ch.n + 1)
                G.tensor_tensor(rel_k[b], exp_k[b], rel_k[b], ALU.add).then_inc(m_phi[b], 1)
                pool.wait_ge(m_exp[b], i * 5 + 4)
                pool.wait_ge(s_pool, ch.n + 2)
                G.tensor_tensor(qT_all[:, t * D:(t + 1) * D], exp_q[b], rel_q[b], ALU.add).then_inc(m_phi[b], 1)
                ch.n += 2

            pool.wait_ge(s_ytab, 16)
            pool.wait_ge(s_moe0, 16)
            pool.wait_ge(m_kv[0], 1)
            zero_reg = pool.alloc_register("gather_zero")
            bound = pool.alloc_register("gather_bound")
            pool.reg_mov(zero_reg, 0)

            def gathers(g, half):
                for u in range(R):
                    pool.wait_ge(idx_ready, g * R + u + 1)
                    if i_is_late(g):
                        pool.wait_ge(summed[u], g)
                    pool.reg_add(bound, zero_reg, NP_ - 1)
                    at = half * R + u
                    G.indirect_dma_start(out=rows_g[u], out_offset=None, in_=y_table,
                                         in_offset=bass.IndirectOffsetOnAxis(ap=idx_g[:, at:at + 1], axis=0),
                                         bounds_check=bound, oob_is_err=True).then_inc(gathered[u], 16)

            def two_groups(i):
                gathers(i * 2, 0)
                gathers(i * 2 + 1, 1)

            repeat(pool, GROUPS // 2, two_groups)
            gathers(GROUPS - 1, 0)

            pool.wait_ge(s_slot, 2)
            pool.wait_ge(s_xn, NT)
            for t in range(NT):
                n = TAIL if t == NT - 1 else P
                for slot in (slot_1, slot_2):
                    G.indirect_dma_start(out=moe_in, out_offset=bass.IndirectOffsetOnAxis(ap=slot[0:n, t:t + 1], axis=0),
                                         in_=h_all[0:n, t * D:(t + 1) * D], in_offset=None,
                                         bounds_check=SLOTS - 1, oob_is_err=True).then_inc(s_scat, 16)

            pool.wait_ge(x_out[0], 16 * (XT // 2))
            pool.wait_ge(x_out[1], 16 * (XT // 2))
            pool.wait_ge(x_y[0], XT // 2)
            pool.wait_ge(x_y[1], XT // 2)
            for t in range(NT):
                n = TAIL if t == NT - 1 else P
                b, i = t % 2, t // 2
                if i:
                    pool.wait_ge(f_y[b], i)
                for rows, slot, done in ((fin_1, slot_1, f_1), (fin_2, slot_2, f_2)):
                    G.indirect_dma_start(out=rows[b][0:n], out_offset=None, in_=moe_out,
                                         in_offset=bass.IndirectOffsetOnAxis(ap=slot[0:n, t:t + 1], axis=0),
                                         bounds_check=SLOTS - 1, oob_is_err=True).then_inc(done[b], 16)

        @block.sync
        def _(sp):
            sp.dma_start(src_i[0:EP, :], src.rearrange("(p c) -> p c", c=EC)).then_inc(s_edges, 16)
            sp.dma_start(dst_e[0:EP, :], dst.rearrange("(p c) -> p c", c=EC)).then_inc(s_edges, 16)
            full = (NT - 1) * P
            sp.dma_start(xn_all[:, 0:(NT - 1) * D].rearrange("p (t d) -> p t d", d=D),
                         x[0:full, :].rearrange("(t p) d -> p t d", p=P)).then_inc(s_x, 16)
            sp.wait_ge(s_hzero, 2)
            sp.dma_start(xn_all[0:TAIL, (NT - 1) * D:NT * D], x[full:N, :]).then_inc(s_x, 16)
            for w_sb, w_d, n in ((wqkv_sb, wqkv_t, 3 * D), (w1_sb, w1_t, D), (w2_sb, w2_t, D), (gw_sb, gnn_w, D)):
                sp.dma_start(w_sb.rearrange("p (k n) -> p k n", n=n),
                             w_d.rearrange("(k p) n -> p k n", p=P)).then_inc(s_wts, 16)
            for r, v in zip((ln1g_r, ln1b_r, ln2g_r, ln2b_r, b2_r, gb_r), (ln1_g, ln1_b, ln2_g, ln2_b, b2, gnn_b)):
                sp.dma_start(r, rep(v, D)).then_inc(s_reps, 16)
            with nc.allow_non_contiguous_dma(reason="a few columns"):
                sp.dma_start(b1_col[:, :], b1.rearrange("(k p) -> p k", p=P)).then_inc(s_small, 16)
                sp.dma_start(eg_col[:, :], ffn_g.rearrange("e (k p) -> p (e k)", p=P)).then_inc(s_small, 16)
                sp.dma_start(eb_col[:, :], ffn_b.rearrange("e (k p) -> p (e k)", p=P)).then_inc(s_small, 16)
            sp.dma_start(wr_sb[:, :, :], wr.rearrange("(k p) e -> p k e", p=P)).then_inc(s_small, 16)
            sp.dma_start(br_r[:, :], rep(br, E)).then_inc(s_small, 16)
            sp.wait_ge(s_y, 1)
            sp.dma_start(y_table.rearrange("(t p) d -> p t d", p=P),
                         y_all.rearrange("p (t d) -> p t d", d=D)).then_inc(s_ytab, 16)
            sp.wait_ge(s_zero, 1)
            sp.dma_start(moe_in.rearrange("(p s) d -> p s d", p=P),
                         zero_w.unsqueeze(1).broadcast_to([P, XT, D])).then_inc(s_moe0, 16)
            sp.wait_ge(s_tiles, 1)
            with nc.allow_non_contiguous_dma(reason="a column of tile numbers"):
                sp.dma_start(path_dram.rearrange("a (c p) -> p (a c)", p=P), tile_i[:, :]).then_inc(s_pdram, 16)
            sp.wait_ge(s_pdram, 16)
            sp.dma_start(path[:, :], path_dram).then_inc(s_prow, 16)

            def combine(i, b, t, tail):
                n = TAIL if tail else P
                sp.wait_ge(c_x2[b], i)
                sp.dma_start(rows_g[b][0:n], x[ds(t * P, n), :]).then_inc(c_x[b], 16)
                sp.wait_ge(c_x2[b], i + 1)
                sp.dma_start(x2_rows[ds(t * P, P), :], work[b][1]).then_inc(c_x2o[b], 16)

            sp.wait_ge(added, STEPS)
            node_tiles(sp, combine)

            sp.wait_ge(c_lc[0], HALF + 1)
            sp.wait_ge(c_lc[1], HALF)
            sp.dma_start(w1_all.rearrange("p (e k f) -> p e k f", e=E, k=KC),
                         ffn_w1.rearrange("e (k p) f -> p e k f", p=P)).then_inc(s_w1, 16)
            sp.wait_ge(c_x2o[0], 16 * (HALF + 1))
            sp.wait_ge(c_x2o[1], 16 * HALF)
            sp.dma_start(b2_all, ffn_b2.rearrange("(a e) d -> a (e d)", a=1).broadcast_to([P, E * D])).then_inc(s_bias, 16)
            sp.dma_start(b1_all, ffn_b1.rearrange("(a e) f -> a (e f)", a=1).broadcast_to([P, E * F])).then_inc(s_bias, 16)
            sp.wait_ge(s_scat, 2 * NT * 16)

            def load_xd(b, i):
                sp.wait_ge(x_tp[b], i)
                sp.dma_start(xd[b], moe_in[ds((i * 2 + b) * P, P), :]).then_inc(x_in[b], 16)

            load_xd(0, 0)
            load_xd(1, 0)
            sp.dma_start(w2_all.rearrange("p (e k d) -> p e k d", e=E, k=FC),
                         ffn_w2.rearrange("e (k p) d -> p e k d", p=P)).then_inc(s_w2, 16)
            def expert_tiles(i):
                for b in range(2):
                    load_xd(b, i + 1)
                    sp.wait_ge(x_yb[b], i + 1)
                    sp.dma_start(moe_out[ds((i * 2 + b) * P, P), :], yt[b]).then_inc(x_out[b], 16)

            repeat(sp, XT // 2 - 1, expert_tiles)
            for b in range(2):
                sp.wait_ge(x_yb[b], XT // 2)
                sp.dma_start(moe_out[(XT - 2 + b) * P:(XT - 1 + b) * P, :], yt[b]).then_inc(x_out[b], 16)

            sp.wait_ge(x_y[0], XT // 2)
            sp.wait_ge(x_y[1], XT // 2)

            def load_f(t):
                n = TAIL if t == NT - 1 else P
                b, i = t % 2, t // 2
                if i:
                    sp.wait_ge(f_out[b], 16 * i)
                sp.dma_start(fin_x[b][0:n], x2_rows[t * P:t * P + n, :]).then_inc(f_x[b], 16)

            load_f(0)
            load_f(1)
            for t in range(NT):
                n = TAIL if t == NT - 1 else P
                b, i = t % 2, t // 2
                sp.wait_ge(f_y[b], i + 1)
                sp.dma_start(out[t * P:t * P + n, :], fin_x[b][0:n]).then_inc(f_out[b], 16)
                if t + 2 < NT:
                    load_f(t + 2)
            sp.wait_ge(f_out[0], 16 * (HALF + 1))
            sp.wait_ge(f_out[1], 16 * HALF)


_INS = ["x", "src", "dst", "L0_gnn_W", "L0_gnn_b", "L0_mix_Wqkv", "L0_mix_ln1_g", "L0_mix_ln1_b", "L0_mix_W1",
        "L0_mix_b1", "L0_mix_W2", "L0_mix_b2", "L0_mix_ln2_g", "L0_mix_ln2_b", "L0_ffn_Wr", "L0_ffn_br",
        "L0_ffn_ln_g", "L0_ffn_ln_b", "L0_ffn_W1", "L0_ffn_b1", "L0_ffn_W2", "L0_ffn_b2"]
_TRANSPOSED = {"L0_mix_Wqkv", "L0_mix_W1", "L0_mix_W2"}


def kernel(**inputs):
    import numpy as _np
    import concourse.bacc as _bacc
    from concourse import mybir as _mybir
    from concourse.bass_utils import run_bass_kernel_spmd as _run

    nc = _bacc.Bacc("TRN2", target_bir_lowering=False, num_devices=1)
    arrays, args = {}, []
    for name in _INS:
        a = _np.asarray(inputs[name])
        a = _np.ascontiguousarray(a.T if name in _TRANSPOSED else a)
        arrays[f"in_{name}"] = a
        args.append(nc.dram_tensor(f"in_{name}", a.shape, _mybir.dt.from_np(a.dtype), kind="ExternalInput").ap())
    out = nc.dram_tensor("out_x", inputs["x"].shape, _mybir.dt.float32, kind="ExternalOutput").ap()
    gps_layer(nc, *args, out)
    r = _run(nc, [arrays], core_ids=[0])
    return r.results[0]["out_x"]
```

```python
from contextlib import ExitStack

import concourse.bass as bass
from concourse import mybir

ALU = mybir.AluOpType
ACT = mybir.ActivationFunctionType
AX = mybir.AxisListType
F32 = mybir.dt.float32
BF16 = mybir.dt.bfloat16
I32 = mybir.dt.int32
ds = bass.ds

P = 128


class Chain:

    def __init__(self, engine, sem, base=0):
        self.engine, self.sem, self.base, self.n = engine, sem, base, 0

    def link(self, ins):
        ins.then_inc(self.sem, 1)
        self.n += 1
        self.engine.wait_ge(self.sem, self.base + self.n)

    def count(self, ins):
        ins.then_inc(self.sem, 1)
        self.n += 1


def gps_layer(nc, x, src, dst, gnn_w, gnn_b, wqkv_t, ln1_g, ln1_b, w1_t, b1, w2_t, b2, ln2_g, ln2_b,
              wr, br, ffn_g, ffn_b, ffn_w1, ffn_b1, ffn_w2, ffn_b2, out):
    N, D = x.shape
    EDGES = src.shape[0]
    H = 8
    HD = D // H
    E, _, F = ffn_w1.shape
    EPS = 1e-5
    EPS_ATTN = 1e-6
    KC = D // P
    FC = F // P
    NT = -(-N // P)
    TAIL = N - (NT - 1) * P
    NP_ = NT * P
    HALF = NT // 2
    assert NT % 2 == 1 and KC == 2 and TAIL <= 64

    EP = 125
    EC = EDGES // EP
    CH = 85
    NCH = EC // CH
    assert EP * EC == EDGES and CH * NCH == EC
    DBITS = 12
    SC = 512
    PAD_KEY = float(NP_ << DBITS)
    ET = -(-EDGES // P)
    STEPS = ET + NT - 1
    R = 8
    GROUPS = STEPS // R
    assert STEPS % R == 0 and GROUPS > 2 * NT and GROUPS % 2 == 1 and (NP_ << DBITS) < 1 << 24 and NP_ <= 1 << DBITS
    PC = -(-STEPS // P)

    XT = -(-(2 * N) // P) + E - 1
    XT += XT % 2
    SLOTS = XT * P

    with ExitStack() as ctx:
        def sb(name, shape, dt=F32):
            return ctx.enter_context(nc.sbuf_tensor(name, shape, dt))

        def sem(name):
            return ctx.enter_context(nc.semaphore(name))

        def sems(name, n=2):
            return [sem(f"{name}{i}") for i in range(n)]

        y_table = nc.dram_tensor("y_table", [NP_, D], F32, kind="Internal").ap()
        x2_rows = nc.dram_tensor("x2_rows", [NP_, D], F32, kind="Internal").ap()
        path_dram = nc.dram_tensor("path_dram", [1, PC * P], I32, kind="Internal").ap()
        moe_in = nc.dram_tensor("moe_in", [SLOTS, D], F32, kind="Internal").ap()
        moe_out = nc.dram_tensor("moe_out", [SLOTS, D], F32, kind="Internal").ap()

        arena_a = sb("arena_a", [P, E * KC * F])
        arena_b = sb("arena_b", [P, E * FC * D + E * F])
        arena_w = sb("arena_w", [P, 7680])

        def carve(arena, at, n, dt=F32):
            v = arena[:, at:at + n]
            return v if dt == F32 else v.bitcast(dt)

        LO_F, HI_F = CH * P // 2, -(-CH * NT // 2)
        oh_lo = [carve(arena_a, b * LO_F, LO_F, BF16) for b in range(2)]
        oh_hi = [carve(arena_a, 2 * LO_F + b * HI_F, HI_F, BF16) for b in range(2)]
        qT_all = carve(arena_a, 0, KC * NP_)
        at = KC * NP_
        key_i = carve(arena_a, at, ET, I32); at += ET
        dst_i = carve(arena_a, at, ET, I32); at += ET
        tmp_i = carve(arena_a, at, ET, I32); at += ET
        src_f = carve(arena_a, at, ET); at += ET
        end_f = carve(arena_a, at, ET); at += ET
        cmp_f = carve(arena_a, at, ET); at += ET
        nT = [carve(arena_a, at + b * D, D) for b in range(2)]; at += 2 * D
        exp_k = [carve(arena_a, at + b * D, D) for b in range(2)]; at += 2 * D
        exp_q = [carve(arena_a, at + b * D, D) for b in range(2)]; at += 2 * D
        rel_k = [carve(arena_a, at + b * D, D) for b in range(2)]; at += 2 * D
        rel_q = [carve(arena_a, at + b * D, D) for b in range(2)]; at += 2 * D
        VW = P + 4
        v_ext = [carve(arena_a, at + b * KC * VW, KC * VW) for b in range(2)]; at += 2 * KC * VW
        assert at <= 13056
        at = 13056
        wqkv_sb = carve(arena_a, at, KC * 3 * D); at += KC * 3 * D
        w1_sb = carve(arena_a, at, KC * D); at += KC * D
        w2_sb = carve(arena_a, at, KC * D); at += KC * D
        gw_sb = carve(arena_a, at, KC * D); at += KC * D
        assert at <= E * KC * F
        xn_all = carve(arena_b, 0, NT * D); at = NT * D
        assert ET <= SC
        iota = carve(arena_b, at, SC); at += SC
        h_odd = carve(arena_b, at, NT * D)
        rows_s = [carve(arena_b, at + b * SC, SC) for b in range(2)]; at += 2 * SC
        cols_s = [carve(arena_b, at + b * SC, SC) for b in range(2)]; at += 2 * SC
        y_all = carve(arena_b, at, NT * D)
        H_AT = E * FC * D + E * F - NT * D
        odd = H_AT - R * D - R * P
        rows_odd = [carve(arena_b, odd + u * D, D) for u in range(R)]
        hot_odd = [carve(arena_b, odd + R * D + u * P, P) for u in range(R)]
        assert NT * D + SC + NT * D <= odd
        iota_lo = carve(arena_b, at, LO_F, BF16)
        iota_hi = carve(arena_b, at + LO_F, HI_F, BF16)
        h_all = carve(arena_b, H_AT, NT * D)
        assert at + max(LO_F + HI_F, NT * D) <= H_AT and E * FC * D + E * FC <= H_AT
        at = 0
        reps = []
        for _ in range(4):
            reps.append(carve(arena_w, at, D)); at += D
        ln2g_r, ln2b_r, b2_r, gb_r = reps
        rows_g = [carve(arena_w, at + u * D, D) for u in range(R)]; at += R * D
        hot_g = [carve(arena_w, at + u * P, P) for u in range(R)]; at += R * P
        work = [[carve(arena_w, at + (3 * b + k) * D, D) for k in range(3)] for b in range(2)]; at += 6 * D
        zero_w = rows_g[0]
        rows_of, hot_of = (rows_g, rows_odd), (hot_g, hot_odd)
        e0, EB = 4 * D + D, -(-EC // 2)
        src_i = carve(arena_w, e0, EC, I32)
        dst_e = carve(arena_w, e0 + EC, EC, I32)
        part_i = carve(arena_w, e0 + 2 * EC, EC, I32)
        lo_b = carve(arena_w, e0 + 3 * EC, EB, BF16)[:, 0:EC]
        hi_b = carve(arena_w, e0 + 3 * EC + EB, EB, BF16)[:, 0:EC]
        assert 3 * EC + 2 * EB <= (R - 1) * D
        assert at <= 7680
        w1_all = carve(arena_a, 0, E * KC * F)
        w2_all = carve(arena_b, 0, E * FC * D)
        b1_all = carve(arena_b, E * FC * D, E * FC)
        w1_now = [carve(arena_b, H_AT + b * KC * F, KC * F) for b in range(2)]
        at = 0
        b2_all = carve(arena_w, at, E * D); at += E * D
        xd = [carve(arena_w, at + b * D, D) for b in range(2)]; at += 2 * D
        xeT = [carve(arena_w, at + b * D, D) for b in range(2)]; at += 2 * D
        hidT = [carve(arena_w, at + b * F, F) for b in range(2)]; at += 2 * F
        yt = [carve(arena_w, at + b * D, D) for b in range(2)]; at += 2 * D
        assert at <= 7680
        SETS = 5
        fin_x = [carve(arena_a, b * D, D) for b in range(SETS)]
        fin_1 = [carve(arena_a, (SETS + b) * D, D) for b in range(SETS)]
        fin_2 = [carve(arena_a, (2 * SETS + b) * D, D) for b in range(SETS)]
        assert NT % SETS == 0

        ident = sb("ident", [P, P])
        below = sb("below", [P, P])
        ones_m = sb("ones_m", [P, P])
        last_m = sb("last_m", [P, P])
        step_f = sb("step_f", [P, PC])
        block_at = sb("block_at", [P, NT])
        tile_f = sb("tile_f", [P, PC])
        tile_i = sb("tile_i", [P, PC], I32)
        path = sb("path", [1, PC * P], I32)
        idx_g = sb("idx_g", [P, 2 * R], I32)
        stats = sb("stats", [P, NT, 6])
        mv = sb("mv", [P, NT, 2])
        rstd = sb("rstd", [P, NT])
        nw_v = sb("nw_v", [P, NT])
        nw_i = sb("nw_i", [P, NT], I32)
        nw_a = sb("nw_a", [P, NT])
        deg = sb("deg", [P, NT])
        has = sb("has", [P, NT])
        dinv = sb("dinv", [P, NT])
        stats_flat = stats[:, :, :].rearrange("p t six -> p (t six)")
        mv_flat = mv[:, :, :].rearrange("p t two -> p (t two)")
        kvbd = sb("kvbd", [P, KC, VW])
        zden = sb("zden", [P, 2, H])
        g1_col = sb("g1_col", [P, KC])
        o1_col = sb("o1_col", [P, KC])
        b1_col = sb("b1_col", [P, KC])
        wr_sb = sb("wr_sb", [P, KC, E])
        br_r = sb("br_r", [P, E])
        eg_col = sb("eg_col", [P, E * KC])
        eb_col = sb("eb_col", [P, E * KC])
        NE = NT * E
        logit = sb("logit", [P, NE])
        prob = sb("prob", [P, NE])
        hot1 = sb("hot1", [P, NE])
        hot2 = sb("hot2", [P, NE])
        rt_a = sb("rt_a", [P, NE])
        rt_b = sb("rt_b", [P, NE])
        rank_w = sb("rank_w", [P, NE])
        valid = sb("valid", [P, NE])
        c_m = sb("c_m", [P, NT])
        slot_f = sb("slot_f", [P, NT])
        shift = slot_f
        c_s = sb("c_s", [P, NT])
        p_1 = sb("p_1", [P, NT])
        p_2 = sb("p_2", [P, NT])
        wt_1 = sb("wt_1", [P, NT])
        wt_2 = sb("wt_2", [P, NT])
        slot_1 = sb("slot_1", [P, NT], I32)
        slot_2 = sb("slot_2", [P, NT], I32)
        e_f = sb("e_f", [P, E])
        e_cum = sb("e_cum", [P, E])
        e_base = sb("e_base", [P, E])
        e_i = sb("e_i", [P, E], I32)
        xt_iota = carve(arena_w, 6144, XT * E)[0:1]
        xt_cmp = carve(arena_w, 6144 + XT * E, XT * E)[0:1]
        xt_f = sb("xt_f", [1, XT])
        expert_of = sb("expert_of", [1, XT + 2], I32)
        const_end = sb("const_end", [1, 2])

        ps = ctx.enter_context(nc.psum_tensor("ps", [P, 8, 512], F32))

        s_edges = sem("s_edges"); s_x = sem("s_x"); s_wts = sem("s_wts"); s_reps = sem("s_reps")
        s_const = sem("s_const"); s_pool = sem("s_pool"); s_hzero = sem("s_hzero")
        s_dve0 = sem("s_dve0")
        oh_ready = sems("oh_ready"); oh_used = sems("oh_used"); s_deg = sem("s_deg")
        s_ln = sem("s_ln"); s_dinv = sem("s_dinv"); s_y = sem("s_y"); s_ytab = sem("s_ytab")
        s_sort = sem("s_sort"); s_turned = sem("s_turned")
        s_path = sem("s_path"); s_last = sem("s_last"); s_tiles = sem("s_tiles"); s_pdram = sem("s_pdram")
        s_prow = sem("s_prow")
        m_tp = sems("m_tp"); m_nT = sems("m_nT"); m_qkv = sems("m_qkv"); m_exp = sems("m_exp")
        m_phi = sems("m_phi"); m_kv = sems("m_kv"); s_vone = sem("s_vone"); s_bd = sem("s_bd")
        a_num = sems("a_num"); a_x1 = sems("a_x1"); a_tp = sems("a_tp"); a_x1T = sems("a_x1T")
        a_h = sems("a_h"); a_hT = sems("a_hT"); a_y = sems("a_y"); a_out = sems("a_out")
        s_tile = sem("s_tile"); s_xn = sem("s_xn"); s_means = sem("s_means"); a_s = sems("a_s")
        idx_ready = sem("idx_ready"); gathered = sems("gathered", 2 * R)
        hot_ready = sem("hot_ready"); summed = sem("summed"); added = sem("added")
        c_sc = sems("c_sc"); c_tp = sems("c_tp"); c_T = sems("c_T"); c_mm = sems("c_mm")
        c_x = sems("c_x"); c_n = sem("c_n"); c_fifth = sem("c_fifth"); c_w = sem("c_w"); c_x2 = sems("c_x2"); c_x2o = sems("c_x2o")
        c_xt = sems("c_xt"); c_tp2 = sems("c_tp2"); c_T2 = sems("c_T2"); c_lg = sem("c_lg")
        c_lc = sem("c_lc")
        s_zero = sem("s_zero"); s_small = sem("s_small"); s_moe0 = sem("s_moe0"); s_bias = sem("s_bias")
        in_place = sems("in_place")
        s_route = sem("s_route"); s_exp = sem("s_exp")
        s_cnt = sem("s_cnt"); s_rank = sem("s_rank"); s_slot = sem("s_slot"); s_etab = sem("s_etab")
        s_scat = sem("s_scat"); s_w1 = sem("s_w1"); s_w2 = sem("s_w2")
        x_in = sems("x_in"); x_tp = sems("x_tp"); x_T = sems("x_T"); x_h = sems("x_h", 4)
        x_g = sems("x_g", 4); x_w1 = sems("x_w1"); x_y = sems("x_y"); x_yb = sems("x_yb"); x_out = sems("x_out")
        f_x = sems("f_x", SETS); f_y = sem("f_y"); f_out = sems("f_out", SETS)
        f_1, f_2 = gathered[0:SETS], gathered[R:R + SETS]
        F1_BASE, F2_BASE = 16 * (GROUPS - GROUPS // 2), 16 * (GROUPS // 2)

        def rep(v, n):
            return v.rearrange("(a n) -> a n", a=1).broadcast_to([P, n])

        def bank(k):
            return ps[:, k, :]

        PH_ROWS = 8
        turns = []

        def node_tiles(engine, body):
            body(0, 0, 0, False)
            body(0, 1, 1, False)
            with engine.Fori(1, HALF) as i:
                body(i, 0, i * 2, False)
                body(i, 1, i * 2 + 1, False)
            body(HALF, 0, NT - 1, True)

        def staggered(engine, front, back, peel=False):
            def turn(i, tail=False):
                front(i, 1, i * 2 + 1, False)
                back(i, 0, i * 2, False)
                front(i + 1, 0, i * 2 + 2, tail)
                back(i, 1, i * 2 + 1, False)

            front(0, 0, 0, False)
            turn(0)
            with engine.Fori(1, HALF - 1 if peel else HALF) as i:
                turn(i)
            if peel:
                turn(HALF - 1, True)
            back(HALF, 0, NT - 1, True)

        def repeat(engine, n, body):
            body(0)
            with engine.Fori(1, n) as i:
                body(i)

        def step_sum(u):
            return ps[:, 4 + u // 2, (u % 2) * D:(u % 2 + 1) * D]

        def i_is_late(t):
            return not (isinstance(t, int) and t == 0)

        block = ctx.enter_context(nc.Block())

        @block.vector
        def _(dve):
            V = nc.vector
            ch = Chain(dve, s_dve0)

            def inv_sqrt(c, dst, var, eps):
                c.link(V.tensor_scalar(nw_v[:, :], var, eps, None, ALU.add))
                c.link(V.tensor_single_scalar(nw_i[:, :], nw_v[:, :].bitcast(I32), 1, ALU.logical_shift_right))
                c.link(V.tensor_scalar(dst[:, :].bitcast(I32), nw_i[:, :], -1.0, float(0x5F3759DF), ALU.mult, ALU.add))
                for _ in range(3):
                    c.link(V.tensor_tensor(nw_a[:, :], dst[:, :], dst[:, :], ALU.mult))
                    c.link(V.tensor_tensor(nw_a[:, :], nw_a[:, :], nw_v[:, :], ALU.mult))
                    c.link(V.tensor_scalar(nw_a[:, :], nw_a[:, :], -0.5, 1.5, ALU.mult, ALU.add))
                    c.link(V.tensor_tensor(dst[:, :], dst[:, :], nw_a[:, :], ALU.mult))

            V.memset(rows_s[0], PAD_KEY).then_inc(s_sort, 1)
            V.memset(kvbd[:, :, :], 0.0).then_inc(s_bd, 1)
            dve.wait_ge(s_edges, 32)
            dve.wait_ge(s_sort, 1)
            V.scalar_tensor_tensor(out=rows_s[0][0:EP, 0:EC], in0=src_i[0:EP, :], scalar=float(1 << DBITS),
                                   in1=dst_e[0:EP, :], op0=ALU.mult, op1=ALU.add).then_inc(s_sort, 1)
            n_sort = [2]
            cur = [0, 0]

            def settle():
                dve.wait_ge(s_sort, n_sort[0])

            def exchange(which, dist):
                a = (rows_s, cols_s)[which]
                s = a[cur[which]].rearrange("p (a two d) -> p a two d", two=2, d=dist)
                o = a[1 - cur[which]].rearrange("p (a two d) -> p a two d", two=2, d=dist)
                V.tensor_tensor(o[:, :, 0, :], s[:, :, 0, :], s[:, :, 1, :], ALU.min).then_inc(s_sort, 1)
                V.tensor_tensor(o[:, :, 1, :], s[:, :, 0, :], s[:, :, 1, :], ALU.max).then_inc(s_sort, 1)
                n_sort[0] += 2
                settle()
                cur[which] = 1 - cur[which]

            def negate(view):
                V.tensor_scalar(view, view, -1.0, None, ALU.mult).then_inc(s_sort, 1)
                n_sort[0] += 1
                settle()

            def turn(to_cols):
                turns.append((to_cols, cur[0 if to_cols else 1], n_sort[0]))
                k = len(turns)
                dve.wait_ge(s_turned, k)
                b = bank(0)
                if to_cols:
                    cur[1] = 0
                    V.tensor_copy(cols_s[0].rearrange("q (p c) -> q c p", c=4),
                                  b.rearrange("q (c p) -> q c p", c=4)).then_inc(s_sort, 1)
                else:
                    cur[0] = 0
                    V.tensor_copy(rows_s[0], b).then_inc(s_sort, 1)
                n_sort[0] += 1
                settle()

            def half_view(a, h):
                return a.rearrange("p (a two h) -> p a two h", two=2, h=h)[:, :, 1, :]

            def mid_view(a, h):
                return a.rearrange("p (a q h) -> p a q h", q=4, h=h)[:, :, 1:3, :]

            settle()
            negate(half_view(rows_s[0], 2))
            for k in range(1, PH_ROWS + 1):
                for j in range(k - 1, -1, -1):
                    exchange(0, 1 << j)
                if k < PH_ROWS:
                    negate(mid_view(rows_s[cur[0]], 1 << k))
            negate(rows_s[cur[0]][:, SC // 2:SC])

            ch.link(V.tensor_single_scalar(part_i[0:EP, :], src_i[0:EP, :], P - 1, ALU.bitwise_and))
            ch.link(V.tensor_copy(lo_b[0:EP, :], part_i[0:EP, :]))
            ch.link(V.tensor_single_scalar(part_i[0:EP, :], src_i[0:EP, :], 7, ALU.logical_shift_right))
            ch.link(V.tensor_copy(hi_b[0:EP, :], part_i[0:EP, :]))
            dve.wait_ge(s_const, 2)
            for c in range(NCH):
                b = c % 2
                if c >= 2:
                    dve.wait_ge(oh_used[b], c // 2)
                lo = lo_b[0:EP, c * CH:(c + 1) * CH].unsqueeze(1).broadcast_to([EP, P, CH])
                hi = hi_b[0:EP, c * CH:(c + 1) * CH].unsqueeze(1).broadcast_to([EP, NT, CH])
                V.tensor_tensor(oh_lo[b][0:EP, 0:P * CH].rearrange("p (n c) -> p n c", c=CH), lo,
                                iota_lo[0:EP, 0:P * CH].rearrange("p (n c) -> p n c", c=CH),
                                ALU.is_equal).then_inc(oh_ready[b], 1)
                V.tensor_tensor(oh_hi[b][0:EP, 0:NT * CH].rearrange("p (n c) -> p n c", c=CH), hi,
                                iota_hi[0:EP, 0:NT * CH].rearrange("p (n c) -> p n c", c=CH),
                                ALU.is_equal).then_inc(oh_ready[b], 1)
            dve.wait_ge(s_x, 32)
            dve.wait_ge(s_hzero, 1)
            for t in range(NT):
                last = V.bn_stats(stats[:, t, :], xn_all[:, t * D:(t + 1) * D])
            ch.link(last)
            for t in range(NT):
                last = V.bn_aggr(mv[:, t, :], stats[:, t, :])
            ch.link(last)
            inv_sqrt(ch, rstd, mv[:, :, 1], EPS)
            V.scalar_tensor_tensor(out=shift[:, :], in0=mv[:, :, 0], scalar=-1.0, in1=rstd[:, :],
                                   op0=ALU.mult, op1=ALU.mult).then_inc(s_means, 1)
            dve.wait_ge(s_deg, 1)
            ch.link(V.tensor_copy(deg[:, :], bank(7)[:, 0:NT]))
            ch.link(V.tensor_scalar(has[:, :], deg[:, :], 0.0, None, ALU.is_gt))
            ch.link(V.tensor_scalar(deg[:, :], deg[:, :], 1.0, None, ALU.max))
            inv_sqrt(ch, deg, deg[:, :], 0.0)
            V.tensor_tensor(dinv[:, :], deg[:, :], has[:, :], ALU.mult).then_inc(s_dinv, 1)

            turn(True)
            negate(half_view(cols_s[0], 4))
            for k in range(PH_ROWS + 1, 17):
                for j in range(k - 8, -1, -1):
                    exchange(1, 1 << j)
                turn(False)
                for j in range(6, -1, -1):
                    exchange(0, 1 << j)
                turn(True)
                if k < 15:
                    negate(mid_view(cols_s[0], 1 << (k - 7)))
                elif k == 15:
                    negate(cols_s[0][:, SC // 2:SC])

            ch.link(V.tensor_copy(key_i, cols_s[0][:, 0:ET]))
            ch.link(V.tensor_single_scalar(dst_i, key_i, (1 << DBITS) - 1, ALU.bitwise_and))
            ch.link(V.tensor_single_scalar(tmp_i, key_i, DBITS, ALU.logical_shift_right))
            ch.link(V.tensor_copy(src_f, tmp_i))
            ch.link(V.tensor_single_scalar(tmp_i, key_i, DBITS + 7, ALU.logical_shift_right))
            ch.link(V.tensor_copy(cmp_f, tmp_i))
            dve.wait_ge(s_const, 3)
            V.tensor_tensor(end_f[:, 0:ET - 1], cmp_f[:, 0:ET - 1], iota[:, 0:ET - 1],
                            ALU.add).then_inc(s_path, 1)
            dve.wait_ge(s_last, 1)
            for c in range(PC):
                ch.link(V.tensor_scalar(cmp_f[:, 0:ET - 1], bank(0)[:, 0:ET - 1], step_f[:, c:c + 1], None,
                                        ALU.is_lt))
                ch.link(V.tensor_reduce(tile_f[:, c:c + 1], cmp_f[:, 0:ET - 1], AX.X, ALU.add))
            V.tensor_copy(tile_i[:, :], tile_f[:, :]).then_inc(s_tiles, 1)

            dve.wait_ge(m_kv[0], HALF + 1)
            dve.wait_ge(m_kv[1], HALF)
            dve.wait_ge(s_bd, 1)
            for c in range(KC):
                for h in range(4):
                    r = slice(h * HD, (h + 1) * HD)
                    V.tensor_copy(kvbd[r, c, r], bank(6 + c)[r, r]).then_inc(s_bd, 1)
                    V.tensor_copy(kvbd[r, c, P + h:P + h + 1], bank(6 + c)[r, P:P + 1]).then_inc(s_bd, 1)

            tiles = [dve.alloc_register(f"dve_tile{u}") for u in range(R)]

            def group_at(g):
                dve.reg_load(tiles, path[0:1, ds(g * R, R)])
                at_tile = [dve.snap(r, min_val=0, max_val=ET - 1) for r in tiles]
                at_block = [nc.s_assert_within(
                    dve.snap(g * R + u - at_tile[u]), 0, NT - 1,
                    skip_runtime_bounds_check_because="a step moves either the tile or the block on")
                            for u in range(R)]
                return at_tile, at_block

            def make_hots(g, half):
                at_tile, at_block = group_at(g)
                for u in range(R):
                    V.tensor_scalar(hot_of[half][u], iota[:, 0:P], block_at[:, ds(at_block[u], 1)],
                                    src_f[:, ds(at_tile[u], 1)], ALU.add, ALU.is_equal).then_inc(hot_ready, 1)

            def sum_rows(g):
                at_block = group_at(g)[1]
                for u in range(R):
                    if u == 0:
                        dve.wait_ge(summed, g * R + R)
                    if u > 1 or i_is_late(g):
                        dve.wait_ge(added, g * R + (u - 1))
                    block_h = (h_all, h_odd)[u % 2][:, ds(at_block[u] * D, D)]
                    V.tensor_tensor(block_h, block_h, step_sum(u), ALU.add).then_inc(added, 1)

            def moments(c, rows, t):
                c.count(V.bn_stats(stats_flat[:, ds(t * 6, 6)], rows))

            def keep(out_, in_):
                return V.tensor_scalar(out_, in_, 1.0, None, ALU.mult)

            def means(c):
                dve.wait_ge(s_tile, c.base)
                for t in range(NT):
                    last = V.bn_aggr(mv[:, t, :], stats[:, t, :])
                c.link(last)
                inv_sqrt(c, rstd, mv[:, :, 1], EPS)

            def normed(out_, in_, t):
                return V.tensor_scalar(out_, in_, mv_flat[:, ds(t * 2, 1)], rstd[:, ds(t, 1)],
                                       ALU.subtract, ALU.mult)

            def tile_of(a, t):
                return a[:, ds(t * D, D)]

            per = 5
            base = [0]

            def pass2(i, b, t, tail):
                if i_is_late(t):
                    sum_rows(t - 1)
                c = Chain(dve, s_tile, t * per + base[0])
                w0 = work[b][0]
                dve.wait_ge(a_num[b], i + 1)
                num = bank(b)[:, 0:KC * VW].rearrange("p (c v) -> p c v", c=KC)
                z = zden[:, b, :].rearrange("p (c h) -> p c h", c=KC)
                c.link(V.tensor_scalar(z, num[:, :, P:VW], EPS_ATTN, None, ALU.add))
                c.link(V.reciprocal(zden[:, b, :], zden[:, b, :]))
                for cc in range(KC):
                    ins = V.tensor_tensor(w0[:, cc * P:(cc + 1) * P].rearrange("p (h d) -> p h d", d=HD),
                                          num[:, cc, 0:P].rearrange("p (h d) -> p h d", d=HD),
                                          zden[:, b, cc * 4:cc * 4 + 4].unsqueeze(2).broadcast_to([P, 4, HD]),
                                          ALU.mult)
                    if cc == 0:
                        c.link(ins)
                ins.then_inc(a_s[b], 1)
                dve.wait_ge(a_s[b], i + 1)
                c.link(V.tensor_tensor(w0, w0, tile_of(xn_all, t), ALU.add))
                keep(tile_of(xn_all, t), w0)
                moments(c, w0, t)
                assert c.n == per, c.n
                make_hots(t + 1, 1 - b)

            dve.wait_ge(s_y, NT)
            dve.wait_ge(s_const, 3)
            dve.wait_ge(s_prow, 16)
            dve.wait_ge(s_hzero, 3)
            dve.wait_ge(s_ytab, 32)
            make_hots(0, 0)
            node_tiles(dve, pass2)
            base[0] += NT * per
            c = Chain(dve, s_tile, base[0])
            means(c)
            base[0] += c.n

            dve.wait_ge(s_reps, 4 * 16)
            base_x1 = base[0]

            def ffn_front(i, b, t, tail):
                dve.wait_ge(a_tp[b], i)
                normed(work[b][1], tile_of(xn_all, t), t).then_inc(a_x1[b], 1)

            def ffn_back(i, b, t, tail):
                sum_rows(t + (NT - 1))
                c = Chain(dve, s_tile, base_x1 + t * 2)
                w2 = work[b][2]
                dve.wait_ge(a_y[b], i + 1)
                c.link(V.tensor_tensor(w2, bank(2 + b)[:, 0:D], b2_r, ALU.add))
                keep(tile_of(xn_all, t), w2).then_inc(a_out[b], 1)
                moments(c, w2, t)
                make_hots(t + (NT + 1), b)

            staggered(dve, ffn_front, ffn_back)
            base[0] += NT * 2
            c = Chain(dve, s_tile, base[0])
            means(c)
            base[0] += c.n

            with dve.Fori(NT, (GROUPS - 1) // 2) as i:
                for q in range(2):
                    sum_rows(i * 2 + q - 1)
                    make_hots(i * 2 + q + 1, 1 - q)
            sum_rows(GROUPS - 2)
            sum_rows(GROUPS - 1)

            base_x2 = base[0]

            def combine_front(i, b, t, tail):
                normed(work[b][2], tile_of(xn_all, t), t).then_inc(c_n, 1)

            def combine_back(i, b, t, tail):
                c = Chain(dve, s_tile, base_x2 + t * 3)
                w0, w1, w2 = work[b]
                dve.wait_ge(c_fifth, t + 1)
                dve.wait_ge(c_x[b], i * 16 + 16)
                c.link(V.tensor_tensor(w0, w0, bank(4 + b)[:, 0:D], ALU.max))
                c.link(V.tensor_tensor(w0, w0, rows_g[b], ALU.add))
                dve.wait_ge(c_w, t + 1)
                dve.wait_ge(c_x2o[b], 16 * i)
                V.tensor_tensor(w1, w0, w2, ALU.add).then_inc(c_x2[b], 1)
                dve.wait_ge(c_x2[b], i + 1)
                keep(tile_of(h_all, t), w1)
                moments(c, w1, t)

            staggered(dve, combine_front, combine_back)
            base[0] += NT * 3
            c = Chain(dve, s_tile, base[0])
            means(c)
            base[0] += c.n
            base_xt = base[0]

            def route_in(i, b, t, tail):
                c = Chain(dve, s_tile, base_xt + t)
                w2 = work[b][2]
                dve.wait_ge(c_tp2[b], i)
                normed(w2, tile_of(h_all, t), t).then_inc(c_xt[b], 1)
                dve.wait_ge(c_xt[b], i + 1)
                keep(tile_of(h_all, t), w2)
                moments(c, w2, t)

            node_tiles(dve, route_in)
            base[0] += NT

            def te(a):
                return a.rearrange("p (t e) -> p t e", e=E)

            def over_e(a):
                return a[:, :].unsqueeze(2).broadcast_to([P, NT, E])

            def over_t(a):
                return a[:, :].unsqueeze(1).broadcast_to([P, NT, E])

            dve.wait_ge(s_small, 7 * 16)
            dve.wait_ge(c_lg, NT)
            V.tensor_tensor(te(logit[:, :]), te(bank(6)[:, 0:NE]),
                            br_r[:, :].unsqueeze(1).broadcast_to([P, NT, E]), ALU.add).then_inc(c_lc, 1)
            dve.wait_ge(c_lc, 1)
            ch.link(V.tensor_reduce(c_m[:, :], te(logit[:, :]), AX.X, ALU.max))
            V.tensor_tensor(te(logit[:, :]), te(logit[:, :]), over_e(c_m), ALU.subtract).then_inc(s_route, 1)
            c = Chain(dve, s_tile, base[0])
            means(c)
            base[0] += c.n
            V.scalar_tensor_tensor(out=nw_v[:, :], in0=mv[:, :, 0], scalar=-1.0, in1=rstd[:, :],
                                   op0=ALU.mult, op1=ALU.mult).then_inc(s_means, 1)
            dve.wait_ge(s_exp, 1)
            ch.link(V.tensor_reduce(c_s[:, :], te(prob[:, :]), AX.X, ALU.add))
            ch.link(V.reciprocal(c_s[:, :], c_s[:, :]))
            ch.link(V.tensor_tensor(te(prob[:, :]), te(prob[:, :]), over_e(c_s), ALU.mult))
            dve.wait_ge(s_const, 3)
            for p_k, hot in ((p_1, hot1), (p_2, hot2)):
                ch.link(V.tensor_reduce(p_k[:, :], te(prob[:, :]), AX.X, ALU.max))
                ch.link(V.tensor_tensor(te(rt_a[:, :]), te(prob[:, :]), over_e(p_k), ALU.is_equal))
                ch.link(V.tensor_tensor(rt_a[:, :], rt_a[:, :], rank_w[:, :], ALU.mult))
                ch.link(V.tensor_reduce(c_m[:, :], te(rt_a[:, :]), AX.X, ALU.max))
                ch.link(V.tensor_tensor(te(hot[:, :]), te(rt_a[:, :]), over_e(c_m), ALU.is_equal))
                if hot is hot1:
                    ch.link(V.scalar_tensor_tensor(out=prob[:, :], in0=hot[:, :], scalar=-2.0, in1=prob[:, :],
                                                   op0=ALU.mult, op1=ALU.add))
            ch.link(V.tensor_tensor(c_s[:, :], p_1[:, :], p_2[:, :], ALU.add))
            ch.link(V.reciprocal(c_s[:, :], c_s[:, :]))
            ch.link(V.tensor_tensor(wt_1[:, :], p_1[:, :], c_s[:, :], ALU.mult))
            ch.link(V.tensor_tensor(wt_2[:, :], p_2[:, :], c_s[:, :], ALU.mult))
            ch.link(V.tensor_tensor(rt_b[:, :], hot1[:, :], hot2[:, :], ALU.add))
            V.tensor_tensor(rt_b[:, :], rt_b[:, :], valid[:, :], ALU.mult).then_inc(s_cnt, 1)
            dve.wait_ge(s_rank, 1)
            ch.link(V.tensor_copy(rt_b[:, :], bank(1)[:, 0:NE]))
            for e in range(E):
                last = V.tensor_tensor_scan(te(rt_a[:, :])[:, :, e], ones_m[:, 0:NT], te(rt_b[:, :])[:, :, e],
                                            0.0, ALU.mult, ALU.add)
            ch.link(last)
            ch.link(V.tensor_copy(e_f[:, :], te(rt_a[:, :])[:, NT - 1, :]))
            ch.link(V.tensor_tensor(rt_a[:, :], rt_a[:, :], rt_b[:, :], ALU.subtract))
            ch.link(V.tensor_scalar(e_f[:, :], e_f[:, :], float(P - 1), None, ALU.add))
            ch.link(V.tensor_copy(e_i[:, :], e_f[:, :]))
            ch.link(V.tensor_single_scalar(e_i[:, :], e_i[:, :], 7, ALU.logical_shift_right))
            ch.link(V.tensor_copy(e_f[:, :], e_i[:, :]))
            ch.link(V.tensor_tensor_scan(e_cum[:, :], ones_m[:, 0:E], e_f[:, :], 0.0, ALU.mult, ALU.add))
            ch.link(V.tensor_tensor(e_base[:, :], e_cum[:, :], e_f[:, :], ALU.subtract))
            ch.link(V.tensor_scalar(e_base[:, :], e_base[:, :], float(P), None, ALU.mult))
            ch.link(V.tensor_tensor(rt_a[:, :], rt_a[:, :], bank(0)[:, 0:NE], ALU.add))
            ch.link(V.tensor_tensor(te(rt_a[:, :]), te(rt_a[:, :]), over_t(e_base), ALU.add))
            for hot, slot in ((hot1, slot_1), (hot2, slot_2)):
                ch.link(V.tensor_tensor(rt_b[:, :], hot[:, :], rt_a[:, :], ALU.mult))
                ch.link(V.tensor_reduce(slot_f[:, :], te(rt_b[:, :]), AX.X, ALU.add))
                V.tensor_copy(slot[:, :], slot_f[:, :]).then_inc(s_slot, 1)
                dve.wait_ge(s_slot, 1 if hot is hot1 else 2)
            ch.link(V.tensor_tensor(xt_cmp[:, :].rearrange("p (k e) -> p k e", e=E),
                                    xt_iota[:, :].rearrange("p (k e) -> p k e", e=E),
                                    e_cum[0:1, :].unsqueeze(1).broadcast_to([1, XT, E]), ALU.is_ge))
            ch.link(V.tensor_reduce(xt_f[:, :], xt_cmp[:, :].rearrange("p (k e) -> p k e", e=E), AX.X, ALU.add))
            V.memset(expert_of[:, XT:XT + 2], 0).then_inc(s_etab, 1)
            V.tensor_scalar(expert_of[:, 0:XT], xt_f[:, :], float(E - 1), None, ALU.min).then_inc(s_etab, 1)

            dve.wait_ge(s_etab, 2)
            dve.wait_ge(s_bias, 32)
            dve.wait_ge(s_scat, 2 * NT * 16)
            dve.wait_ge(s_w1, 16)
            er = [dve.alloc_register(f"dve_expert{n}") for n in range(4)]

            def copy_w1(e, b, i):
                dve.wait_ge(x_h[2 * b + 1], i)
                keep(w1_now[b], w1_all[:, ds(e * (KC * F), KC * F)]).then_inc(x_w1[b], 1)

            def evac_x(e, b, i):
                dve.wait_ge(x_tp[b], i + 1)
                for k in range(KC):
                    V.tensor_scalar(xeT[b][:, k * P:(k + 1) * P], bank(4)[:, k * P:(k + 1) * P],
                                    eg_col[:, ds(e * KC + k, 1)], eb_col[:, ds(e * KC + k, 1)],
                                    ALU.mult, ALU.add).then_inc(x_T[b], 1)

            def bias_y(e, b, i):
                dve.wait_ge(x_y[b], i + 1)
                dve.wait_ge(x_out[b], 16 * i)
                V.tensor_tensor(yt[b], bank(6 + b)[:, 0:D], b2_all[:, ds(e * D, D)], ALU.add).then_inc(x_yb[b], 1)

            def experts(regs, at):
                dve.reg_load(regs, expert_of[0:1, ds(at, len(regs))])
                return [dve.snap(r, min_val=0, max_val=E - 1) for r in regs]

            e0, e1 = experts(er[0:2], 0)
            for b, e in enumerate((e0, e1)):
                copy_w1(e, b, 0)
                evac_x(e, b, 0)

            def expert_tiles(i):
                es = experts(er, i * 2)
                for b in range(2):
                    copy_w1(es[2 + b], b, i + 1)
                    evac_x(es[2 + b], b, i + 1)
                    bias_y(es[b], b, i)

            repeat(dve, XT // 2 - 1, expert_tiles)
            es = experts(er[0:2], XT - 2)
            for b in range(2):
                bias_y(es[b], b, XT // 2 - 1)

            base_fin = base[0]

            for t in range(NT):
                n = TAIL if t == NT - 1 else P
                i, b = t // SETS, t % SETS
                dve.wait_ge(f_x[b], 16 * (i + 1))
                dve.wait_ge(f_1[b], F1_BASE + 16 * (i + 1))
                V.scalar_tensor_tensor(out=fin_x[b][0:n], in0=fin_1[b][0:n], scalar=wt_1[0:n, t:t + 1],
                                       in1=fin_x[b][0:n], op0=ALU.mult, op1=ALU.add).then_inc(s_tile, 1)
                dve.wait_ge(s_tile, base_fin + t + 1)
                dve.wait_ge(f_2[b], F2_BASE + 16 * (i + 1))
                V.scalar_tensor_tensor(out=fin_x[b][0:n], in0=fin_2[b][0:n], scalar=wt_2[0:n, t:t + 1],
                                       in1=fin_x[b][0:n], op0=ALU.mult, op1=ALU.add).then_inc(f_y, 1)

        @block.tensor
        def _(pe):
            T = nc.tensor
            for c in range(NCH):
                b = c % 2
                pe.wait_ge(oh_ready[b], 2 * (c // 2 + 1))
                lo = oh_lo[b][0:EP, 0:P * CH].rearrange("p (n c) -> p n c", c=CH)
                hi = oh_hi[b][0:EP, 0:NT * CH].rearrange("p (n c) -> p n c", c=CH)
                for j in range(CH):
                    last = T.matmul(bank(7)[:, 0:NT], lo[:, :, j], hi[:, :, j],
                                    start=(c == 0 and j == 0), stop=(c == NCH - 1 and j == CH - 1))
                last.then_inc(oh_used[b] if c < NCH - 1 else s_deg, 1)
            pe.wait_ge(s_const, 3)

            def turn2(dst, rows, signal):
                for k in range(KC):
                    last = T.transpose(dst[:, k * P:(k + 1) * P], rows(k), ident[:, :])
                last.then_inc(signal, 1)

            def wkv(k, o, n):
                return wqkv_sb[:, k * 3 * D + o:k * 3 * D + o + n]

            def pass1_turn(t):
                i, b = t // 2, t % 2
                pe.wait_ge(in_place[b], i + 1)
                if t:
                    pe.wait_ge(m_nT[1 - b], i + b)
                turn2(bank(1), lambda k: work[b][0][:, k * P:(k + 1) * P], m_tp[b])

            def pass1_front(t):
                i, b = t // 2, t % 2
                pe.wait_ge(m_nT[b], i + 1)
                if i:
                    pe.wait_ge(m_exp[b], i * 5)
                for k in range(KC):
                    T.matmul(bank(2 + b), nT[b][:, k * P:(k + 1) * P], wkv(k, D, 2 * D),
                             start=(k == 0), stop=(k == KC - 1))
                for o in range(KC):
                    for k in range(KC):
                        last = T.matmul(bank(4 + b)[:, o * P:(o + 1) * P], wkv(k, o * P, P),
                                        nT[b][:, k * P:(k + 1) * P], start=(k == 0), stop=(k == KC - 1))
                last.then_inc(m_qkv[b], 1)

            def pass1_back(t):
                i, b = t // 2, t % 2
                pe.wait_ge(m_phi[b], (i + 1) * 2)
                pe.wait_ge(m_exp[b], (i + 1) * 5)
                n = TAIL if t == NT - 1 else P
                for c in range(KC):
                    last = T.matmul(bank(6 + c)[:, 0:P + 1], rel_k[b][0:n, c * P:(c + 1) * P],
                                    v_ext[b][0:n, c * VW:c * VW + P + 1], start=False, stop=(t == NT - 1),
                                    skip_group_check=True)
                last.then_inc(m_kv[b], 1)

            fronts = [0]

            def pass1(n):
                for t in range(fronts[0], min(fronts[0] + n, NT)):
                    if t == 0:
                        pass1_turn(0)
                    if t + 1 < NT:
                        pass1_turn(t + 1)
                    pass1_front(t)
                    if t:
                        pass1_back(t - 1)
                    fronts[0] = t + 1

            pe.wait_ge(s_wts, 4 * 16)
            pe.wait_ge(s_dinv, 1)
            pe.wait_ge(s_zero, 1)
            pe.wait_ge(s_vone, 2)
            for c in range(KC):
                T.matmul(bank(6 + c)[:, 0:P + 1], zero_w[:, 0:P], zero_w[:, 0:P + 1], start=True, stop=False,
                         skip_group_check=True)
            for k, (to_cols, live, count) in enumerate(turns):
                pe.wait_ge(s_sort, count)
                for c in range(4):
                    if to_cols:
                        blk = rows_s[live][:, c * P:(c + 1) * P]
                    else:
                        blk = cols_s[live].rearrange("q (p c) -> q c p", c=4)[:, c, :]
                    last = T.transpose(bank(0)[:, c * P:(c + 1) * P], blk, ident[:, :])
                last.then_inc(s_turned, 1)
                if k:
                    pass1(1 if to_cols else 2)
            pe.wait_ge(s_path, 1)
            T.matmul(bank(0)[:, 0:ET - 1], last_m[:, :], end_f[:, 0:ET - 1], start=True,
                     stop=True).then_inc(s_last, 1)
            pass1(NT)
            pass1_back(NT - 1)

            pe.wait_ge(s_reps, 4 * 16)

            def edge_steps(turn, half):
                g = turn * 2 + half
                for u in range(R):
                    pe.wait_ge(gathered[half * R + u], 16 * (turn + 1))
                    pe.wait_ge(hot_ready, g * R + u + 1)
                    if u % 2 == 0 and i_is_late(g):
                        pe.wait_ge(added, g * R + (u + 2 - R))
                    T.matmul(step_sum(u), hot_of[half][u], rows_of[half][u], start=True,
                             stop=True).then_inc(summed, 1)

            pe.wait_ge(s_bd, 1 + 8 * KC)

            def pass2(i, b, t, tail):
                pe.wait_ge(in_place[b], i + 1 + (HALF + 1 - b))
                pe.wait_ge(a_s[b], i)
                for c in range(KC):
                    last = T.matmul(bank(b)[:, c * VW:(c + 1) * VW], exp_q[b][:, c * P:(c + 1) * P],
                                    kvbd[:, c, :], start=True, stop=True)
                last.then_inc(a_num[b], 1)
                edge_steps(i, b)

            node_tiles(pe, pass2)

            def ffn_front(i, b, t, tail):
                pe.wait_ge(a_x1[b], i + 1)
                pe.wait_ge(a_x1T[1 - b], 2 * i + 2 * b)
                turn2(bank(0), lambda k: work[b][1][:, k * P:(k + 1) * P], a_tp[b])
                pe.wait_ge(a_x1T[b], 2 * (i + 1))
                pe.wait_ge(a_hT[1 - b], 2 * i + 2 * b)
                for o in range(KC):
                    for k in range(KC):
                        last = T.matmul(bank(1)[:, o * P:(o + 1) * P], w1_sb[:, k * D + o * P:k * D + (o + 1) * P],
                                        nT[b][:, k * P:(k + 1) * P], start=(k == 0), stop=(k == KC - 1))
                last.then_inc(a_h[b], 1)

            def ffn_back(i, b, t, tail):
                pe.wait_ge(a_hT[b], 2 * (i + 1))
                pe.wait_ge(a_out[b], i)
                for k in range(KC):
                    last = T.matmul(bank(2 + b)[:, 0:D], exp_k[b][:, k * P:(k + 1) * P],
                                    w2_sb[:, k * D:(k + 1) * D], start=(k == 0), stop=(k == KC - 1))
                    if k == 0:
                        for o in range(KC):
                            T.matmul(bank(2 + b)[:, o * P:(o + 1) * P], nT[b][:, o * P:(o + 1) * P],
                                     ident[:, :], start=False, stop=False)
                last.then_inc(a_y[b], 1)
                edge_steps(i + (HALF + b), 1 - b)

            staggered(pe, ffn_front, ffn_back)

            with pe.Fori(NT, (GROUPS - 1) // 2) as i:
                edge_steps(i, 0)
                edge_steps(i, 1)
            edge_steps(GROUPS // 2, 0)

            def combine_front(i, b, t, tail):
                pe.wait_ge(c_sc[b], 2 * (i + 1))
                pe.wait_ge(c_T[b], i)
                for k in range(KC):
                    for h in (exp_k[b], exp_q[b]):
                        last = T.matmul(bank(b)[:, k * P:(k + 1) * P], h[:, k * P:(k + 1) * P], ident[:, :],
                                        start=(h is exp_k[b]), stop=(h is exp_q[b]))
                last.then_inc(c_tp[b], 1)

            def combine_back(i, b, t, tail):
                pe.wait_ge(c_T[b], i + 1)
                pe.wait_ge(c_x2[b], i)
                T.matmul(bank(4 + b)[:, 0:D], ones_m[0:1, :], gb_r[0:1, :], start=True, stop=False)
                for k in range(KC):
                    last = T.matmul(bank(4 + b)[:, 0:D], nT[b][:, k * P:(k + 1) * P],
                                    gw_sb[:, k * D:(k + 1) * D], start=False, stop=(k == KC - 1))
                last.then_inc(c_mm[b], 1)

            def route_front(i, b, t, tail):
                pe.wait_ge(c_xt[b], i + 1)
                pe.wait_ge(c_T2[b], i)
                turn2(bank(2 + b), lambda k: work[b][2][:, k * P:(k + 1) * P], c_tp2[b])

            def route_back(i, b, t, tail):
                pe.wait_ge(c_T2[b], i + 1)
                for k in range(KC):
                    last = T.matmul(bank(6)[:, ds(t * E, E)], exp_q[b][:, k * P:(k + 1) * P], wr_sb[:, k, :],
                                    start=(k == 0), stop=(k == KC - 1))
                last.then_inc(c_lg, 1)

            pe.wait_ge(added, STEPS)
            staggered(pe, combine_front, combine_back)
            pe.wait_ge(s_small, 7 * 16)
            staggered(pe, route_front, route_back)
            pe.wait_ge(s_cnt, 1)
            T.matmul(bank(0)[:, 0:NE], below[:, :], rt_b[:, :], start=True, stop=True)
            T.matmul(bank(1)[:, 0:NE], ones_m[:, :], rt_b[:, :], start=True, stop=True).then_inc(s_rank, 1)

            pe.wait_ge(s_slot, 2)
            pe.wait_ge(s_etab, 2)
            er = [pe.alloc_register(f"pe_expert{n}") for n in range(2)]

            def turn_x(b, i, seen):
                pe.wait_ge(x_in[b], 16 * (i + 1))
                pe.wait_ge(x_T[1 - b], 2 * seen)
                turn2(bank(4), lambda k: xd[b][:, k * P:(k + 1) * P], x_tp[b])

            def first(b, i):
                pe.wait_ge(x_T[b], 2 * (i + 1))
                pe.wait_ge(x_w1[b], i + 1)
                for s in range(2):
                    pe.wait_ge(x_g[2 * b + s], 4 * i)
                    for f in range(4):
                        for k in range(KC):
                            at = k * F + (4 * s + f) * P
                            last = T.matmul(bank(2 * b + s)[:, f * P:(f + 1) * P], w1_now[b][:, at:at + P],
                                            xeT[b][:, k * P:(k + 1) * P], start=(k == 0), stop=(k == KC - 1))
                    last.then_inc(x_h[2 * b + s], 1)

            def second(e, b, i):
                pe.wait_ge(x_yb[b], i)
                for k in range(FC):
                    if k % 4 == 0:
                        pe.wait_ge(x_g[2 * b + k // 4], 4 * (i + 1))
                    last = T.matmul(bank(6 + b)[:, 0:D], hidT[b][:, k * P:(k + 1) * P],
                                    w2_all[:, ds(e * (FC * D) + k * D, D)], start=(k == 0), stop=(k == FC - 1))
                last.then_inc(x_y[b], 1)

            def experts(regs, at):
                pe.reg_load(regs, expert_of[0:1, ds(at, len(regs))])
                return [pe.snap(r, min_val=0, max_val=E - 1) for r in regs]

            turn_x(0, 0, 0)
            turn_x(1, 0, 1)
            first(0, 0)
            pe.wait_ge(s_w2, 16)

            def expert_tiles(i):
                ea, eb = experts(er, i * 2)
                first(1, i)
                turn_x(0, i + 1, i + 1)
                second(ea, 0, i)
                first(0, i + 1)
                turn_x(1, i + 1, i + 2)
                second(eb, 1, i)

            repeat(pe, XT // 2 - 1, expert_tiles)
            n = XT // 2 - 1
            ea, eb = experts(er, XT - 2)
            first(1, n)
            second(ea, 0, n)
            second(eb, 1, n)

        @block.scalar
        def _(act):
            A = nc.scalar
            act.wait_ge(s_means, 1)
            for t in range(NT):
                xt = xn_all[:, t * D:(t + 1) * D]
                last = A.activation(xt, xt, ACT.Identity, bias=shift[:, t:t + 1], scale=rstd[:, t:t + 1])
            last.then_inc(s_ln, 1)
            act.wait_ge(s_ln, 1)

            def pass1_front(i, b, t, tail):
                act.wait_ge(m_tp[b], i)
                A.activation(work[b][0], xn_all[:, ds(t * D, D)], ACT.Copy).then_inc(in_place[b], 1)
                A.activation(y_all[:, ds(t * D, D)], xn_all[:, ds(t * D, D)], ACT.Copy,
                             scale=dinv[:, ds(t, 1)]).then_inc(s_y, 1)
                act.wait_ge(m_tp[b], i + 1)
                act.wait_ge(m_qkv[b], i)
                A.activation(nT[b], bank(1)[:, 0:D], ACT.Copy).then_inc(m_nT[b], 1)

            def pass1_back(i, b, t, tail):
                act.wait_ge(m_qkv[b], i + 1)
                act.wait_ge(m_phi[b], 2 * i)
                act.wait_ge(m_kv[b], i)
                A.activation(exp_k[b], bank(2 + b)[:, 0:D], ACT.Exp).then_inc(m_exp[b], 1)
                A.activation(rel_k[b], bank(2 + b)[:, 0:D], ACT.Relu).then_inc(m_exp[b], 1)
                A.activation(exp_q[b], bank(4 + b)[:, 0:D], ACT.Exp).then_inc(m_exp[b], 1)
                A.activation(rel_q[b], bank(4 + b)[:, 0:D], ACT.Relu).then_inc(m_exp[b], 1)
                A.activation(v_ext[b].rearrange("p (c v) -> p c v", c=KC)[:, :, 0:P],
                             bank(2 + b)[:, D:2 * D].rearrange("p (c v) -> p c v", c=KC),
                             ACT.Copy).then_inc(m_exp[b], 1)

            act.wait_ge(s_vone, 2)
            act.wait_ge(s_dinv, 1)
            staggered(act, pass1_front, pass1_back)

            act.wait_ge(s_prow, 16)
            tiles = [act.alloc_register(f"act_tile{u}") for u in range(R)]

            def indices(turn, half):
                g = turn * 2 + half
                act.reg_load(tiles, path[0:1, ds(g * R, R)])
                for u in range(R):
                    t = act.snap(tiles[u], min_val=0, max_val=ET - 1)
                    if i_is_late(turn):
                        act.wait_ge(gathered[half * R + u], 16 * turn)
                    A.activation(idx_g[:, half * R + u:half * R + u + 1], dst_i[:, ds(t, 1)],
                                 ACT.Copy).then_inc(idx_ready, 1)

            indices(0, 0)

            def pass2(i, b, t, tail):
                act.wait_ge(a_num[b], i)
                act.wait_ge(m_phi[b], 2 * (HALF + (1 - b)))
                A.activation(exp_q[b], qT_all[:, ds(t * D, D)], ACT.Copy).then_inc(in_place[b], 1)
                indices(i + b, 1 - b)

            node_tiles(act, pass2)

            def ffn(i, b, t, tail):
                act.wait_ge(a_tp[b], i + 1)
                act.wait_ge(a_y[b], i)
                for k in range(KC):
                    A.activation(nT[b][:, k * P:(k + 1) * P], bank(0)[:, k * P:(k + 1) * P], ACT.Identity,
                                 bias=o1_col[:, k:k + 1], scale=g1_col[:, k:k + 1]).then_inc(a_x1T[b], 1)
                act.wait_ge(a_h[b], i + 1)
                for o in range(KC):
                    A.activation(exp_k[b][:, o * P:(o + 1) * P], bank(1)[:, o * P:(o + 1) * P], ACT.Gelu,
                                 bias=b1_col[:, o:o + 1]).then_inc(a_hT[b], 1)
                indices(i + (HALF + 1), b)

            act.wait_ge(s_small, 7 * 16)
            node_tiles(act, ffn)
            for g in range(2 * NT + 1, GROUPS):
                indices(g // 2, g % 2)

            act.wait_ge(added, STEPS)

            def combine_front(i, b, t, tail):
                act.wait_ge(c_tp[b], i)
                for h, to in ((h_all, exp_k[b]), (h_odd, exp_q[b])):
                    A.activation(to, h[:, ds(t * D, D)], ACT.Copy, scale=dinv[:, ds(t, 1)]).then_inc(c_sc[b], 1)

            def fifth(b, count):
                act.wait_ge(c_mm[b], count)
                A.activation(work[b][0], bank(4 + b)[:, 0:D], ACT.Copy, scale=0.2).then_inc(c_fifth, 1)

            def combine_back(i, b, t, tail):
                act.wait_ge(c_tp[b], i + 1)
                A.activation(nT[b], bank(b)[:, 0:D], ACT.Copy).then_inc(c_T[b], 1)
                if i_is_late(t):
                    fifth(1 - b, i + b)

            def route_in(i, b, t, tail):
                act.wait_ge(c_tp2[b], i + 1)
                if i_is_late(i):
                    act.wait_ge(c_lg, t - 1)
                A.activation(exp_q[b], bank(2 + b)[:, 0:D], ACT.Copy).then_inc(c_T2[b], 1)

            staggered(act, combine_front, combine_back)
            fifth(0, HALF + 1)
            node_tiles(act, route_in)
            act.wait_ge(s_route, 1)
            A.activation(prob[:, :], logit[:, :], ACT.Exp).then_inc(s_exp, 1)
            act.wait_ge(s_means, 2)
            for t in range(NT):
                h = h_all[:, t * D:(t + 1) * D]
                A.activation(h, h, ACT.Identity, bias=nw_v[:, t:t + 1], scale=rstd[:, t:t + 1]).then_inc(s_xn, 1)

            act.wait_ge(s_etab, 2)
            act.wait_ge(s_bias, 32)
            er = [act.alloc_register(f"act_expert{n}") for n in range(2)]

            def gelu(e, b, i):
                act.wait_ge(x_y[b], i)
                for s in range(2):
                    act.wait_ge(x_h[2 * b + s], i + 1)
                    for f in range(4):
                        c = 4 * s + f
                        A.activation(hidT[b][:, c * P:(c + 1) * P], bank(2 * b + s)[:, f * P:(f + 1) * P],
                                     ACT.Gelu, bias=b1_all[:, ds(e * FC + c, 1)]).then_inc(x_g[2 * b + s], 1)

            def expert_tiles(i):
                act.reg_load(er, expert_of[0:1, ds(i * 2, 2)])
                for b in range(2):
                    gelu(act.snap(er[b], min_val=0, max_val=E - 1), b, i)

            repeat(act, XT // 2, expert_tiles)

        @block.gpsimd
        def _(pool):
            G = nc.gpsimd
            ch = Chain(pool, s_pool)
            G.memset(xn_all[:, (NT - 1) * D:NT * D], 0.0).then_inc(s_hzero, 1)
            G.memset(zero_w, 0.0).then_inc(s_zero, 1)
            G.iota(iota_lo[:, 0:P * CH], pattern=[[1, P], [0, CH]], base=0, channel_multiplier=0,
                   allow_small_or_imprecise_dtypes=True).then_inc(s_const, 1)
            G.iota(iota_hi[:, 0:NT * CH], pattern=[[1, NT], [0, CH]], base=0, channel_multiplier=0,
                   allow_small_or_imprecise_dtypes=True).then_inc(s_const, 1)
            ch.link(G.memset(ident[:, :], 0.0))
            ch.link(G.affine_select(out=ident[:, :], in_=ident[:, :], compare_op=ALU.not_equal, fill=1.0,
                                    base=0, pattern=[[-1, P]], channel_multiplier=1))
            ch.link(G.memset(last_m[:, :], 0.0))
            ch.link(G.affine_select(out=last_m[:, :], in_=last_m[:, :], compare_op=ALU.not_equal, fill=1.0,
                                    base=-(P - 1), pattern=[[0, P]], channel_multiplier=1))
            ch.link(G.memset(below[:, :], 1.0))
            ch.link(G.affine_select(out=below[:, :], in_=below[:, :], compare_op=ALU.is_gt, fill=0.0,
                                    base=0, pattern=[[1, P]], channel_multiplier=-1))
            G.memset(ones_m[:, :], 1.0)
            G.iota(step_f[:, :], pattern=[[P, PC]], base=0, channel_multiplier=1,
                   allow_small_or_imprecise_dtypes=True)
            G.iota(block_at[:, :], pattern=[[P, NT]], base=0, channel_multiplier=0,
                   allow_small_or_imprecise_dtypes=True)
            G.iota(rank_w[:, :], pattern=[[0, NT], [-1, E]], base=E, channel_multiplier=0,
                   allow_small_or_imprecise_dtypes=True)
            G.iota(xt_iota[:, :], pattern=[[1, XT], [0, E]], base=0, channel_multiplier=0,
                   allow_small_or_imprecise_dtypes=True)
            ch.link(G.memset(valid[:, :], 1.0))
            ch.link(G.affine_select(out=valid[:, :], in_=valid[:, :], compare_op=ALU.is_ge, fill=0.0,
                                    base=N - 1, pattern=[[-P, NT], [0, E]], channel_multiplier=-1))
            ch.link(G.iota(iota, pattern=[[1, SC]], base=0, channel_multiplier=0,
                           allow_small_or_imprecise_dtypes=True))
            G.memset(const_end[:, :], 0.0).then_inc(s_const, 1)

            G.memset(h_all, 0.0).then_inc(s_hzero, 1)
            pool.wait_ge(s_deg, 1)
            for b in range(2):
                G.memset(v_ext[b], 1.0).then_inc(s_vone, 1)

            for t in range(NT):
                i, b = t // 2, t % 2
                pool.wait_ge(m_exp[b], i * 5 + 1)
                G.tensor_scalar(exp_k[b], exp_k[b], 1.0, None, ALU.min).then_inc(s_pool, 1)
                pool.wait_ge(m_exp[b], i * 5 + 3)
                G.tensor_scalar(exp_q[b], exp_q[b], 1.0, None, ALU.min).then_inc(s_pool, 1)
                pool.wait_ge(s_pool, ch.n + 1)
                G.tensor_tensor(rel_k[b], exp_k[b], rel_k[b], ALU.add).then_inc(m_phi[b], 1)
                pool.wait_ge(m_exp[b], i * 5 + 4)
                pool.wait_ge(s_pool, ch.n + 2)
                G.tensor_tensor(qT_all[:, t * D:(t + 1) * D], exp_q[b], rel_q[b], ALU.add).then_inc(m_phi[b], 1)
                ch.n += 2

            pool.wait_ge(s_ytab, 32)
            pool.wait_ge(s_path, 1)
            G.memset(h_odd, 0.0).then_inc(s_hzero, 1)
            pool.wait_ge(s_moe0, 16)
            pool.wait_ge(m_kv[0], 1)
            zero_reg = pool.alloc_register("gather_zero")
            bound = pool.alloc_register("gather_bound")
            pool.reg_mov(zero_reg, 0)

            def gathers(turn, half):
                g = turn * 2 + half
                for u in range(R):
                    pool.wait_ge(idx_ready, g * R + u + 1)
                    if i_is_late(turn):
                        pool.wait_ge(summed, g * R + (u + 1 - 2 * R))
                    pool.reg_add(bound, zero_reg, NP_ - 1)
                    at = half * R + u
                    G.indirect_dma_start(out=rows_of[half][u], out_offset=None, in_=y_table,
                                         in_offset=bass.IndirectOffsetOnAxis(ap=idx_g[:, at:at + 1], axis=0),
                                         bounds_check=bound, oob_is_err=True).then_inc(gathered[at], 16)

            def two_groups(i):
                gathers(i, 0)
                gathers(i, 1)

            repeat(pool, GROUPS // 2, two_groups)
            gathers(GROUPS // 2, 0)

            def combine(i, b, t, tail):
                w2 = work[b][2]
                pool.wait_ge(c_n, t + 1)
                G.tensor_tensor(w2, w2, ln2g_r, ALU.mult).then_inc(s_pool, 1)
                pool.wait_ge(s_pool, t + (ch.n + 1))
                G.tensor_tensor(w2, w2, ln2b_r, ALU.add).then_inc(c_w, 1)

            node_tiles(pool, combine)

            pool.wait_ge(s_slot, 2)
            pool.wait_ge(s_xn, NT)
            for t in range(NT):
                n = TAIL if t == NT - 1 else P
                for slot in (slot_1, slot_2):
                    G.indirect_dma_start(out=moe_in, out_offset=bass.IndirectOffsetOnAxis(ap=slot[0:n, t:t + 1], axis=0),
                                         in_=h_all[0:n, t * D:(t + 1) * D], in_offset=None,
                                         bounds_check=SLOTS - 1, oob_is_err=True).then_inc(s_scat, 16)

            pool.wait_ge(x_out[0], 16 * (XT // 2))
            pool.wait_ge(x_out[1], 16 * (XT // 2))
            pool.wait_ge(x_y[0], XT // 2)
            pool.wait_ge(x_y[1], XT // 2)
            for t in range(NT):
                n = TAIL if t == NT - 1 else P
                b = t % SETS
                if t >= SETS:
                    pool.wait_ge(f_y, t + 1 - SETS)
                for rows, slot, done in ((fin_1, slot_1, f_1), (fin_2, slot_2, f_2)):
                    G.indirect_dma_start(out=rows[b][0:n], out_offset=None, in_=moe_out,
                                         in_offset=bass.IndirectOffsetOnAxis(ap=slot[0:n, t:t + 1], axis=0),
                                         bounds_check=SLOTS - 1, oob_is_err=True).then_inc(done[b], 16)

        @block.sync
        def _(sp):
            sp.dma_start(src_i[0:EP, :], src.rearrange("(p c) -> p c", c=EC)).then_inc(s_edges, 16)
            sp.dma_start(dst_e[0:EP, :], dst.rearrange("(p c) -> p c", c=EC)).then_inc(s_edges, 16)
            full = (NT - 1) * P
            sp.dma_start(xn_all[:, 0:(NT - 1) * D].rearrange("p (t d) -> p t d", d=D),
                         x[0:full, :].rearrange("(t p) d -> p t d", p=P)).then_inc(s_x, 16)
            sp.wait_ge(s_hzero, 1)
            sp.dma_start(xn_all[0:TAIL, (NT - 1) * D:NT * D], x[full:N, :]).then_inc(s_x, 16)
            for w_sb, w_d, n in ((wqkv_sb, wqkv_t, 3 * D), (w1_sb, w1_t, D), (w2_sb, w2_t, D), (gw_sb, gnn_w, D)):
                sp.dma_start(w_sb.rearrange("p (k n) -> p k n", n=n),
                             w_d.rearrange("(k p) n -> p k n", p=P)).then_inc(s_wts, 16)
            for r, v in zip((ln2g_r, ln2b_r, b2_r, gb_r), (ln2_g, ln2_b, b2, gnn_b)):
                sp.dma_start(r, rep(v, D)).then_inc(s_reps, 16)
            with nc.allow_non_contiguous_dma(reason="a few columns"):
                sp.dma_start(g1_col[:, :], ln1_g.rearrange("(k p) -> p k", p=P)).then_inc(s_small, 16)
                sp.dma_start(o1_col[:, :], ln1_b.rearrange("(k p) -> p k", p=P)).then_inc(s_small, 16)
                sp.dma_start(b1_col[:, :], b1.rearrange("(k p) -> p k", p=P)).then_inc(s_small, 16)
                sp.dma_start(eg_col[:, :], ffn_g.rearrange("e (k p) -> p (e k)", p=P)).then_inc(s_small, 16)
                sp.dma_start(eb_col[:, :], ffn_b.rearrange("e (k p) -> p (e k)", p=P)).then_inc(s_small, 16)
            sp.dma_start(wr_sb[:, :, :], wr.rearrange("(k p) e -> p k e", p=P)).then_inc(s_small, 16)
            sp.dma_start(br_r[:, :], rep(br, E)).then_inc(s_small, 16)
            sp.wait_ge(s_zero, 1)
            sp.dma_start(moe_in.rearrange("(p s) d -> p s d", p=P),
                         zero_w.unsqueeze(1).broadcast_to([P, XT, D])).then_inc(s_moe0, 16)
            for t0, t1 in ((0, 2 * NT // 3), (2 * NT // 3, NT)):
                sp.wait_ge(s_y, t1)
                sp.dma_start(y_table[t0 * P:t1 * P, :].rearrange("(t p) d -> p t d", p=P),
                             y_all[:, t0 * D:t1 * D].rearrange("p (t d) -> p t d", d=D)).then_inc(s_ytab, 16)
            sp.wait_ge(s_tiles, 1)
            with nc.allow_non_contiguous_dma(reason="a column of tile numbers"):
                sp.dma_start(path_dram.rearrange("a (c p) -> p (a c)", p=P), tile_i[:, :]).then_inc(s_pdram, 16)
            sp.wait_ge(s_pdram, 16)
            sp.dma_start(path[:, :], path_dram).then_inc(s_prow, 16)

            def load_x(i, b, t, tail):
                n = TAIL if tail else P
                sp.wait_ge(c_x2[b], i)
                sp.dma_start(rows_g[b][0:n], x[ds(t * P, n), :]).then_inc(c_x[b], 16)

            def store_x2(i, b, t, tail):
                sp.wait_ge(c_x2[b], i + 1)
                sp.dma_start(x2_rows[ds(t * P, P), :], work[b][1]).then_inc(c_x2o[b], 16)

            sp.wait_ge(added, STEPS)
            staggered(sp, load_x, store_x2, peel=True)

            sp.wait_ge(c_n, NT)
            sp.dma_start(w2_all.rearrange("p (e k d) -> p e k d", e=E, k=FC),
                         ffn_w2.rearrange("e (k p) d -> p e k d", p=P)).then_inc(s_w2, 16)
            sp.wait_ge(c_lg, NT)
            sp.dma_start(w1_all.rearrange("p (e k f) -> p e k f", e=E, k=KC),
                         ffn_w1.rearrange("e (k p) f -> p e k f", p=P)).then_inc(s_w1, 16)
            sp.wait_ge(c_x2o[0], 16 * (HALF + 1))
            sp.wait_ge(c_x2o[1], 16 * HALF)
            sp.dma_start(b2_all, ffn_b2.rearrange("(a e) d -> a (e d)", a=1).broadcast_to([P, E * D])).then_inc(s_bias, 16)
            with nc.allow_non_contiguous_dma(reason="a few columns"):
                sp.dma_start(b1_all, ffn_b1.rearrange("e (k p) -> p (e k)", p=P)).then_inc(s_bias, 16)
            sp.wait_ge(s_scat, 2 * NT * 16)

            def load_xd(b, i):
                sp.wait_ge(x_tp[b], i)
                sp.dma_start(xd[b], moe_in[ds((i * 2 + b) * P, P), :]).then_inc(x_in[b], 16)

            def store_y(b, i):
                sp.wait_ge(x_yb[b], i + 1)
                sp.dma_start(moe_out[ds((i * 2 + b) * P, P), :], yt[b]).then_inc(x_out[b], 16)

            load_xd(0, 0)
            load_xd(1, 0)
            load_xd(0, 1)

            def expert_tiles(i):
                load_xd(1, i + 1)
                store_y(0, i)
                load_xd(0, i + 2)
                store_y(1, i)

            repeat(sp, XT // 2 - 2, expert_tiles)
            n = XT // 2 - 1
            load_xd(1, n)
            store_y(0, n - 1)
            store_y(1, n - 1)
            store_y(0, n)
            store_y(1, n)

            sp.wait_ge(x_y[0], XT // 2)
            sp.wait_ge(x_y[1], XT // 2)

            def load_f(t):
                n = TAIL if t == NT - 1 else P
                b, i = t % SETS, t // SETS
                if i:
                    sp.wait_ge(f_out[b], 16 * i)
                sp.dma_start(fin_x[b][0:n], x2_rows[t * P:t * P + n, :]).then_inc(f_x[b], 16)

            AHEAD = SETS - 2
            for t in range(AHEAD):
                load_f(t)
            for t in range(NT):
                n = TAIL if t == NT - 1 else P
                b = t % SETS
                if t + AHEAD < NT:
                    load_f(t + AHEAD)
                sp.wait_ge(f_y, t + 1)
                sp.dma_start(out[t * P:t * P + n, :], fin_x[b][0:n]).then_inc(f_out[b], 16)
            for b in range(SETS):
                sp.wait_ge(f_out[b], 16 * (NT // SETS))


_INS = ["x", "src", "dst", "L0_gnn_W", "L0_gnn_b", "L0_mix_Wqkv", "L0_mix_ln1_g", "L0_mix_ln1_b", "L0_mix_W1",
        "L0_mix_b1", "L0_mix_W2", "L0_mix_b2", "L0_mix_ln2_g", "L0_mix_ln2_b", "L0_ffn_Wr", "L0_ffn_br",
        "L0_ffn_ln_g", "L0_ffn_ln_b", "L0_ffn_W1", "L0_ffn_b1", "L0_ffn_W2", "L0_ffn_b2"]
_TRANSPOSED = {"L0_mix_Wqkv", "L0_mix_W1", "L0_mix_W2"}


def kernel(**inputs):
    import numpy as _np
    import concourse.bacc as _bacc
    from concourse import mybir as _mybir
    from concourse.bass_utils import run_bass_kernel_spmd as _run

    nc = _bacc.Bacc("TRN2", target_bir_lowering=False, num_devices=1)
    arrays, args = {}, []
    for name in _INS:
        a = _np.asarray(inputs[name])
        a = _np.ascontiguousarray(a.T if name in _TRANSPOSED else a)
        arrays[f"in_{name}"] = a
        args.append(nc.dram_tensor(f"in_{name}", a.shape, _mybir.dt.from_np(a.dtype), kind="ExternalInput").ap())
    out = nc.dram_tensor("out_x", inputs["x"].shape, _mybir.dt.float32, kind="ExternalOutput").ap()
    gps_layer(nc, *args, out)
    r = _run(nc, [arrays], core_ids=[0])
    return r.results[0]["out_x"]
```

```python
from contextlib import ExitStack

import concourse.bass as bass
from concourse import mybir

ALU = mybir.AluOpType
ACT = mybir.ActivationFunctionType
AX = mybir.AxisListType
F32 = mybir.dt.float32
BF16 = mybir.dt.bfloat16
I32 = mybir.dt.int32
ds = bass.ds

P = 128


class Chain:

    def __init__(self, engine, sem, base=0):
        self.engine, self.sem, self.base, self.n = engine, sem, base, 0

    def link(self, ins):
        ins.then_inc(self.sem, 1)
        self.n += 1
        self.engine.wait_ge(self.sem, self.base + self.n)

    def count(self, ins):
        ins.then_inc(self.sem, 1)
        self.n += 1


def gps_layer(nc, x, src, dst, gnn_w, gnn_b, wqkv_t, ln1_g, ln1_b, w1_t, b1, w2_t, b2, ln2_g, ln2_b,
              wr, br, ffn_g, ffn_b, ffn_w1, ffn_b1, ffn_w2, ffn_b2, out):
    N, D = x.shape
    EDGES = src.shape[0]
    H = 8
    HD = D // H
    E, _, F = ffn_w1.shape
    EPS = 1e-5
    EPS_ATTN = 1e-6
    KC = D // P
    FC = F // P
    NT = -(-N // P)
    TAIL = N - (NT - 1) * P
    NP_ = NT * P
    HALF = NT // 2
    assert NT % 2 == 1 and KC == 2 and TAIL <= 64

    EP = 125
    EC = EDGES // EP
    CH = 85
    NCH = EC // CH
    assert EP * EC == EDGES and CH * NCH == EC
    DBITS = 12
    SC = 512
    PAD_KEY = float(NP_ << DBITS)
    ET = -(-EDGES // P)
    STEPS = ET + NT - 1
    R = 8
    GROUPS = STEPS // R
    FF = NT + 2
    assert STEPS % R == 0 and GROUPS == FF + NT + 3 and GROUPS % 2 == 1 and (NP_ << DBITS) < 1 << 24 and NP_ <= 1 << DBITS
    PC = -(-STEPS // P)

    XT = -(-(2 * N) // P) + E - 1
    XT += XT % 2

    with ExitStack() as ctx:
        def sb(name, shape, dt=F32):
            return ctx.enter_context(nc.sbuf_tensor(name, shape, dt))

        def sem(name):
            return ctx.enter_context(nc.semaphore(name))

        def sems(name, n=2):
            return [sem(f"{name}{i}") for i in range(n)]

        y_table = nc.dram_tensor("y_table", [NP_, D], F32, kind="Internal").ap()
        x2_rows = nc.dram_tensor("x2_rows", [NP_ + P, D], F32, kind="Internal").ap()
        x3_rows = nc.dram_tensor("x3_rows", [NP_ + P, D + E], F32, kind="Internal").ap()
        path_dram = nc.dram_tensor("path_dram", [1, PC * P], I32, kind="Internal").ap()

        arena_a = sb("arena_a", [P, E * KC * F])
        arena_b = sb("arena_b", [P, E * FC * D + E * F])
        arena_w = sb("arena_w", [P, 7680])

        def carve(arena, at, n, dt=F32):
            v = arena[:, at:at + n]
            return v if dt == F32 else v.bitcast(dt)

        LO, HI = P // 2, 2 * NT
        LO_F, HI_F = CH * LO // 2, CH * HI // 2
        oh_lo = [carve(arena_a, b * LO_F, LO_F, BF16) for b in range(2)]
        oh_hi = [carve(arena_a, 2 * LO_F + b * HI_F, HI_F, BF16) for b in range(2)]
        qT_all = carve(arena_a, 0, KC * NP_)
        at = KC * NP_
        key_i = carve(arena_a, at, ET, I32); at += ET
        dst_i = carve(arena_a, at, ET, I32); at += ET
        tmp_i = carve(arena_a, at, ET, I32); at += ET
        src_f = carve(arena_a, at, ET); at += ET
        end_f = carve(arena_a, at, ET); at += ET
        cmp_f = carve(arena_a, at, ET); at += ET
        nT = [carve(arena_a, at + b * D, D) for b in range(2)]; at += 2 * D
        exp_k = [carve(arena_a, at + b * D, D) for b in range(2)]; at += 2 * D
        exp_q = [carve(arena_a, at + b * D, D) for b in range(2)]; at += 2 * D
        rel_k = [carve(arena_a, at + b * D, D) for b in range(2)]; at += 2 * D
        rel_q = [carve(arena_a, at + b * D, D) for b in range(2)]; at += 2 * D
        VW = P + 4
        v_ext = [carve(arena_a, at + b * KC * VW, KC * VW) for b in range(2)]; at += 2 * KC * VW
        assert at <= 13056
        at = 13056
        wqkv_sb = carve(arena_a, at, KC * 3 * D); at += KC * 3 * D
        w1_sb = carve(arena_a, at, KC * D); at += KC * D
        w2_sb = carve(arena_a, at, KC * D); at += KC * D
        gw_sb = carve(arena_a, at, KC * D); at += KC * D
        assert at <= E * KC * F
        xn_all = carve(arena_b, 0, NT * D); at = NT * D
        assert ET <= SC
        iota = carve(arena_b, at, SC); at += SC
        h_odd = carve(arena_b, at, NT * D)
        rows_s = [carve(arena_b, at + b * SC, SC) for b in range(2)]; at += 2 * SC
        cols_s = [carve(arena_b, at + b * SC, SC) for b in range(2)]; at += 2 * SC
        y_all = carve(arena_b, at, NT * D)
        H_AT = E * FC * D + E * F - NT * D
        odd = H_AT - R * D - R * P
        rows_odd = [carve(arena_b, odd + u * D, D) for u in range(R)]
        hot_odd = [carve(arena_b, odd + R * D + u * P, P) for u in range(R)]
        assert NT * D + SC + NT * D <= odd
        iota_lo = carve(arena_b, at, LO_F, BF16)
        iota_hi = carve(arena_b, at + LO_F, HI_F, BF16)
        h_all = carve(arena_b, H_AT, NT * D)
        assert at + max(LO_F + HI_F, NT * D) <= H_AT and E * FC * D + E * FC <= H_AT
        at = 0
        reps = []
        for _ in range(4):
            reps.append(carve(arena_w, at, D)); at += D
        ln2g_r, ln2b_r, b2_r, gb_r = reps
        rows_g = [carve(arena_w, at + u * D, D) for u in range(R)]; at += R * D
        hot_g = [carve(arena_w, at + u * P, P) for u in range(R)]; at += R * P
        work = [[carve(arena_w, at + (3 * b + k) * D, D) for k in range(3)] for b in range(2)]; at += 6 * D
        zero_w = rows_g[0]
        rows_of, hot_of = (rows_g, rows_odd), (hot_g, hot_odd)
        e0, EB = 4 * D + D, -(-EC // 2)
        src_i = carve(arena_w, e0, EC, I32)
        dst_e = carve(arena_w, e0 + EC, EC, I32)
        part_i = carve(arena_w, e0 + 2 * EC, EC, I32)
        lo_b = carve(arena_w, e0 + 3 * EC, EB, BF16)[:, 0:EC]
        hi_b = carve(arena_w, e0 + 3 * EC + EB, EB, BF16)[:, 0:EC]
        assert 3 * EC + 2 * EB <= (R - 1) * D
        assert at <= 7680
        w1_all = carve(arena_a, 0, E * KC * F)
        w2_all = carve(arena_b, 0, E * FC * D)
        b1_all = carve(arena_b, E * FC * D, E * FC)
        w1_now = [carve(arena_b, H_AT + b * KC * F, KC * F) for b in range(2)]
        at = 0
        b2_all = carve(arena_w, at, E * D); at += E * D
        XW = D + E
        xd = [carve(arena_w, at + b * XW, XW) for b in range(2)]; at += 2 * XW
        xeT = [carve(arena_w, at + b * D, D) for b in range(2)]; at += 2 * D
        hidT = [carve(arena_w, at + b * F, F) for b in range(2)]; at += 2 * F
        yt = [carve(arena_w, at + b * D, D) for b in range(2)]; at += 2 * D
        LO_W, HI_W = NT * P // 2, NT * XT
        slot_lo = [carve(arena_w, E * D + k * LO_W, LO_W, BF16) for k in range(2)]
        hi_at = E * D + 2 * LO_W
        slot_hi = [carve(arena_b, E * FC * D + E * FC, HI_W, BF16), carve(arena_w, hi_at, HI_W, BF16)]
        slot_iota = carve(arena_b, E * FC * D + E * FC + HI_W, P)
        XT_AT = 7680 - 2 * XT * E
        assert at <= XT_AT and hi_at + HI_W <= XT_AT and E * FC * D + E * FC + HI_W + P <= H_AT
        ident = sb("ident", [P, P])
        below = sb("below", [P, P])
        ones_m = sb("ones_m", [P, P])
        last_m = sb("last_m", [P, P])
        step_f = sb("step_f", [P, PC])
        tile_no = sb("tile_no", [P, NT])
        block_at = sb("block_at", [P, NT])
        tile_f = sb("tile_f", [P, PC])
        tile_i = sb("tile_i", [P, PC], I32)
        path = sb("path", [1, PC * P], I32)
        idx_g = sb("idx_g", [P, 2 * R], I32)
        stats = sb("stats", [P, NT, 6])
        mv = sb("mv", [P, NT, 2])
        rstd = sb("rstd", [P, NT])
        nw_v = sb("nw_v", [P, NT])
        nw_i = sb("nw_i", [P, NT], I32)
        nw_a = sb("nw_a", [P, NT])
        deg = sb("deg", [P, NT])
        has = sb("has", [P, NT])
        dinv = sb("dinv", [P, NT])
        y_scale, y_shift = deg, has
        stats_flat = stats[:, :, :].rearrange("p t six -> p (t six)")
        mv_flat = mv[:, :, :].rearrange("p t two -> p (t two)")
        kvbd = sb("kvbd", [P, KC, VW])
        zden = sb("zden", [P, 2, H])
        g1_col = sb("g1_col", [P, KC])
        o1_col = sb("o1_col", [P, KC])
        b1_col = sb("b1_col", [P, KC])
        wr_sb = sb("wr_sb", [P, KC, E])
        br_r = sb("br_r", [P, E])
        eg_col = sb("eg_col", [P, E * KC])
        eb_col = sb("eb_col", [P, E * KC])
        NE = NT * E
        logit = sb("logit", [P, NE])
        prob = sb("prob", [P, NE])
        hot1 = sb("hot1", [P, NE])
        hot2 = sb("hot2", [P, NE])
        rt_a = sb("rt_a", [P, NE])
        rt_b = sb("rt_b", [P, NE])
        rank_w = sb("rank_w", [P, NE])
        valid = sb("valid", [P, NE])
        c_m = sb("c_m", [P, NT])
        slot_f = sb("slot_f", [P, NT])
        shift = slot_f
        c_s = sb("c_s", [P, NT])
        p_1 = sb("p_1", [P, NT])
        p_2 = sb("p_2", [P, NT])
        wt_1 = sb("wt_1", [P, NT])
        wt_2 = sb("wt_2", [P, NT])
        slot_i = sb("slot_i", [P, NT], I32)
        part_f = sb("part_f", [P, NT])
        token_of = sb("token_of", [P, XT], I32)
        lane = sb("lane", [P, 1])
        spare = sb("spare", [P, 1])
        w_now = sb("w_now", [P, 2])
        w_next = sb("w_next", [P, 2])
        e_f = sb("e_f", [P, E])
        e_cum = sb("e_cum", [P, E])
        e_base = sb("e_base", [P, E])
        e_i = sb("e_i", [P, E], I32)
        xt_iota = carve(arena_w, XT_AT, XT * E)[0:1]
        xt_cmp = carve(arena_w, XT_AT + XT * E, XT * E)[0:1]
        xt_f = sb("xt_f", [1, XT])
        expert_of = sb("expert_of", [1, XT + 2], I32)
        const_end = sb("const_end", [1, 2])

        ps = ctx.enter_context(nc.psum_tensor("ps", [P, 8, 512], F32))

        s_edges = sem("s_edges"); s_x = sem("s_x"); s_wts = sem("s_wts"); s_reps = sem("s_reps")
        s_const = sem("s_const"); s_pool = sem("s_pool"); s_hzero = sem("s_hzero")
        s_dve0 = sem("s_dve0")
        oh_ready = sems("oh_ready"); oh_used = sems("oh_used"); s_deg = sem("s_deg")
        s_ln = sem("s_ln"); s_dinv = sem("s_dinv"); s_y = sem("s_y"); s_ytab = sem("s_ytab")
        s_sort = sem("s_sort"); s_turned = sem("s_turned")
        s_path = sem("s_path"); s_last = sem("s_last"); s_tiles = sem("s_tiles"); s_pdram = sem("s_pdram")
        s_prow = sem("s_prow")
        m_tp = sems("m_tp"); m_nT = sems("m_nT"); m_qkv = sems("m_qkv"); m_exp = sems("m_exp")
        m_phi = sems("m_phi"); m_kv = sems("m_kv"); s_vone = sem("s_vone"); s_bd = sem("s_bd")
        a_num = sems("a_num"); a_x1 = sems("a_x1"); a_tp = sems("a_tp"); a_x1T = sems("a_x1T")
        a_h = sems("a_h"); a_hT = sems("a_hT"); a_y = sems("a_y"); a_out = sems("a_out")
        s_tile = sem("s_tile"); s_xn = sem("s_xn"); s_means = sem("s_means"); a_s = sems("a_s")
        idx_ready = sem("idx_ready"); gathered = sems("gathered", 2 * R)
        hot_ready = sem("hot_ready"); summed = sem("summed"); added = sem("added")
        c_sc = sems("c_sc"); c_tp = sems("c_tp"); c_T = sems("c_T"); c_mm = sems("c_mm")
        c_x = sems("c_x"); c_n = sem("c_n"); c_fifth = sem("c_fifth"); c_w = sem("c_w"); c_x2 = sems("c_x2"); c_x2o = sems("c_x2o")
        c_xt = sems("c_xt"); c_tp2 = sems("c_tp2"); c_T2 = sems("c_T2"); c_lg = sem("c_lg")
        c_lc = sem("c_lc")
        s_zero = sem("s_zero"); s_small = sem("s_small"); s_spare = sem("s_spare"); s_bias = sem("s_bias")
        in_place = sems("in_place")
        s_route = sem("s_route"); s_exp = sem("s_exp")
        s_cnt = sem("s_cnt"); s_rank = sem("s_rank"); s_hots = sem("s_hots"); s_inv = sem("s_inv"); s_token = sem("s_token"); s_gates = sem("s_gates"); s_etab = sem("s_etab")
        s_table = sem("s_table"); s_w1 = sem("s_w1"); s_w2 = sem("s_w2")
        x_in = sems("x_in"); x_tp = sems("x_tp"); x_T = sems("x_T"); x_h = sems("x_h", 4)
        x_g = sems("x_g", 4); x_w1 = sems("x_w1"); x_y = sems("x_y"); x_yb = sems("x_yb"); x_out = sems("x_out")
        s_out = sem("s_out")

        def rep(v, n):
            return v.rearrange("(a n) -> a n", a=1).broadcast_to([P, n])

        def bank(k):
            return ps[:, k, :]

        TILES_BEHIND = (1, 2, 0, 2, 1, 2, 1, 2, 1, 2, 1, 1, 2, 2, 3, 2, 0)
        PH_ROWS = 8
        turns = []

        def node_tiles(engine, body):
            body(0, 0, 0, False)
            body(0, 1, 1, False)
            with engine.Fori(1, HALF) as i:
                body(i, 0, i * 2, False)
                body(i, 1, i * 2 + 1, False)
            body(HALF, 0, NT - 1, True)

        def staggered(engine, front, back, peel=False):
            def turn(i, tail=False):
                front(i, 1, i * 2 + 1, False)
                back(i, 0, i * 2, False)
                front(i + 1, 0, i * 2 + 2, tail)
                back(i, 1, i * 2 + 1, False)

            front(0, 0, 0, False)
            turn(0)
            with engine.Fori(1, HALF - 1 if peel else HALF) as i:
                turn(i)
            if peel:
                turn(HALF - 1, True)
            back(HALF, 0, NT - 1, True)

        def repeat(engine, n, body):
            body(0)
            with engine.Fori(1, n) as i:
                body(i)

        def step_sum(u):
            return ps[:, 4 + u // 2, (u % 2) * D:(u % 2 + 1) * D]

        def past_first(t):
            return not (isinstance(t, int) and t == 0)

        block = ctx.enter_context(nc.Block())

        @block.vector
        def _(dve):
            V = nc.vector
            ch = Chain(dve, s_dve0)

            def inv_sqrt(c, dst, var, eps):
                c.link(V.tensor_scalar(nw_v[:, :], var, eps, None, ALU.add))
                c.link(V.tensor_single_scalar(nw_i[:, :], nw_v[:, :].bitcast(I32), 1, ALU.logical_shift_right))
                c.link(V.tensor_scalar(dst[:, :].bitcast(I32), nw_i[:, :], -1.0, float(0x5F3759DF), ALU.mult, ALU.add))
                for _ in range(3):
                    c.link(V.tensor_tensor(nw_a[:, :], dst[:, :], dst[:, :], ALU.mult))
                    c.link(V.tensor_tensor(nw_a[:, :], nw_a[:, :], nw_v[:, :], ALU.mult))
                    c.link(V.tensor_scalar(nw_a[:, :], nw_a[:, :], -0.5, 1.5, ALU.mult, ALU.add))
                    c.link(V.tensor_tensor(dst[:, :], dst[:, :], nw_a[:, :], ALU.mult))

            V.memset(rows_s[0], PAD_KEY).then_inc(s_sort, 1)
            V.memset(kvbd[:, :, :], 0.0).then_inc(s_bd, 1)
            dve.wait_ge(s_edges, 32)
            dve.wait_ge(s_sort, 1)
            V.scalar_tensor_tensor(out=rows_s[0][0:EP, 0:EC], in0=src_i[0:EP, :], scalar=float(1 << DBITS),
                                   in1=dst_e[0:EP, :], op0=ALU.mult, op1=ALU.add).then_inc(s_sort, 1)
            n_sort = [2]
            cur = [0, 0]

            def settle():
                dve.wait_ge(s_sort, n_sort[0])

            def exchange(which, dist):
                a = (rows_s, cols_s)[which]
                s = a[cur[which]].rearrange("p (a two d) -> p a two d", two=2, d=dist)
                o = a[1 - cur[which]].rearrange("p (a two d) -> p a two d", two=2, d=dist)
                V.tensor_tensor(o[:, :, 0, :], s[:, :, 0, :], s[:, :, 1, :], ALU.min).then_inc(s_sort, 1)
                V.tensor_tensor(o[:, :, 1, :], s[:, :, 0, :], s[:, :, 1, :], ALU.max).then_inc(s_sort, 1)
                n_sort[0] += 2
                settle()
                cur[which] = 1 - cur[which]

            def negate(view):
                V.tensor_scalar(view, view, -1.0, None, ALU.mult).then_inc(s_sort, 1)
                n_sort[0] += 1
                settle()

            def turn(to_cols):
                turns.append((to_cols, cur[0 if to_cols else 1], n_sort[0]))
                k = len(turns)
                dve.wait_ge(s_turned, k)
                b = bank(0)
                if to_cols:
                    cur[1] = 0
                    V.tensor_copy(cols_s[0].rearrange("q (p c) -> q c p", c=4),
                                  b.rearrange("q (c p) -> q c p", c=4)).then_inc(s_sort, 1)
                else:
                    cur[0] = 0
                    V.tensor_copy(rows_s[0], b).then_inc(s_sort, 1)
                n_sort[0] += 1
                settle()

            def half_view(a, h):
                return a.rearrange("p (a two h) -> p a two h", two=2, h=h)[:, :, 1, :]

            def mid_view(a, h):
                return a.rearrange("p (a q h) -> p a q h", q=4, h=h)[:, :, 1:3, :]

            settle()
            negate(half_view(rows_s[0], 2))
            for k in range(1, PH_ROWS + 1):
                for j in range(k - 1, -1, -1):
                    exchange(0, 1 << j)
                if k < PH_ROWS:
                    negate(mid_view(rows_s[cur[0]], 1 << k))
            negate(rows_s[cur[0]][:, SC // 2:SC])

            ch.link(V.tensor_single_scalar(part_i[0:EP, :], src_i[0:EP, :], LO - 1, ALU.bitwise_and))
            ch.link(V.tensor_copy(lo_b[0:EP, :], part_i[0:EP, :]))
            ch.link(V.tensor_single_scalar(part_i[0:EP, :], src_i[0:EP, :], 6, ALU.logical_shift_right))
            ch.link(V.tensor_copy(hi_b[0:EP, :], part_i[0:EP, :]))
            dve.wait_ge(s_const, 2)
            for c in range(NCH):
                b = c % 2
                if c >= 2:
                    dve.wait_ge(oh_used[b], c // 2)
                lo = lo_b[0:EP, c * CH:(c + 1) * CH].unsqueeze(1).broadcast_to([EP, LO, CH])
                hi = hi_b[0:EP, c * CH:(c + 1) * CH].unsqueeze(1).broadcast_to([EP, HI, CH])
                V.tensor_tensor(oh_lo[b][0:EP, 0:LO * CH].rearrange("p (n c) -> p n c", c=CH), lo,
                                iota_lo[0:EP, 0:LO * CH].rearrange("p (n c) -> p n c", c=CH),
                                ALU.is_equal).then_inc(oh_ready[b], 1)
                V.tensor_tensor(oh_hi[b][0:EP, 0:HI * CH].rearrange("p (n c) -> p n c", c=CH), hi,
                                iota_hi[0:EP, 0:HI * CH].rearrange("p (n c) -> p n c", c=CH),
                                ALU.is_equal).then_inc(oh_ready[b], 1)
            dve.wait_ge(s_x, 32)
            dve.wait_ge(s_hzero, 1)
            for t in range(NT):
                last = V.bn_stats(stats[:, t, :], xn_all[:, t * D:(t + 1) * D])
            ch.link(last)
            for t in range(NT):
                last = V.bn_aggr(mv[:, t, :], stats[:, t, :])
            ch.link(last)
            inv_sqrt(ch, rstd, mv[:, :, 1], EPS)
            V.scalar_tensor_tensor(out=shift[:, :], in0=mv[:, :, 0], scalar=-1.0, in1=rstd[:, :],
                                   op0=ALU.mult, op1=ALU.mult).then_inc(s_means, 1)
            dve.wait_ge(s_deg, 1)
            halves = bank(7)[0:LO, 0:HI].rearrange("p (t two) -> p t two", two=2)
            for h in range(2):
                last = V.tensor_copy(deg[h * LO:(h + 1) * LO, :], halves[:, :, h])
            ch.link(last)
            ch.link(V.tensor_scalar(has[:, :], deg[:, :], 0.0, None, ALU.is_gt))
            ch.link(V.tensor_scalar(deg[:, :], deg[:, :], 1.0, None, ALU.max))
            inv_sqrt(ch, deg, deg[:, :], 0.0)
            ch.link(V.tensor_tensor(dinv[:, :], deg[:, :], has[:, :], ALU.mult))
            V.tensor_tensor(y_scale[:, :], rstd[:, :], dinv[:, :], ALU.mult).then_inc(s_dinv, 1)
            V.tensor_tensor(y_shift[:, :], shift[:, :], dinv[:, :], ALU.mult).then_inc(s_dinv, 1)

            turn(True)
            negate(half_view(cols_s[0], 4))
            for k in range(PH_ROWS + 1, 17):
                for j in range(k - 8, -1, -1):
                    exchange(1, 1 << j)
                turn(False)
                for j in range(6, -1, -1):
                    exchange(0, 1 << j)
                turn(True)
                if k < 15:
                    negate(mid_view(cols_s[0], 1 << (k - 7)))
                elif k == 15:
                    negate(cols_s[0][:, SC // 2:SC])

            ch.link(V.tensor_copy(key_i, cols_s[0][:, 0:ET]))
            ch.link(V.tensor_single_scalar(dst_i, key_i, (1 << DBITS) - 1, ALU.bitwise_and))
            ch.link(V.tensor_single_scalar(tmp_i, key_i, DBITS, ALU.logical_shift_right))
            ch.link(V.tensor_copy(src_f, tmp_i))
            ch.link(V.tensor_single_scalar(tmp_i, key_i, DBITS + 7, ALU.logical_shift_right))
            ch.link(V.tensor_copy(cmp_f, tmp_i))
            dve.wait_ge(s_const, 3)
            V.tensor_tensor(end_f[:, 0:ET - 1], cmp_f[:, 0:ET - 1], iota[:, 0:ET - 1],
                            ALU.add).then_inc(s_path, 1)
            dve.wait_ge(s_last, 1)
            for c in range(PC):
                ch.link(V.tensor_scalar(cmp_f[:, 0:ET - 1], bank(0)[:, 0:ET - 1], step_f[:, c:c + 1], None,
                                        ALU.is_lt))
                ch.link(V.tensor_reduce(tile_f[:, c:c + 1], cmp_f[:, 0:ET - 1], AX.X, ALU.add))
            V.tensor_copy(tile_i[:, :], tile_f[:, :]).then_inc(s_tiles, 1)

            dve.wait_ge(m_kv[0], HALF + 1)
            dve.wait_ge(m_kv[1], HALF)
            dve.wait_ge(s_bd, 1)
            for c in range(KC):
                for h in range(4):
                    r = slice(h * HD, (h + 1) * HD)
                    V.tensor_copy(kvbd[r, c, r], bank(6 + c)[r, r]).then_inc(s_bd, 1)
                    V.tensor_copy(kvbd[r, c, P + h:P + h + 1], bank(6 + c)[r, P:P + 1]).then_inc(s_bd, 1)

            tiles = [dve.alloc_register(f"dve_tile{u}") for u in range(R)]

            def group_at(g):
                dve.reg_load(tiles, path[0:1, ds(g * R, R)])
                at_tile = [dve.snap(r, min_val=0, max_val=ET - 1) for r in tiles]
                at_block = [nc.s_assert_within(
                    dve.snap(g * R + u - at_tile[u]), 0, NT - 1,
                    skip_runtime_bounds_check_because="a step moves either the tile or the block on")
                            for u in range(R)]
                return at_tile, at_block

            def make_hots(g, half):
                at_tile, at_block = group_at(g)
                for u in range(R):
                    V.tensor_scalar(hot_of[half][u], iota[:, 0:P], block_at[:, ds(at_block[u], 1)],
                                    src_f[:, ds(at_tile[u], 1)], ALU.add, ALU.is_equal).then_inc(hot_ready, 1)

            def sum_rows(g):
                at_block = group_at(g)[1]
                for u in range(R):
                    if u == 0:
                        dve.wait_ge(summed, g * R + R)
                    if u > 1 or past_first(g):
                        dve.wait_ge(added, g * R + (u - 1))
                    block_h = (h_all, h_odd)[u % 2][:, ds(at_block[u] * D, D)]
                    V.tensor_tensor(block_h, block_h, step_sum(u), ALU.add).then_inc(added, 1)

            def moments(c, rows, t):
                c.count(V.bn_stats(stats_flat[:, ds(t * 6, 6)], rows))

            def keep(out_, in_):
                return V.tensor_scalar(out_, in_, 1.0, None, ALU.mult)

            def means(c):
                dve.wait_ge(s_tile, c.base)
                for t in range(NT):
                    last = V.bn_aggr(mv[:, t, :], stats[:, t, :])
                c.link(last)
                inv_sqrt(c, rstd, mv[:, :, 1], EPS)

            def normed(out_, in_, t):
                return V.tensor_scalar(out_, in_, mv_flat[:, ds(t * 2, 1)], rstd[:, ds(t, 1)],
                                       ALU.subtract, ALU.mult)

            def tile_of(a, t):
                return a[:, ds(t * D, D)]

            per = 5
            base = [0]

            def pass2(i, b, t, tail):
                if past_first(t):
                    sum_rows(t - 1)
                c = Chain(dve, s_tile, t * per + base[0])
                w0 = work[b][0]
                dve.wait_ge(a_num[b], i + 1)
                num = bank(b)[:, 0:KC * VW].rearrange("p (c v) -> p c v", c=KC)
                z = zden[:, b, :].rearrange("p (c h) -> p c h", c=KC)
                c.link(V.tensor_scalar(z, num[:, :, P:VW], EPS_ATTN, None, ALU.add))
                c.link(V.reciprocal(zden[:, b, :], zden[:, b, :]))
                for cc in range(KC):
                    ins = V.tensor_tensor(w0[:, cc * P:(cc + 1) * P].rearrange("p (h d) -> p h d", d=HD),
                                          num[:, cc, 0:P].rearrange("p (h d) -> p h d", d=HD),
                                          zden[:, b, cc * 4:cc * 4 + 4].unsqueeze(2).broadcast_to([P, 4, HD]),
                                          ALU.mult)
                    if cc == 0:
                        c.link(ins)
                ins.then_inc(a_s[b], 1)
                dve.wait_ge(a_s[b], i + 1)
                c.link(V.tensor_tensor(w0, w0, tile_of(xn_all, t), ALU.add))
                keep(tile_of(xn_all, t), w0)
                moments(c, w0, t)
                assert c.n == per, c.n
                make_hots(t + 1, 1 - b)

            dve.wait_ge(s_ln, NT)
            dve.wait_ge(s_const, 3)
            dve.wait_ge(s_prow, 16)
            dve.wait_ge(s_hzero, 3)
            dve.wait_ge(s_ytab, 32)
            make_hots(0, 0)
            node_tiles(dve, pass2)
            sum_rows(FF - 3)
            make_hots(FF - 1, 0)
            base[0] += NT * per
            c = Chain(dve, s_tile, base[0])
            means(c)
            base[0] += c.n

            dve.wait_ge(s_reps, 4 * 16)
            base_x1 = base[0]

            def ffn_front(i, b, t, tail):
                dve.wait_ge(a_tp[b], i)
                normed(work[b][1], tile_of(xn_all, t), t).then_inc(a_x1[b], 1)
                if not past_first(t):
                    sum_rows(FF - 2)
                    make_hots(FF, 1)

            def ffn_back(i, b, t, tail):
                sum_rows(t + (FF - 1))
                c = Chain(dve, s_tile, base_x1 + t * 2)
                w2 = work[b][2]
                dve.wait_ge(a_y[b], i + 1)
                c.link(V.tensor_tensor(w2, bank(2 + b)[:, 0:D], b2_r, ALU.add))
                keep(tile_of(xn_all, t), w2).then_inc(a_out[b], 1)
                moments(c, w2, t)
                make_hots(t + (FF + 1), b)

            staggered(dve, ffn_front, ffn_back)
            base[0] += NT * 2
            for g in range(FF + NT, GROUPS):
                sum_rows(g - 1)
                if g + 1 < GROUPS:
                    make_hots(g + 1, (g + 1) % 2)
                if g == FF + NT:
                    c = Chain(dve, s_tile, base[0])
                    means(c)
                    base[0] += c.n
            sum_rows(GROUPS - 1)

            base_x2 = base[0]

            def combine_front(i, b, t, tail):
                normed(work[b][2], tile_of(xn_all, t), t).then_inc(c_n, 1)

            def combine_back(i, b, t, tail):
                c = Chain(dve, s_tile, base_x2 + t * 2)
                w0, w1, w2 = work[b]
                dve.wait_ge(c_fifth, t + 1)
                c.link(V.tensor_tensor(w0, w0, bank(4 + b)[:, 0:D], ALU.max))
                dve.wait_ge(c_w, t + 1)
                dve.wait_ge(c_x2o[b], 16 * i)
                V.tensor_tensor(w1, w0, w2, ALU.add).then_inc(c_x2[b], 1)
                dve.wait_ge(c_x2[b], i + 1)
                keep(tile_of(h_all, t), w1)
                moments(c, w1, t)

            staggered(dve, combine_front, combine_back)
            base[0] += NT * 2
            c = Chain(dve, s_tile, base[0])
            means(c)
            base[0] += c.n
            base_xt = base[0]

            def route_in(i, b, t, tail):
                c = Chain(dve, s_tile, base_xt + t)
                w2 = work[b][2]
                dve.wait_ge(c_tp2[b], i)
                normed(w2, tile_of(h_all, t), t).then_inc(c_xt[b], 1)
                dve.wait_ge(c_xt[b], i + 1)
                keep(tile_of(h_all, t), w2)
                moments(c, w2, t)

            node_tiles(dve, route_in)
            base[0] += NT

            def te(a):
                return a.rearrange("p (t e) -> p t e", e=E)

            def over_e(a):
                return a[:, :].unsqueeze(2).broadcast_to([P, NT, E])

            def over_t(a):
                return a[:, :].unsqueeze(1).broadcast_to([P, NT, E])

            dve.wait_ge(s_small, 7 * 16)
            dve.wait_ge(c_lg, NT)
            V.tensor_tensor(te(logit[:, :]), te(bank(6)[:, 0:NE]),
                            br_r[:, :].unsqueeze(1).broadcast_to([P, NT, E]), ALU.add).then_inc(c_lc, 1)
            dve.wait_ge(c_lc, 1)
            ch.link(V.tensor_reduce(c_m[:, :], te(logit[:, :]), AX.X, ALU.max))
            V.tensor_tensor(te(logit[:, :]), te(logit[:, :]), over_e(c_m), ALU.subtract).then_inc(s_route, 1)
            c = Chain(dve, s_tile, base[0])
            means(c)
            base[0] += c.n
            V.scalar_tensor_tensor(out=nw_v[:, :], in0=mv[:, :, 0], scalar=-1.0, in1=rstd[:, :],
                                   op0=ALU.mult, op1=ALU.mult).then_inc(s_means, 1)
            dve.wait_ge(s_exp, 1)
            ch.link(V.tensor_reduce(c_s[:, :], te(prob[:, :]), AX.X, ALU.add))
            ch.link(V.reciprocal(c_s[:, :], c_s[:, :]))
            ch.link(V.tensor_tensor(te(prob[:, :]), te(prob[:, :]), over_e(c_s), ALU.mult))
            dve.wait_ge(s_const, 3)
            for p_k, hot in ((p_1, hot1), (p_2, hot2)):
                ch.link(V.tensor_reduce(p_k[:, :], te(prob[:, :]), AX.X, ALU.max))
                ch.link(V.tensor_tensor(te(rt_a[:, :]), te(prob[:, :]), over_e(p_k), ALU.is_equal))
                ch.link(V.tensor_tensor(rt_a[:, :], rt_a[:, :], rank_w[:, :], ALU.mult))
                ch.link(V.tensor_reduce(c_m[:, :], te(rt_a[:, :]), AX.X, ALU.max))
                ch.link(V.tensor_tensor(te(hot[:, :]), te(rt_a[:, :]), over_e(c_m), ALU.is_equal))
                if hot is hot1:
                    ch.link(V.scalar_tensor_tensor(out=prob[:, :], in0=hot[:, :], scalar=-2.0, in1=prob[:, :],
                                                   op0=ALU.mult, op1=ALU.add))
            ch.link(V.tensor_tensor(c_s[:, :], p_1[:, :], p_2[:, :], ALU.add))
            ch.link(V.reciprocal(c_s[:, :], c_s[:, :]))
            ch.link(V.tensor_tensor(wt_1[:, :], p_1[:, :], c_s[:, :], ALU.mult))
            ch.link(V.tensor_tensor(wt_2[:, :], p_2[:, :], c_s[:, :], ALU.mult))
            ch.link(V.tensor_tensor(rt_b[:, :], hot1[:, :], hot2[:, :], ALU.add))
            V.tensor_tensor(rt_b[:, :], rt_b[:, :], valid[:, :], ALU.mult).then_inc(s_cnt, 1)
            dve.wait_ge(s_rank, 1)
            ch.link(V.tensor_copy(rt_b[:, :], bank(1)[:, 0:NE]))
            for e in range(E):
                last = V.tensor_tensor_scan(te(rt_a[:, :])[:, :, e], ones_m[:, 0:NT], te(rt_b[:, :])[:, :, e],
                                            0.0, ALU.mult, ALU.add)
            ch.link(last)
            ch.link(V.tensor_copy(e_f[:, :], te(rt_a[:, :])[:, NT - 1, :]))
            ch.link(V.tensor_tensor(rt_a[:, :], rt_a[:, :], rt_b[:, :], ALU.subtract))
            ch.link(V.tensor_scalar(e_f[:, :], e_f[:, :], float(P - 1), None, ALU.add))
            ch.link(V.tensor_copy(e_i[:, :], e_f[:, :]))
            ch.link(V.tensor_single_scalar(e_i[:, :], e_i[:, :], 7, ALU.logical_shift_right))
            ch.link(V.tensor_copy(e_f[:, :], e_i[:, :]))
            ch.link(V.tensor_tensor_scan(e_cum[:, :], ones_m[:, 0:E], e_f[:, :], 0.0, ALU.mult, ALU.add))
            ch.link(V.tensor_tensor(e_base[:, :], e_cum[:, :], e_f[:, :], ALU.subtract))
            ch.link(V.tensor_scalar(e_base[:, :], e_base[:, :], float(P), None, ALU.mult))
            ch.link(V.tensor_tensor(rt_a[:, :], rt_a[:, :], bank(0)[:, 0:NE], ALU.add))
            ch.link(V.tensor_tensor(te(rt_a[:, :]), te(rt_a[:, :]), over_t(e_base), ALU.add))
            dve.wait_ge(s_const, 4)
            dve.wait_ge(c_x2o[0], 16 * (HALF + 1))
            dve.wait_ge(c_x2o[1], 16 * HALF)
            for k, hot in enumerate((hot1, hot2)):
                ch.link(V.tensor_tensor(rt_b[:, :], hot[:, :], rt_a[:, :], ALU.mult))
                ch.link(V.tensor_reduce(slot_f[:, :], te(rt_b[:, :]), AX.X, ALU.add))
                ch.link(V.tensor_copy(slot_i[:, :], slot_f[:, :]))
                ch.link(V.tensor_single_scalar(nw_i[:, :], slot_i[:, :], P - 1, ALU.bitwise_and))
                ch.link(V.tensor_copy(part_f[:, :], nw_i[:, :]))
                V.tensor_tensor(slot_lo[k].rearrange("p (t n) -> p t n", n=P),
                                part_f[:, :].unsqueeze(2).broadcast_to([P, NT, P]),
                                slot_iota.unsqueeze(1).broadcast_to([P, NT, P]),
                                ALU.is_equal).then_inc(s_hots, 1)
                ch.link(V.tensor_single_scalar(nw_i[:, :], slot_i[:, :], 7, ALU.logical_shift_right))
                ch.link(V.tensor_copy(slot_f[:, :], nw_i[:, :]))
                hi = slot_hi[k].rearrange("p (t two x) -> p t two x", two=2, x=XT)
                ch.link(V.tensor_tensor(hi[:, :, 1, :], slot_f[:, :].unsqueeze(2).broadcast_to([P, NT, XT]),
                                        slot_iota[:, 0:XT].unsqueeze(1).broadcast_to([P, NT, XT]), ALU.is_equal))
                V.tensor_tensor(hi[:, :, 0, :], hi[:, :, 1, :],
                                tile_no[:, :].unsqueeze(2).broadcast_to([P, NT, XT]), ALU.mult).then_inc(s_hots, 1)
                dve.wait_ge(s_hots, 3 * k + 2)
                V.tensor_scalar(hi[:, :, 1, :], hi[:, :, 1, :], lane[:, 0:1], None, ALU.mult).then_inc(s_hots, 1)
            ch.link(V.tensor_tensor(te(prob[:, :]), te(hot1[:, :]), over_e(wt_1), ALU.mult))
            ch.link(V.tensor_tensor(te(hot2[:, :]), te(hot2[:, :]), over_e(wt_2), ALU.mult))
            V.tensor_tensor(prob[:, :], prob[:, :], hot2[:, :], ALU.add).then_inc(s_gates, 1)
            ch.link(V.tensor_tensor(xt_cmp[:, :].rearrange("p (k e) -> p k e", e=E),
                                    xt_iota[:, :].rearrange("p (k e) -> p k e", e=E),
                                    e_cum[0:1, :].unsqueeze(1).broadcast_to([1, XT, E]), ALU.is_ge))
            ch.link(V.tensor_reduce(xt_f[:, :], xt_cmp[:, :].rearrange("p (k e) -> p k e", e=E), AX.X, ALU.add))
            V.memset(expert_of[:, XT:XT + 2], 0).then_inc(s_etab, 1)
            V.tensor_scalar(expert_of[:, 0:XT], xt_f[:, :], float(E - 1), None, ALU.min).then_inc(s_etab, 1)
            dve.wait_ge(s_inv, 1)
            no, pt = bank(2)[:, 0:XT], bank(2)[:, XT:2 * XT]
            tok_f, free_f = hot1[:, 0:XT], hot2[:, 0:XT]
            ch.link(V.tensor_scalar(free_f, no, 0.0, spare[:, 0:1], ALU.is_equal, ALU.mult))
            ch.link(V.tensor_scalar(tok_f, no, float(P), -float(P), ALU.mult, ALU.add))
            ch.link(V.tensor_tensor(tok_f, tok_f, pt, ALU.add))
            V.tensor_tensor(token_of[:, :], tok_f, free_f, ALU.add).then_inc(s_token, 1)

            dve.wait_ge(s_etab, 2)
            dve.wait_ge(s_bias, 32)
            dve.wait_ge(s_table, 32)
            dve.wait_ge(s_w1, 16)
            er = [dve.alloc_register(f"dve_expert{n}") for n in range(4)]

            def copy_w1(e, b, i):
                dve.wait_ge(x_h[2 * b + 1], i)
                keep(w1_now[b], w1_all[:, ds(e * (KC * F), KC * F)]).then_inc(x_w1[b], 1)

            def evac_x(e, b, i, weight):
                dve.wait_ge(x_tp[b], i + 1)
                keep(weight[:, b:b + 1], xd[b][:, ds(e + D, 1)]).then_inc(s_tile, 1)
                for k in range(KC):
                    V.tensor_scalar(xeT[b][:, k * P:(k + 1) * P], bank(4)[:, k * P:(k + 1) * P],
                                    eg_col[:, ds(e * KC + k, 1)], eb_col[:, ds(e * KC + k, 1)],
                                    ALU.mult, ALU.add).then_inc(x_T[b], 1)

            base_y = base[0] + 2

            def weigh_y(e, b, i, last=False):
                dve.wait_ge(x_y[b], i + 1)
                dve.wait_ge(x_out[b], 16 * i)
                V.tensor_tensor(yt[b], bank(6 + b)[:, 0:D], b2_all[:, ds(e * D, D)], ALU.add).then_inc(s_tile, 1)
                if last:
                    dve.wait_ge(s_tile, base_y + 3 * (XT - 2) + 1 + b)
                else:
                    dve.wait_ge(s_tile, i * 6 + (3 * b + base_y + 2))
                V.tensor_scalar(yt[b], yt[b], w_now[:, b:b + 1], None, ALU.mult).then_inc(x_yb[b], 1)
                if not last:
                    dve.wait_ge(x_yb[b], i + 1)
                    V.tensor_copy(w_now[:, b:b + 1], w_next[:, b:b + 1]).then_inc(s_tile, 1)

            def experts(regs, at):
                dve.reg_load(regs, expert_of[0:1, ds(at, len(regs))])
                return [dve.snap(r, min_val=0, max_val=E - 1) for r in regs]

            e0, e1 = experts(er[0:2], 0)
            for b, e in enumerate((e0, e1)):
                copy_w1(e, b, 0)
                evac_x(e, b, 0, w_now)

            def expert_tiles(i):
                es = experts(er, i * 2)
                for b in range(2):
                    copy_w1(es[2 + b], b, i + 1)
                    evac_x(es[2 + b], b, i + 1, w_next)
                    weigh_y(es[b], b, i)

            repeat(dve, XT // 2 - 1, expert_tiles)
            es = experts(er[0:2], XT - 2)
            for b in range(2):
                weigh_y(es[b], b, XT // 2 - 1, last=True)

        @block.tensor
        def _(pe):
            T = nc.tensor
            for c in range(NCH):
                b = c % 2
                pe.wait_ge(oh_ready[b], 2 * (c // 2 + 1))
                lo = oh_lo[b][0:EP, 0:LO * CH].rearrange("p (n c) -> p n c", c=CH)
                hi = oh_hi[b][0:EP, 0:HI * CH].rearrange("p (n c) -> p n c", c=CH)
                for j in range(CH):
                    last = T.matmul(bank(7)[0:LO, 0:HI], lo[:, :, j], hi[:, :, j],
                                    start=(c == 0 and j == 0), stop=(c == NCH - 1 and j == CH - 1))
                last.then_inc(oh_used[b] if c < NCH - 1 else s_deg, 1)
            pe.wait_ge(s_const, 3)

            def turn2(dst, rows, signal):
                for k in range(KC):
                    last = T.transpose(dst[:, k * P:(k + 1) * P], rows(k), ident[:, :])
                last.then_inc(signal, 1)

            def wkv(k, o, n):
                return wqkv_sb[:, k * 3 * D + o:k * 3 * D + o + n]

            def pass1_turn(t):
                i, b = t // 2, t % 2
                pe.wait_ge(in_place[b], i + 1)
                if t:
                    pe.wait_ge(m_nT[1 - b], i + b)
                turn2(bank(1), lambda k: work[b][0][:, k * P:(k + 1) * P], m_tp[b])

            def pass1_front(t):
                i, b = t // 2, t % 2
                pe.wait_ge(m_nT[b], i + 1)
                if i:
                    pe.wait_ge(m_exp[b], i * 5)
                for k in range(KC):
                    T.matmul(bank(2 + b), nT[b][:, k * P:(k + 1) * P], wkv(k, D, 2 * D),
                             start=(k == 0), stop=(k == KC - 1))
                for o in range(KC):
                    for k in range(KC):
                        last = T.matmul(bank(4 + b)[:, o * P:(o + 1) * P], wkv(k, o * P, P),
                                        nT[b][:, k * P:(k + 1) * P], start=(k == 0), stop=(k == KC - 1))
                last.then_inc(m_qkv[b], 1)

            def pass1_back(t):
                i, b = t // 2, t % 2
                pe.wait_ge(m_phi[b], i * 2 + 1)
                pe.wait_ge(m_exp[b], i * 5 + 3)
                n = TAIL if t == NT - 1 else P
                for c in range(KC):
                    last = T.matmul(bank(6 + c)[:, 0:P + 1], rel_k[b][0:n, c * P:(c + 1) * P],
                                    v_ext[b][0:n, c * VW:c * VW + P + 1], start=False, stop=(t == NT - 1),
                                    skip_group_check=True)
                last.then_inc(m_kv[b], 1)

            fronts = [0]

            def pass1(n):
                for t in range(fronts[0], min(fronts[0] + n, NT)):
                    if t == 0:
                        pass1_turn(0)
                    if t + 1 < NT:
                        pass1_turn(t + 1)
                    pass1_front(t)
                    if t:
                        pass1_back(t - 1)
                    fronts[0] = t + 1

            pe.wait_ge(s_wts, 4 * 16)
            pe.wait_ge(s_dinv, 2)
            pe.wait_ge(s_zero, 1)
            pe.wait_ge(s_vone, 2)
            for c in range(KC):
                T.matmul(bank(6 + c)[:, 0:P + 1], zero_w[:, 0:P], zero_w[:, 0:P + 1], start=True, stop=False,
                         skip_group_check=True)
            for k, (to_cols, live, count) in enumerate(turns):
                pe.wait_ge(s_sort, count)
                for c in range(4):
                    if to_cols:
                        blk = rows_s[live][:, c * P:(c + 1) * P]
                    else:
                        blk = cols_s[live].rearrange("q (p c) -> q c p", c=4)[:, c, :]
                    last = T.transpose(bank(0)[:, c * P:(c + 1) * P], blk, ident[:, :])
                last.then_inc(s_turned, 1)
                pass1(TILES_BEHIND[k])
            pe.wait_ge(s_path, 1)
            T.matmul(bank(0)[:, 0:ET - 1], last_m[:, :], end_f[:, 0:ET - 1], start=True,
                     stop=True).then_inc(s_last, 1)
            pass1(NT)
            pass1_back(NT - 1)

            pe.wait_ge(s_reps, 4 * 16)

            def edge_steps(turn, half):
                g = turn * 2 + half
                for u in range(R):
                    pe.wait_ge(gathered[half * R + u], 16 * (turn + 1))
                    pe.wait_ge(hot_ready, g * R + u + 1)
                    if u % 2 == 0 and past_first(g):
                        pe.wait_ge(added, g * R + (u + 2 - R))
                    T.matmul(step_sum(u), hot_of[half][u], rows_of[half][u], start=True,
                             stop=True).then_inc(summed, 1)

            pe.wait_ge(s_bd, 1 + 8 * KC)

            def pass2(i, b, t, tail):
                pe.wait_ge(in_place[b], i + 1 + (HALF + 1 - b))
                pe.wait_ge(a_s[b], i)
                for c in range(KC):
                    last = T.matmul(bank(b)[:, c * VW:(c + 1) * VW], exp_q[b][:, c * P:(c + 1) * P],
                                    kvbd[:, c, :], start=True, stop=True)
                last.then_inc(a_num[b], 1)
                edge_steps(i, b)

            node_tiles(pe, pass2)
            edge_steps(NT // 2, 1)

            def ffn_front(i, b, t, tail):
                pe.wait_ge(a_x1[b], i + 1)
                pe.wait_ge(a_x1T[1 - b], 2 * i + 2 * b)
                turn2(bank(0), lambda k: work[b][1][:, k * P:(k + 1) * P], a_tp[b])
                pe.wait_ge(a_x1T[b], 2 * (i + 1))
                pe.wait_ge(a_hT[1 - b], 2 * i + 2 * b)
                for o in range(KC):
                    for k in range(KC):
                        last = T.matmul(bank(1)[:, o * P:(o + 1) * P], w1_sb[:, k * D + o * P:k * D + (o + 1) * P],
                                        nT[b][:, k * P:(k + 1) * P], start=(k == 0), stop=(k == KC - 1))
                last.then_inc(a_h[b], 1)
                if not past_first(t):
                    edge_steps(FF // 2, 0)

            def ffn_back(i, b, t, tail):
                pe.wait_ge(a_hT[b], 2 * (i + 1))
                pe.wait_ge(a_out[b], i)
                for k in range(KC):
                    last = T.matmul(bank(2 + b)[:, 0:D], exp_k[b][:, k * P:(k + 1) * P],
                                    w2_sb[:, k * D:(k + 1) * D], start=(k == 0), stop=(k == KC - 1))
                    if k == 0:
                        for o in range(KC):
                            T.matmul(bank(2 + b)[:, o * P:(o + 1) * P], nT[b][:, o * P:(o + 1) * P],
                                     ident[:, :], start=False, stop=False)
                last.then_inc(a_y[b], 1)
                edge_steps(i + (FF // 2 + b), 1 - b)

            staggered(pe, ffn_front, ffn_back)

            for g in range(FF + NT, GROUPS):
                edge_steps(g // 2, g % 2)

            def combine_front(i, b, t, tail):
                pe.wait_ge(c_sc[b], 2 * (i + 1))
                pe.wait_ge(c_T[b], i)
                for k in range(KC):
                    for h in (exp_k[b], exp_q[b]):
                        last = T.matmul(bank(b)[:, k * P:(k + 1) * P], h[:, k * P:(k + 1) * P], ident[:, :],
                                        start=(h is exp_k[b]), stop=(h is exp_q[b]))
                last.then_inc(c_tp[b], 1)

            def combine_back(i, b, t, tail):
                pe.wait_ge(c_T[b], i + 1)
                pe.wait_ge(c_x2[b], i)
                T.matmul(bank(4 + b)[:, 0:D], ones_m[0:1, :], gb_r[0:1, :], start=True, stop=False)
                for k in range(KC):
                    last = T.matmul(bank(4 + b)[:, 0:D], nT[b][:, k * P:(k + 1) * P],
                                    gw_sb[:, k * D:(k + 1) * D], start=False, stop=(k == KC - 1))
                last.then_inc(c_mm[b], 1)

            def route_front(i, b, t, tail):
                pe.wait_ge(c_xt[b], i + 1)
                pe.wait_ge(c_T2[b], i)
                turn2(bank(2 + b), lambda k: work[b][2][:, k * P:(k + 1) * P], c_tp2[b])

            def route_back(i, b, t, tail):
                pe.wait_ge(c_T2[b], i + 1)
                for k in range(KC):
                    last = T.matmul(bank(6)[:, ds(t * E, E)], exp_q[b][:, k * P:(k + 1) * P], wr_sb[:, k, :],
                                    start=(k == 0), stop=(k == KC - 1))
                last.then_inc(c_lg, 1)

            pe.wait_ge(added, STEPS)
            staggered(pe, combine_front, combine_back)
            pe.wait_ge(s_small, 7 * 16)
            staggered(pe, route_front, route_back)
            pe.wait_ge(s_cnt, 1)
            T.matmul(bank(0)[:, 0:NE], below[:, :], rt_b[:, :], start=True, stop=True)
            T.matmul(bank(1)[:, 0:NE], ones_m[:, :], rt_b[:, :], start=True, stop=True).then_inc(s_rank, 1)

            for k in range(2):
                pe.wait_ge(s_hots, 3 * (k + 1))
                lo = slot_lo[k].rearrange("p (t n) -> p t n", n=P)
                hi = slot_hi[k].rearrange("p (t x) -> p t x", x=2 * XT)
                for t in range(NT):
                    n = TAIL if t == NT - 1 else P
                    last = T.matmul(bank(2)[:, 0:2 * XT], lo[0:n, t, :], hi[0:n, t, :],
                                    start=(k == 0 and t == 0), stop=(k == 1 and t == NT - 1))
            last.then_inc(s_inv, 1)

            pe.wait_ge(s_etab, 2)
            er = [pe.alloc_register(f"pe_expert{n}") for n in range(2)]

            def turn_x(b, i, seen):
                pe.wait_ge(x_in[b], 16 * (i + 1))
                pe.wait_ge(x_T[1 - b], 2 * seen)
                turn2(bank(4), lambda k: xd[b][:, k * P:(k + 1) * P], x_tp[b])

            def first(b, i):
                pe.wait_ge(x_T[b], 2 * (i + 1))
                pe.wait_ge(x_w1[b], i + 1)
                for s in range(2):
                    pe.wait_ge(x_g[2 * b + s], 4 * i)
                    for f in range(4):
                        for k in range(KC):
                            at = k * F + (4 * s + f) * P
                            last = T.matmul(bank(2 * b + s)[:, f * P:(f + 1) * P], w1_now[b][:, at:at + P],
                                            xeT[b][:, k * P:(k + 1) * P], start=(k == 0), stop=(k == KC - 1))
                    last.then_inc(x_h[2 * b + s], 1)

            def second(e, b, i):
                pe.wait_ge(x_yb[b], i)
                for k in range(FC):
                    if k % 4 == 0:
                        pe.wait_ge(x_g[2 * b + k // 4], 4 * (i + 1))
                    last = T.matmul(bank(6 + b)[:, 0:D], hidT[b][:, k * P:(k + 1) * P],
                                    w2_all[:, ds(e * (FC * D) + k * D, D)], start=(k == 0), stop=(k == FC - 1))
                last.then_inc(x_y[b], 1)

            def experts(regs, at):
                pe.reg_load(regs, expert_of[0:1, ds(at, len(regs))])
                return [pe.snap(r, min_val=0, max_val=E - 1) for r in regs]

            turn_x(0, 0, 0)
            turn_x(1, 0, 1)
            first(0, 0)
            pe.wait_ge(s_w2, 16)

            def expert_tiles(i):
                ea, eb = experts(er, i * 2)
                first(1, i)
                turn_x(0, i + 1, i + 1)
                second(ea, 0, i)
                first(0, i + 1)
                turn_x(1, i + 1, i + 2)
                second(eb, 1, i)

            repeat(pe, XT // 2 - 1, expert_tiles)
            n = XT // 2 - 1
            ea, eb = experts(er, XT - 2)
            first(1, n)
            second(ea, 0, n)
            second(eb, 1, n)

        @block.scalar
        def _(act):
            A = nc.scalar
            def place(b, i, t):
                xt = xn_all[:, ds(t * D, D)]
                if past_first(t):
                    act.wait_ge(m_tp[b], i)
                A.activation(work[b][0], xt, ACT.Identity, bias=shift[:, ds(t, 1)],
                             scale=rstd[:, ds(t, 1)]).then_inc(in_place[b], 1)
                A.activation(y_all[:, ds(t * D, D)], xt, ACT.Identity, bias=y_shift[:, ds(t, 1)],
                             scale=y_scale[:, ds(t, 1)]).then_inc(s_y, 1)
                A.activation(xt, xt, ACT.Identity, bias=shift[:, ds(t, 1)], scale=rstd[:, ds(t, 1)]).then_inc(s_ln, 1)

            def pass1_front(i, b, t, tail):
                act.wait_ge(m_tp[b], i + 1)
                act.wait_ge(m_qkv[b], i)
                A.activation(nT[b], bank(1)[:, 0:D], ACT.Copy).then_inc(m_nT[b], 1)
                if not tail:
                    place(1 - b, i + b, t + 1)

            def pass1_back(i, b, t, tail):
                act.wait_ge(m_qkv[b], i + 1)
                act.wait_ge(m_phi[b], 2 * i)
                act.wait_ge(m_kv[b], i)
                A.activation(exp_k[b], bank(2 + b)[:, 0:D], ACT.Exp).then_inc(m_exp[b], 1)
                A.activation(rel_k[b], bank(2 + b)[:, 0:D], ACT.Relu).then_inc(m_exp[b], 1)
                A.activation(v_ext[b].rearrange("p (c v) -> p c v", c=KC)[:, :, 0:P],
                             bank(2 + b)[:, D:2 * D].rearrange("p (c v) -> p c v", c=KC),
                             ACT.Copy).then_inc(m_exp[b], 1)
                A.activation(exp_q[b], bank(4 + b)[:, 0:D], ACT.Exp).then_inc(m_exp[b], 1)
                A.activation(rel_q[b], bank(4 + b)[:, 0:D], ACT.Relu).then_inc(m_exp[b], 1)

            act.wait_ge(s_vone, 2)
            act.wait_ge(s_means, 1)
            act.wait_ge(s_dinv, 2)
            place(0, 0, 0)
            staggered(act, pass1_front, pass1_back, peel=True)

            act.wait_ge(s_prow, 16)
            tiles = [act.alloc_register(f"act_tile{u}") for u in range(R)]

            def indices(turn, half):
                g = turn * 2 + half
                act.reg_load(tiles, path[0:1, ds(g * R, R)])
                for u in range(R):
                    t = act.snap(tiles[u], min_val=0, max_val=ET - 1)
                    if past_first(turn):
                        act.wait_ge(gathered[half * R + u], 16 * turn)
                    A.activation(idx_g[:, half * R + u:half * R + u + 1], dst_i[:, ds(t, 1)],
                                 ACT.Copy).then_inc(idx_ready, 1)

            indices(0, 0)

            def pass2(i, b, t, tail):
                act.wait_ge(a_num[b], i)
                act.wait_ge(m_phi[b], 2 * (HALF + (1 - b)))
                A.activation(exp_q[b], qT_all[:, ds(t * D, D)], ACT.Copy).then_inc(in_place[b], 1)
                indices(i + b, 1 - b)

            node_tiles(act, pass2)
            indices(FF // 2, 0)
            indices(FF // 2, 1)

            def ffn(i, b, t, tail):
                act.wait_ge(a_tp[b], i + 1)
                act.wait_ge(a_y[b], i)
                for k in range(KC):
                    A.activation(nT[b][:, k * P:(k + 1) * P], bank(0)[:, k * P:(k + 1) * P], ACT.Identity,
                                 bias=o1_col[:, k:k + 1], scale=g1_col[:, k:k + 1]).then_inc(a_x1T[b], 1)
                act.wait_ge(a_h[b], i + 1)
                for o in range(KC):
                    A.activation(exp_k[b][:, o * P:(o + 1) * P], bank(1)[:, o * P:(o + 1) * P], ACT.Gelu,
                                 bias=b1_col[:, o:o + 1]).then_inc(a_hT[b], 1)
                indices(i + (FF // 2 + 1), b)

            act.wait_ge(s_small, 7 * 16)
            node_tiles(act, ffn)
            for g in range(FF + NT + 1, GROUPS):
                indices(g // 2, g % 2)

            act.wait_ge(added, STEPS)

            def combine_front(i, b, t, tail):
                act.wait_ge(c_tp[b], i)
                for h, to in ((h_all, exp_k[b]), (h_odd, exp_q[b])):
                    A.activation(to, h[:, ds(t * D, D)], ACT.Copy, scale=dinv[:, ds(t, 1)]).then_inc(c_sc[b], 1)

            def fifth(b, count):
                act.wait_ge(c_mm[b], count)
                A.activation(work[b][0], bank(4 + b)[:, 0:D], ACT.Copy, scale=0.2).then_inc(c_fifth, 1)

            def combine_back(i, b, t, tail):
                act.wait_ge(c_tp[b], i + 1)
                A.activation(nT[b], bank(b)[:, 0:D], ACT.Copy).then_inc(c_T[b], 1)
                if past_first(t):
                    fifth(1 - b, i + b)

            def route_in(i, b, t, tail):
                act.wait_ge(c_tp2[b], i + 1)
                if past_first(i):
                    act.wait_ge(c_lg, t - 1)
                A.activation(exp_q[b], bank(2 + b)[:, 0:D], ACT.Copy).then_inc(c_T2[b], 1)

            staggered(act, combine_front, combine_back)
            fifth(0, HALF + 1)
            node_tiles(act, route_in)
            act.wait_ge(s_route, 1)
            A.activation(prob[:, :], logit[:, :], ACT.Exp).then_inc(s_exp, 1)
            act.wait_ge(s_means, 2)
            for t in range(NT):
                h = h_all[:, t * D:(t + 1) * D]
                A.activation(h, h, ACT.Identity, bias=nw_v[:, t:t + 1], scale=rstd[:, t:t + 1]).then_inc(s_xn, 1)

            act.wait_ge(s_etab, 2)
            act.wait_ge(s_bias, 32)
            er = [act.alloc_register(f"act_expert{n}") for n in range(2)]

            def gelu(e, b, i):
                act.wait_ge(x_y[b], i)
                for s in range(2):
                    act.wait_ge(x_h[2 * b + s], i + 1)
                    for f in range(4):
                        c = 4 * s + f
                        A.activation(hidT[b][:, c * P:(c + 1) * P], bank(2 * b + s)[:, f * P:(f + 1) * P],
                                     ACT.Gelu, bias=b1_all[:, ds(e * FC + c, 1)]).then_inc(x_g[2 * b + s], 1)

            def expert_tiles(i):
                act.reg_load(er, expert_of[0:1, ds(i * 2, 2)])
                for b in range(2):
                    gelu(act.snap(er[b], min_val=0, max_val=E - 1), b, i)

            repeat(act, XT // 2, expert_tiles)

        @block.gpsimd
        def _(pool):
            G = nc.gpsimd
            ch = Chain(pool, s_pool)
            G.memset(xn_all[:, (NT - 1) * D:NT * D], 0.0).then_inc(s_hzero, 1)
            G.memset(zero_w, 0.0).then_inc(s_zero, 1)
            G.iota(iota_lo[:, 0:LO * CH], pattern=[[1, LO], [0, CH]], base=0, channel_multiplier=0,
                   allow_small_or_imprecise_dtypes=True).then_inc(s_const, 1)
            G.iota(iota_hi[:, 0:HI * CH], pattern=[[1, HI], [0, CH]], base=0, channel_multiplier=0,
                   allow_small_or_imprecise_dtypes=True).then_inc(s_const, 1)
            ch.link(G.memset(ident[:, :], 0.0))
            ch.link(G.affine_select(out=ident[:, :], in_=ident[:, :], compare_op=ALU.not_equal, fill=1.0,
                                    base=0, pattern=[[-1, P]], channel_multiplier=1))
            ch.link(G.memset(last_m[:, :], 0.0))
            ch.link(G.affine_select(out=last_m[:, :], in_=last_m[:, :], compare_op=ALU.not_equal, fill=1.0,
                                    base=-(P - 1), pattern=[[0, P]], channel_multiplier=1))
            ch.link(G.memset(below[:, :], 1.0))
            ch.link(G.affine_select(out=below[:, :], in_=below[:, :], compare_op=ALU.is_gt, fill=0.0,
                                    base=0, pattern=[[1, P]], channel_multiplier=-1))
            G.memset(ones_m[:, :], 1.0)
            G.iota(step_f[:, :], pattern=[[P, PC]], base=0, channel_multiplier=1,
                   allow_small_or_imprecise_dtypes=True)
            G.iota(block_at[:, :], pattern=[[P, NT]], base=0, channel_multiplier=0,
                   allow_small_or_imprecise_dtypes=True)
            G.iota(tile_no[:, :], pattern=[[1, NT]], base=1, channel_multiplier=0,
                   allow_small_or_imprecise_dtypes=True)
            G.iota(lane[:, :], pattern=[[0, 1]], base=0, channel_multiplier=1,
                   allow_small_or_imprecise_dtypes=True)
            G.iota(spare[:, :], pattern=[[0, 1]], base=NP_ + P, channel_multiplier=1,
                   allow_small_or_imprecise_dtypes=True)
            G.iota(rank_w[:, :], pattern=[[0, NT], [-1, E]], base=E, channel_multiplier=0,
                   allow_small_or_imprecise_dtypes=True)
            G.iota(xt_iota[:, :], pattern=[[1, XT], [0, E]], base=0, channel_multiplier=0,
                   allow_small_or_imprecise_dtypes=True)
            ch.link(G.memset(valid[:, :], 1.0))
            ch.link(G.affine_select(out=valid[:, :], in_=valid[:, :], compare_op=ALU.is_ge, fill=0.0,
                                    base=N - 1, pattern=[[-P, NT], [0, E]], channel_multiplier=-1))
            ch.link(G.iota(iota, pattern=[[1, SC]], base=0, channel_multiplier=0,
                           allow_small_or_imprecise_dtypes=True))
            G.memset(const_end[:, :], 0.0).then_inc(s_const, 1)

            G.memset(h_all, 0.0).then_inc(s_hzero, 1)
            pool.wait_ge(s_deg, 1)
            for b in range(2):
                G.memset(v_ext[b], 1.0).then_inc(s_vone, 1)

            for t in range(NT):
                i, b = t // 2, t % 2
                pool.wait_ge(m_exp[b], i * 5 + 1)
                G.tensor_scalar(exp_k[b], exp_k[b], 1.0, None, ALU.min).then_inc(s_pool, 1)
                pool.wait_ge(m_exp[b], i * 5 + 2)
                pool.wait_ge(s_pool, ch.n + 1)
                G.tensor_tensor(rel_k[b], exp_k[b], rel_k[b], ALU.add).then_inc(m_phi[b], 1)
                pool.wait_ge(m_exp[b], i * 5 + 4)
                G.tensor_scalar(exp_q[b], exp_q[b], 1.0, None, ALU.min).then_inc(s_pool, 1)
                pool.wait_ge(m_exp[b], i * 5 + 5)
                pool.wait_ge(s_pool, ch.n + 2)
                G.tensor_tensor(qT_all[:, t * D:(t + 1) * D], exp_q[b], rel_q[b], ALU.add).then_inc(m_phi[b], 1)
                ch.n += 2

            pool.wait_ge(s_ytab, 32)
            pool.wait_ge(s_path, 1)
            G.memset(h_odd, 0.0).then_inc(s_hzero, 1)
            pool.wait_ge(s_spare, 48)
            pool.wait_ge(m_kv[0], 1)
            zero_reg = pool.alloc_register("gather_zero")
            bound = pool.alloc_register("gather_bound")
            pool.reg_mov(zero_reg, 0)

            def gathers(turn, half):
                g = turn * 2 + half
                for u in range(R):
                    pool.wait_ge(idx_ready, g * R + u + 1)
                    if past_first(turn):
                        pool.wait_ge(summed, g * R + (u + 1 - 2 * R))
                    pool.reg_add(bound, zero_reg, NP_ - 1)
                    at = half * R + u
                    G.indirect_dma_start(out=rows_of[half][u], out_offset=None, in_=y_table,
                                         in_offset=bass.IndirectOffsetOnAxis(ap=idx_g[:, at:at + 1], axis=0),
                                         bounds_check=bound, oob_is_err=True).then_inc(gathered[at], 16)

            def two_groups(i):
                gathers(i, 0)
                gathers(i, 1)

            repeat(pool, GROUPS // 2, two_groups)
            gathers(GROUPS // 2, 0)

            pool.wait_ge(added, STEPS)
            G.iota(slot_iota, pattern=[[1, P]], base=0, channel_multiplier=0,
                   allow_small_or_imprecise_dtypes=True).then_inc(s_const, 1)

            def combine(i, b, t, tail):
                w2 = work[b][2]
                pool.wait_ge(c_n, t + 1)
                G.tensor_tensor(w2, w2, ln2g_r, ALU.mult).then_inc(s_pool, 1)
                pool.wait_ge(s_pool, t * 2 + (ch.n + 1))
                G.tensor_tensor(w2, w2, ln2b_r, ALU.add).then_inc(s_pool, 1)
                pool.wait_ge(c_x[b], i * 16 + 16)
                pool.wait_ge(s_pool, t * 2 + (ch.n + 2))
                G.tensor_tensor(w2, w2, rows_g[b], ALU.add).then_inc(c_w, 1)

            node_tiles(pool, combine)

            pool.wait_ge(s_token, 1)
            pool.wait_ge(s_table, 32)
            pool.wait_ge(c_x2o[0], 16 * (HALF + 1))
            pool.wait_ge(c_x2o[1], 16 * HALF)

            def gather_x(t):
                b, i = t % 2, t // 2
                if i:
                    pool.wait_ge(x_T[b], 2 * i)
                G.indirect_dma_start(out=xd[b], out_offset=None, in_=x3_rows,
                                     in_offset=bass.IndirectOffsetOnAxis(ap=token_of[:, t:t + 1], axis=0),
                                     bounds_check=NP_ + P - 1, oob_is_err=True).then_inc(x_in[b], 16)

            def add_y(t):
                b, i = t % 2, t // 2
                pool.wait_ge(x_yb[b], i + 1)
                if t:
                    pool.wait_ge(x_out[1 - b], 16 * ((t - 1) // 2 + 1))
                G.indirect_dma_start(out=x2_rows, out_offset=bass.IndirectOffsetOnAxis(ap=token_of[:, t:t + 1], axis=0),
                                     in_=yt[b], in_offset=None, bounds_check=NP_ + P - 1, oob_is_err=True,
                                     compute_op=ALU.add).then_inc(x_out[b], 16)

            for t in range(3):
                gather_x(t)
            for t in range(XT):
                if t + 3 < XT:
                    gather_x(t + 3)
                add_y(t)

        @block.sync
        def _(sp):
            sp.dma_start(src_i[0:EP, :], src.rearrange("(p c) -> p c", c=EC)).then_inc(s_edges, 16)
            sp.dma_start(dst_e[0:EP, :], dst.rearrange("(p c) -> p c", c=EC)).then_inc(s_edges, 16)
            full = (NT - 1) * P
            sp.dma_start(xn_all[:, 0:(NT - 1) * D].rearrange("p (t d) -> p t d", d=D),
                         x[0:full, :].rearrange("(t p) d -> p t d", p=P)).then_inc(s_x, 16)
            sp.wait_ge(s_hzero, 1)
            sp.dma_start(xn_all[0:TAIL, (NT - 1) * D:NT * D], x[full:N, :]).then_inc(s_x, 16)
            for w_sb, w_d, n in ((wqkv_sb, wqkv_t, 3 * D), (w1_sb, w1_t, D), (w2_sb, w2_t, D), (gw_sb, gnn_w, D)):
                sp.dma_start(w_sb.rearrange("p (k n) -> p k n", n=n),
                             w_d.rearrange("(k p) n -> p k n", p=P)).then_inc(s_wts, 16)
            for r, v in zip((ln2g_r, ln2b_r, b2_r, gb_r), (ln2_g, ln2_b, b2, gnn_b)):
                sp.dma_start(r, rep(v, D)).then_inc(s_reps, 16)
            with nc.allow_non_contiguous_dma(reason="a few columns"):
                sp.dma_start(g1_col[:, :], ln1_g.rearrange("(k p) -> p k", p=P)).then_inc(s_small, 16)
                sp.dma_start(o1_col[:, :], ln1_b.rearrange("(k p) -> p k", p=P)).then_inc(s_small, 16)
                sp.dma_start(b1_col[:, :], b1.rearrange("(k p) -> p k", p=P)).then_inc(s_small, 16)
                sp.dma_start(eg_col[:, :], ffn_g.rearrange("e (k p) -> p (e k)", p=P)).then_inc(s_small, 16)
                sp.dma_start(eb_col[:, :], ffn_b.rearrange("e (k p) -> p (e k)", p=P)).then_inc(s_small, 16)
            sp.dma_start(wr_sb[:, :, :], wr.rearrange("(k p) e -> p k e", p=P)).then_inc(s_small, 16)
            sp.dma_start(br_r[:, :], rep(br, E)).then_inc(s_small, 16)
            sp.wait_ge(s_zero, 1)
            sp.dma_start(x2_rows[NP_:NP_ + P, :], zero_w).then_inc(s_spare, 16)
            sp.dma_start(x3_rows[NP_:NP_ + P, 0:D], zero_w).then_inc(s_spare, 16)
            sp.dma_start(x3_rows[NP_:NP_ + P, D:D + E], zero_w[:, 0:E]).then_inc(s_spare, 16)
            for t0, t1 in ((0, 2 * NT // 3), (2 * NT // 3, NT)):
                sp.wait_ge(s_y, t1)
                sp.dma_start(y_table[t0 * P:t1 * P, :].rearrange("(t p) d -> p t d", p=P),
                             y_all[:, t0 * D:t1 * D].rearrange("p (t d) -> p t d", d=D)).then_inc(s_ytab, 16)
            sp.wait_ge(s_tiles, 1)
            with nc.allow_non_contiguous_dma(reason="a column of tile numbers"):
                sp.dma_start(path_dram.rearrange("a (c p) -> p (a c)", p=P), tile_i[:, :]).then_inc(s_pdram, 16)
            sp.wait_ge(s_pdram, 16)
            sp.dma_start(path[:, :], path_dram).then_inc(s_prow, 16)

            def load_x(i, b, t, tail):
                n = TAIL if tail else P
                sp.wait_ge(c_x2[b], i)
                sp.dma_start(rows_g[b][0:n], x[ds(t * P, n), :]).then_inc(c_x[b], 16)

            def store_x2(i, b, t, tail):
                sp.wait_ge(c_x2[b], i + 1)
                sp.dma_start(x2_rows[ds(t * P, P), :], work[b][1]).then_inc(c_x2o[b], 16)

            sp.wait_ge(added, STEPS)
            staggered(sp, load_x, store_x2, peel=True)

            sp.wait_ge(c_n, NT)
            sp.dma_start(w2_all.rearrange("p (e k d) -> p e k d", e=E, k=FC),
                         ffn_w2.rearrange("e (k p) d -> p e k d", p=P)).then_inc(s_w2, 16)
            sp.wait_ge(c_lg, NT)
            sp.dma_start(w1_all.rearrange("p (e k f) -> p e k f", e=E, k=KC),
                         ffn_w1.rearrange("e (k p) f -> p e k f", p=P)).then_inc(s_w1, 16)
            sp.wait_ge(c_x2o[0], 16 * (HALF + 1))
            sp.wait_ge(c_x2o[1], 16 * HALF)
            sp.dma_start(b2_all, ffn_b2.rearrange("(a e) d -> a (e d)", a=1).broadcast_to([P, E * D])).then_inc(s_bias, 16)
            with nc.allow_non_contiguous_dma(reason="a few columns"):
                sp.dma_start(b1_all, ffn_b1.rearrange("e (k p) -> p (e k)", p=P)).then_inc(s_bias, 16)
            sp.wait_ge(s_xn, NT)
            sp.dma_start(x3_rows[0:NP_, 0:D].rearrange("(t p) d -> p t d", p=P),
                         h_all.rearrange("p (t d) -> p t d", d=D)).then_inc(s_table, 16)
            sp.wait_ge(s_gates, 1)
            sp.dma_start(x3_rows[0:NP_, D:D + E].rearrange("(t p) e -> p t e", p=P),
                         prob[:, :].rearrange("p (t e) -> p t e", e=E)).then_inc(s_table, 16)

            for b in range(2):
                sp.wait_ge(x_out[b], 16 * (XT // 2))
            sp.dma_start(out, x2_rows[0:N, :]).then_inc(s_out, 16)
            sp.wait_ge(s_out, 16)


_INS = ["x", "src", "dst", "L0_gnn_W", "L0_gnn_b", "L0_mix_Wqkv", "L0_mix_ln1_g", "L0_mix_ln1_b", "L0_mix_W1",
        "L0_mix_b1", "L0_mix_W2", "L0_mix_b2", "L0_mix_ln2_g", "L0_mix_ln2_b", "L0_ffn_Wr", "L0_ffn_br",
        "L0_ffn_ln_g", "L0_ffn_ln_b", "L0_ffn_W1", "L0_ffn_b1", "L0_ffn_W2", "L0_ffn_b2"]
_TRANSPOSED = {"L0_mix_Wqkv", "L0_mix_W1", "L0_mix_W2"}


def kernel(**inputs):
    import numpy as _np
    import concourse.bacc as _bacc
    from concourse import mybir as _mybir
    from concourse.bass_utils import run_bass_kernel_spmd as _run

    nc = _bacc.Bacc("TRN2", target_bir_lowering=False, num_devices=1)
    arrays, args = {}, []
    for name in _INS:
        a = _np.asarray(inputs[name])
        a = _np.ascontiguousarray(a.T if name in _TRANSPOSED else a)
        arrays[f"in_{name}"] = a
        args.append(nc.dram_tensor(f"in_{name}", a.shape, _mybir.dt.from_np(a.dtype), kind="ExternalInput").ap())
    out = nc.dram_tensor("out_x", inputs["x"].shape, _mybir.dt.float32, kind="ExternalOutput").ap()
    gps_layer(nc, *args, out)
    r = _run(nc, [arrays], core_ids=[0])
    return r.results[0]["out_x"]
```
